# Optimizing a Trainium2 kernel written in Bass

```python
import numpy as np
import jax
import jax.numpy as jnp

def _softmax(x, axis=-1):
    return jax.nn.softmax(x, axis=axis)

def _gelu(x):
    return jax.nn.gelu(x, approximate=True)

def _silu(x):
    return jax.nn.silu(x)

def _sigmoid(x):
    return jax.nn.sigmoid(x)

def _layernorm(x, axis=-1, eps=1e-05):
    m = jnp.mean(x, axis=axis, keepdims=True)
    v = jnp.var(x, axis=axis, keepdims=True)
    return (x - m) / jnp.sqrt(v + eps)

def _scatter_add(tgt, idx, src, axis=0):
    return tgt.at[idx].add(src)

def _segment_sum(src, seg, n):
    return jax.ops.segment_sum(src, seg, n)
kernel_name = 'mk_decoder_postln_d2_seqx_r8_21abf2'

def setup_inputs(seed: int=0):
    np.random.seed(seed)
    _w = jnp.asarray

    def _rec_inputs():
        import jax
        import jax.numpy as jnp
        _rk = jax.random.key(seed)
        x = 7.22e-05 + 1 * jax.random.normal(jax.random.fold_in(_rk, 1), (2, 512, 128), jnp.float32)
        _lenS = 512 - jax.random.randint(jax.random.fold_in(_rk, 7), (2,), 0, max(1, 512 // 4) + 1, jnp.int32)
        _lenS2 = 77 - jax.random.randint(jax.random.fold_in(_rk, 8), (2,), 0, max(1, 77 // 4) + 1, jnp.int32)
        _ctx_768P = jax.random.normal(jax.random.fold_in(_rk, 11), (2, 16, 96), jnp.float32)
        _ctx_768c = jax.random.dirichlet(jax.random.fold_in(_rk, 511), 0.3 * jnp.ones((16,), jnp.float32), (2, 77))
        _ctx_768t = jnp.einsum('bsk,bkd->bsd', _ctx_768c, _ctx_768P)
        _ctx_768t = _ctx_768t * jax.lax.rsqrt(jnp.mean(jnp.square(_ctx_768t)) + 1e-12) * 0.953939
        ctx_768 = -0.000191848 + 0.999787 * (_ctx_768t + 0.3 * jax.random.normal(jax.random.fold_in(_rk, 611), (2, 77, 96), jnp.float32))
        _validS = jnp.arange(512)[None, :] < _lenS[:, None]
        _validS2 = jnp.arange(77)[None, :] < _lenS2[:, None]
        _causal = jnp.tril(jnp.ones((512, 512), dtype=bool))
        mask_1x1xSxS2_bk0 = jnp.logical_not(jnp.broadcast_to(_validS2[0:1, None, None, :], (1, 1, 512, 77)))
        return (x, ctx_768, mask_1x1xSxS2_bk0)
    x, ctx_768, mask_1x1xSxS2_bk0 = _rec_inputs()

    def _L0_attn_setup():
        import jax, jax.numpy as jnp
        import numpy as np
        SL, BS, E, H, PF, STRIDE, SHIFT = (256, 2, 128, 16, 16, 1, 0)
        DH = E // H

        def _layernorm(x, g, b, eps=1e-05):
            m = x.mean(-1, keepdims=True)
            v = jnp.var(x, axis=-1, keepdims=True)
            return (x - m) * jax.lax.rsqrt(v + eps) * g + b

        def _sparsify(context, h):
            c = context.shape[0]
            base = (jnp.arange(h) + 1) * STRIDE - PF + SHIFT
            idx = (base[None, :] + jnp.arange(PF)[:, None]) % c
            return context[idx.reshape(-1)].reshape(PF, h, context.shape[1], context.shape[2])
        key = jax.random.key(seed)
        ks = jax.random.split(key, 6)
        s = 0.02
        return {'x': jax.random.normal(ks[0], (SL, BS, E), jnp.float32), 'ln_g': jnp.ones((E,), jnp.float32), 'ln_b': jnp.zeros((E,), jnp.float32), 'Wq': jax.random.normal(ks[1], (E, E), jnp.float32) * s, 'bq': jnp.zeros((E,), jnp.float32), 'Wk': jax.random.normal(ks[2], (E, E), jnp.float32) * s, 'bk': jnp.zeros((E,), jnp.float32), 'Wv': jax.random.normal(ks[3], (E, E), jnp.float32) * s, 'bv': jnp.zeros((E,), jnp.float32), 'Wo': jax.random.normal(ks[4], (E, E), jnp.float32) * s, 'bo': jnp.zeros((E,), jnp.float32)}
    _L0_attn_all = _L0_attn_setup()
    _L0_attn_in = {k: v for k, v in _L0_attn_all.items() if k in ('ln_g', 'ln_b', 'Wq', 'bq', 'Wk', 'bk', 'Wv', 'bv', 'Wo', 'bo')}
    del _L0_attn_all

    def _L0_xattn_setup():
        import jax, jax.numpy as jnp
        import numpy as np
        B, T, Q_DIM, KV_DIM = (4, 256, 128, 96)
        HEADS, DIM_HEAD = (16, 64)
        INNER = HEADS * DIM_HEAD
        NUM_FRAMES, NUM_PATCHES = (8, 32)
        LN_EPS = 1e-05

        def diagonal_frame_mask(num_patches, num_frames):
            fid = np.repeat(np.arange(num_frames), num_patches)
            m = fid[:, None] == fid[None, :]
            return jnp.asarray(m[None, None])
        key = jax.random.key(seed)
        ks = jax.random.split(key, 6)
        s = lambda d: 1.0 / np.sqrt(d)
        return {'x': jax.random.normal(ks[0], (B, T, Q_DIM), jnp.float32), 'context': jax.random.normal(ks[1], (B, T, KV_DIM), jnp.float32), 'ln_gamma': jnp.ones((Q_DIM,), jnp.float32), 'ln_beta': jnp.zeros((Q_DIM,), jnp.float32), 'Wq': jax.random.normal(ks[2], (Q_DIM, INNER), jnp.float32) * s(Q_DIM), 'Wkv': jax.random.normal(ks[3], (KV_DIM, 2 * INNER), jnp.float32) * s(KV_DIM), 'Wo': jax.random.normal(ks[4], (INNER, Q_DIM), jnp.float32) * s(INNER), 'bo': jnp.zeros((Q_DIM,), jnp.float32), 'mask': diagonal_frame_mask(NUM_PATCHES, NUM_FRAMES)}
    _L0_xattn_all = _L0_xattn_setup()
    _L0_xattn_in = {k: v for k, v in _L0_xattn_all.items() if k in ('ln_gamma', 'ln_beta', 'Wq', 'Wkv', 'Wo', 'bo')}
    del _L0_xattn_all

    def _L0_ffn_setup():
        import jax, jax.numpy as jnp
        import numpy as np
        D_MODEL = 128
        D_FF = 512
        N_EXPERTS = 8
        TOP_K = 2

        def _ffn(x, w1, b1, w2, b2):
            h = jax.nn.gelu(x @ w1.T + b1)
            return h @ w2.T + b2
        key = jax.random.key(seed)
        ks = jax.random.split(key, 12)
        s = 0.02
        x = jax.random.normal(ks[0], (4, 256, D_MODEL), dtype=jnp.float32)
        shared_w1 = jax.random.normal(ks[1], (D_FF, D_MODEL), dtype=jnp.float32) * s
        shared_b1 = jnp.zeros((D_FF,), dtype=jnp.float32)
        shared_w2 = jax.random.normal(ks[2], (D_MODEL, D_FF), dtype=jnp.float32) * s
        shared_b2 = jnp.zeros((D_MODEL,), dtype=jnp.float32)
        router_w = jax.random.normal(ks[3], (N_EXPERTS, D_MODEL), dtype=jnp.float32) * s
        router_b = jnp.zeros((N_EXPERTS,), dtype=jnp.float32)
        spec_w1 = jax.random.normal(ks[4], (N_EXPERTS, D_FF, D_MODEL), dtype=jnp.float32) * s
        spec_b1 = jnp.zeros((N_EXPERTS, D_FF), dtype=jnp.float32)
        spec_w2 = jax.random.normal(ks[5], (N_EXPERTS, D_MODEL, D_FF), dtype=jnp.float32) * s
        spec_b2 = jnp.zeros((N_EXPERTS, D_MODEL), dtype=jnp.float32)
        return dict(x=x, shared_w1=shared_w1, shared_b1=shared_b1, shared_w2=shared_w2, shared_b2=shared_b2, router_w=router_w, router_b=router_b, spec_w1=spec_w1, spec_b1=spec_b1, spec_w2=spec_w2, spec_b2=spec_b2)
    _L0_ffn_all = _L0_ffn_setup()
    _L0_ffn_in = {k: v for k, v in _L0_ffn_all.items() if k in ('shared_w1', 'shared_b1', 'shared_w2', 'shared_b2', 'router_w', 'router_b', 'spec_w1', 'spec_b1', 'spec_w2', 'spec_b2')}
    del _L0_ffn_all

    def _L1_attn_setup():
        import jax, jax.numpy as jnp
        import numpy as np
        D = 128
        H = 4
        DK = 32
        DV = 64
        B, T = (4, 256)

        def _l2norm(t):
            return t * jax.lax.rsqrt(jnp.sum(t * t, axis=-1, keepdims=True) + 1e-06)
        key = jax.random.key(seed)
        ks = jax.random.split(key, 6)
        rn = lambda k, shape, scale: jax.random.normal(k, shape, jnp.float32) * scale
        return {'x': rn(ks[0], (B, T, D), 1.0), 'ln_w': jnp.ones((D,), jnp.float32), 'ln_b': jnp.zeros((D,), jnp.float32), 'Wq': rn(ks[1], (D, H * DK), D ** (-0.5)), 'Wk': rn(ks[2], (D, H * DK), D ** (-0.5)), 'Wv': rn(ks[3], (D, H * DV), D ** (-0.5)), 'Wb': rn(ks[4], (D, H), D ** (-0.5)), 'o_norm_w': jnp.ones((DV,), jnp.float32), 'Wo': rn(ks[5], (H * DV, D), (H * DV) ** (-0.5))}
    _L1_attn_all = _L1_attn_setup()
    _L1_attn_in = {k: v for k, v in _L1_attn_all.items() if k in ('ln_w', 'ln_b', 'Wq', 'Wk', 'Wv', 'Wb', 'o_norm_w', 'Wo')}
    del _L1_attn_all

    def _L1_xattn_setup():
        import jax, jax.numpy as jnp
        import numpy as np
        QUERY_DIM, KV_DIM, EMBED_DIM, NUM_HEADS = (128, 96, 128, 16)
        HEAD_DIM = EMBED_DIM // NUM_HEADS
        SCALE = HEAD_DIM ** (-0.5)
        LN_EPS = 1e-05

        def _l2norm(x, eps=1e-12):
            n = jnp.sqrt(jnp.sum(x * x, axis=-1, keepdims=True))
            return x / jnp.maximum(n, eps)
        key = jax.random.key(seed)
        ks = jax.random.split(key, 12)
        B, Nq, Nk = (2, 256, 256)
        s = lambda d: 1.0 / np.sqrt(d)
        return {'query': jax.random.normal(ks[0], (B, Nq, QUERY_DIM), jnp.float32), 'key': jax.random.normal(ks[1], (B, Nk, KV_DIM), jnp.float32), 'value': jax.random.normal(ks[2], (B, Nk, KV_DIM), jnp.float32), 'Wq': jax.random.normal(ks[3], (QUERY_DIM, EMBED_DIM), jnp.float32) * s(QUERY_DIM), 'bq': jnp.zeros((EMBED_DIM,), jnp.float32), 'Wk': jax.random.normal(ks[4], (KV_DIM, EMBED_DIM), jnp.float32) * s(KV_DIM), 'bk': jnp.zeros((EMBED_DIM,), jnp.float32), 'Wv': jax.random.normal(ks[5], (KV_DIM, EMBED_DIM), jnp.float32) * s(KV_DIM), 'bv': jnp.zeros((EMBED_DIM,), jnp.float32), 'Wo': jax.random.normal(ks[6], (EMBED_DIM, EMBED_DIM), jnp.float32) * s(EMBED_DIM), 'bo': jnp.zeros((EMBED_DIM,), jnp.float32), 'ln_gamma': jnp.ones((EMBED_DIM,), jnp.float32), 'ln_beta': jnp.zeros((EMBED_DIM,), jnp.float32)}
    _L1_xattn_all = _L1_xattn_setup()
    _L1_xattn_in = {k: v for k, v in _L1_xattn_all.items() if k in ('Wq', 'bq', 'Wk', 'bk', 'Wv', 'bv', 'Wo', 'bo', 'ln_gamma', 'ln_beta')}
    del _L1_xattn_all

    def _L1_ffn_setup():
        import jax, jax.numpy as jnp
        import numpy as np
        TOP_K = 2

        def _ffn(x, gw, uw, dw):
            return jax.nn.silu(x @ gw.T) * (x @ uw.T) @ dw.T
        key = jax.random.key(seed)
        ks = jax.random.split(key, 8)
        w = lambda k, shape: jax.random.normal(k, shape, jnp.float32) * 0.02
        return dict(x=jax.random.normal(ks[0], (4, 256, 128), jnp.float32), gate_w=w(ks[1], (8, 128)), expert_gate=w(ks[2], (8, 352, 128)), expert_up=w(ks[3], (8, 352, 128)), expert_down=w(ks[4], (8, 128, 352)), shared_gate=w(ks[5], (352, 128)), shared_up=w(ks[6], (352, 128)), shared_down=w(ks[7], (128, 352)))
    _L1_ffn_all = _L1_ffn_setup()
    _L1_ffn_in = {k: v for k, v in _L1_ffn_all.items() if k in ('gate_w', 'expert_gate', 'expert_up', 'expert_down', 'shared_gate', 'shared_up', 'shared_down')}
    del _L1_ffn_all
    return {'x': x, 'ctx_768': ctx_768, 'mask_1x1xSxS2_bk0': mask_1x1xSxS2_bk0, 'L0_attn_ln_g': _L0_attn_in['ln_g'], 'L0_attn_ln_b': _L0_attn_in['ln_b'], 'L0_attn_Wq': _L0_attn_in['Wq'], 'L0_attn_bq': _L0_attn_in['bq'], 'L0_attn_Wk': _L0_attn_in['Wk'], 'L0_attn_bk': _L0_attn_in['bk'], 'L0_attn_Wv': _L0_attn_in['Wv'], 'L0_attn_bv': _L0_attn_in['bv'], 'L0_attn_Wo': _L0_attn_in['Wo'], 'L0_attn_bo': _L0_attn_in['bo'], 'L0_xattn_ln_gamma': _L0_xattn_in['ln_gamma'], 'L0_xattn_ln_beta': _L0_xattn_in['ln_beta'], 'L0_xattn_Wq': _L0_xattn_in['Wq'], 'L0_xattn_Wkv': _L0_xattn_in['Wkv'], 'L0_xattn_Wo': _L0_xattn_in['Wo'], 'L0_xattn_bo': _L0_xattn_in['bo'], 'L0_ffn_shared_w1': _L0_ffn_in['shared_w1'], 'L0_ffn_shared_b1': _L0_ffn_in['shared_b1'], 'L0_ffn_shared_w2': _L0_ffn_in['shared_w2'], 'L0_ffn_shared_b2': _L0_ffn_in['shared_b2'], 'L0_ffn_router_w': _L0_ffn_in['router_w'], 'L0_ffn_router_b': _L0_ffn_in['router_b'], 'L0_ffn_spec_w1': _L0_ffn_in['spec_w1'], 'L0_ffn_spec_b1': _L0_ffn_in['spec_b1'], 'L0_ffn_spec_w2': _L0_ffn_in['spec_w2'], 'L0_ffn_spec_b2': _L0_ffn_in['spec_b2'], 'L1_attn_ln_w': _L1_attn_in['ln_w'], 'L1_attn_ln_b': _L1_attn_in['ln_b'], 'L1_attn_Wq': _L1_attn_in['Wq'], 'L1_attn_Wk': _L1_attn_in['Wk'], 'L1_attn_Wv': _L1_attn_in['Wv'], 'L1_attn_Wb': _L1_attn_in['Wb'], 'L1_attn_o_norm_w': _L1_attn_in['o_norm_w'], 'L1_attn_Wo': _L1_attn_in['Wo'], 'L1_xattn_Wq': _L1_xattn_in['Wq'], 'L1_xattn_bq': _L1_xattn_in['bq'], 'L1_xattn_Wk': _L1_xattn_in['Wk'], 'L1_xattn_bk': _L1_xattn_in['bk'], 'L1_xattn_Wv': _L1_xattn_in['Wv'], 'L1_xattn_bv': _L1_xattn_in['bv'], 'L1_xattn_Wo': _L1_xattn_in['Wo'], 'L1_xattn_bo': _L1_xattn_in['bo'], 'L1_xattn_ln_gamma': _L1_xattn_in['ln_gamma'], 'L1_xattn_ln_beta': _L1_xattn_in['ln_beta'], 'L1_ffn_gate_w': _L1_ffn_in['gate_w'], 'L1_ffn_expert_gate': _L1_ffn_in['expert_gate'], 'L1_ffn_expert_up': _L1_ffn_in['expert_up'], 'L1_ffn_expert_down': _L1_ffn_in['expert_down'], 'L1_ffn_shared_gate': _L1_ffn_in['shared_gate'], 'L1_ffn_shared_up': _L1_ffn_in['shared_up'], 'L1_ffn_shared_down': _L1_ffn_in['shared_down']}

def reference(x, ctx_768, mask_1x1xSxS2_bk0, L0_attn_ln_g, L0_attn_ln_b, L0_attn_Wq, L0_attn_bq, L0_attn_Wk, L0_attn_bk, L0_attn_Wv, L0_attn_bv, L0_attn_Wo, L0_attn_bo, L0_xattn_ln_gamma, L0_xattn_ln_beta, L0_xattn_Wq, L0_xattn_Wkv, L0_xattn_Wo, L0_xattn_bo, L0_ffn_shared_w1, L0_ffn_shared_b1, L0_ffn_shared_w2, L0_ffn_shared_b2, L0_ffn_router_w, L0_ffn_router_b, L0_ffn_spec_w1, L0_ffn_spec_b1, L0_ffn_spec_w2, L0_ffn_spec_b2, L1_attn_ln_w, L1_attn_ln_b, L1_attn_Wq, L1_attn_Wk, L1_attn_Wv, L1_attn_Wb, L1_attn_o_norm_w, L1_attn_Wo, L1_xattn_Wq, L1_xattn_bq, L1_xattn_Wk, L1_xattn_bk, L1_xattn_Wv, L1_xattn_bv, L1_xattn_Wo, L1_xattn_bo, L1_xattn_ln_gamma, L1_xattn_ln_beta, L1_ffn_gate_w, L1_ffn_expert_gate, L1_ffn_expert_up, L1_ffn_expert_down, L1_ffn_shared_gate, L1_ffn_shared_up, L1_ffn_shared_down):
    import jax
    import jax.numpy as jnp

    def _L0_attn_ref(x, ln_g, ln_b, Wq, bq, Wk, bk, Wv, bv, Wo, bo):
        import jax, jax.numpy as jnp
        import numpy as np
        SL, BS, E, H, PF, STRIDE, SHIFT = (256, 2, 128, 16, 16, 1, 0)
        DH = E // H

        def _layernorm(x, g, b, eps=1e-05):
            m = x.mean(-1, keepdims=True)
            v = jnp.var(x, axis=-1, keepdims=True)
            return (x - m) * jax.lax.rsqrt(v + eps) * g + b

        def _sparsify(context, h):
            c = context.shape[0]
            base = (jnp.arange(h) + 1) * STRIDE - PF + SHIFT
            idx = (base[None, :] + jnp.arange(PF)[:, None]) % c
            return context[idx.reshape(-1)].reshape(PF, h, context.shape[1], context.shape[2])
        sl, bs, e = x.shape
        residual = x
        xn = _layernorm(x, ln_g, ln_b)
        fetch = _sparsify(xn, sl)
        q = (xn @ Wq + bq).reshape(sl, bs, H, DH)
        k = (fetch @ Wk + bk).reshape(PF, sl, bs, H, DH)
        v = (fetch @ Wv + bv).reshape(PF, sl, bs, H, DH)
        scale = 1.0 / jnp.sqrt(jnp.float32(DH))
        scores = jnp.einsum('sbhd,psbhd->sbhp', q, k) * scale
        attn = jax.nn.softmax(scores, axis=-1)
        out = jnp.einsum('sbhp,psbhd->sbhd', attn, v).reshape(sl, bs, e)
        out = out @ Wo + bo
        return residual + out

    def _L0_xattn_ref(x, context, ln_gamma, ln_beta, Wq, Wkv, Wo, bo, mask):
        import jax, jax.numpy as jnp
        import numpy as np
        B, T, Q_DIM, KV_DIM = (4, 256, 128, 96)
        HEADS, DIM_HEAD = (16, 64)
        INNER = HEADS * DIM_HEAD
        NUM_FRAMES, NUM_PATCHES = (8, 32)
        LN_EPS = 1e-05

        def diagonal_frame_mask(num_patches, num_frames):
            fid = np.repeat(np.arange(num_frames), num_patches)
            m = fid[:, None] == fid[None, :]
            return jnp.asarray(m[None, None])
        mu = jnp.mean(x, axis=-1, keepdims=True)
        var = jnp.mean(jnp.square(x - mu), axis=-1, keepdims=True)
        xn = (x - mu) * jax.lax.rsqrt(var + LN_EPS) * ln_gamma + ln_beta
        scale = DIM_HEAD ** (-0.5)
        q = xn @ Wq
        kv = context @ Wkv
        k, v = jnp.split(kv, 2, axis=-1)
        split_heads = lambda t: t.reshape(t.shape[0], t.shape[1], HEADS, DIM_HEAD).transpose(0, 2, 1, 3)
        q, k, v = (split_heads(q), split_heads(k), split_heads(v))
        dots = jnp.einsum('bhnd,bhmd->bhnm', q, k) * scale
        dots = jnp.where(mask, dots, -jnp.inf)
        attn = jax.nn.softmax(dots, axis=-1)
        out = jnp.einsum('bhnm,bhmd->bhnd', attn, v)
        out = out.transpose(0, 2, 1, 3).reshape(x.shape[0], x.shape[1], INNER)
        return out @ Wo + bo

    def _L0_ffn_ref(x, shared_w1, shared_b1, shared_w2, shared_b2, router_w, router_b, spec_w1, spec_b1, spec_w2, spec_b2):
        import jax, jax.numpy as jnp
        import numpy as np
        D_MODEL = 128
        D_FF = 512
        N_EXPERTS = 8
        TOP_K = 2

        def _ffn(x, w1, b1, w2, b2):
            h = jax.nn.gelu(x @ w1.T + b1)
            return h @ w2.T + b2
        B, T, D = x.shape
        xf = x.reshape(-1, D)
        U = xf.shape[0]
        logits = xf @ router_w.T + router_b
        routing = jax.nn.softmax(logits, axis=-1)
        sel_w, sel_idx = jax.lax.top_k(routing, TOP_K)
        sel_w = sel_w / sel_w.sum(axis=-1, keepdims=True)
        comb = jnp.zeros_like(routing).at[jnp.arange(U)[:, None], sel_idx].set(sel_w)
        shared_out = _ffn(xf, shared_w1, shared_b1, shared_w2, shared_b2)

        def body(acc, params):
            w1, b1, w2, b2, we = params
            return (acc + we[:, None] * _ffn(xf, w1, b1, w2, b2), None)
        acc0 = jnp.zeros_like(shared_out)
        acc, _ = jax.lax.scan(body, acc0, (spec_w1, spec_b1, spec_w2, spec_b2, comb.T))
        return (shared_out + acc).reshape(B, T, D)

    def _L1_attn_ref(x, ln_w, ln_b, Wq, Wk, Wv, Wb, o_norm_w, Wo):
        import jax, jax.numpy as jnp
        import numpy as np
        D = 128
        H = 4
        DK = 32
        DV = 64
        B, T = (4, 256)

        def _l2norm(t):
            return t * jax.lax.rsqrt(jnp.sum(t * t, axis=-1, keepdims=True) + 1e-06)
        Bx, Tx, _ = x.shape
        mu = jnp.mean(x, axis=-1, keepdims=True)
        var = jnp.mean((x - mu) ** 2, axis=-1, keepdims=True)
        normed = (x - mu) * jax.lax.rsqrt(var + 1e-05) * ln_w + ln_b
        silu = jax.nn.silu
        q = _l2norm(silu(normed @ Wq).reshape(Bx, Tx, H, DK)) * DK ** (-0.5)
        k = _l2norm(silu(normed @ Wk).reshape(Bx, Tx, H, DK))
        v = silu(normed @ Wv).reshape(Bx, Tx, H, DV)
        beta = jax.nn.sigmoid(normed @ Wb)
        qT = q.transpose(1, 0, 2, 3)
        kT = k.transpose(1, 0, 2, 3)
        vT = v.transpose(1, 0, 2, 3)
        bT = beta.transpose(1, 0, 2)

        def step(S, inp):
            qt, kt, vt, bt = inp
            pred = jnp.einsum('bhk,bhkv->bhv', kt, S)
            vd = bt[..., None] * (vt - pred)
            S = S + kt[..., None] * vd[..., None, :]
            o = jnp.einsum('bhk,bhkv->bhv', qt, S)
            return (S, o)
        S0 = jnp.zeros((Bx, H, DK, DV), x.dtype)
        _, oT = jax.lax.scan(step, S0, (qT, kT, vT, bT))
        o = oT.transpose(1, 0, 2, 3)
        o = o * jax.lax.rsqrt(jnp.mean(o * o, axis=-1, keepdims=True) + 1e-05) * o_norm_w
        out = o.reshape(Bx, Tx, H * DV) @ Wo
        return x + out

    def _L1_xattn_ref(query, key, value, Wq, bq, Wk, bk, Wv, bv, Wo, bo, ln_gamma, ln_beta):
        import jax, jax.numpy as jnp
        import numpy as np
        QUERY_DIM, KV_DIM, EMBED_DIM, NUM_HEADS = (128, 96, 128, 16)
        HEAD_DIM = EMBED_DIM // NUM_HEADS
        SCALE = HEAD_DIM ** (-0.5)
        LN_EPS = 1e-05

        def _l2norm(x, eps=1e-12):
            n = jnp.sqrt(jnp.sum(x * x, axis=-1, keepdims=True))
            return x / jnp.maximum(n, eps)
        B, Nq, _ = query.shape
        Nk = key.shape[1]
        Qp = query @ Wq + bq
        K = _l2norm(key @ Wk + bk)
        V = value @ Wv + bv
        Q = _l2norm(Qp)
        Q = Q.reshape(B, Nq, NUM_HEADS, HEAD_DIM).transpose(0, 2, 1, 3)
        K = K.reshape(B, Nk, NUM_HEADS, HEAD_DIM).transpose(0, 2, 1, 3)
        V = V.reshape(B, Nk, NUM_HEADS, HEAD_DIM).transpose(0, 2, 1, 3)
        scores = jnp.einsum('bhqd,bhkd->bhqk', Q, K) * SCALE
        attn = jax.nn.softmax(scores, axis=-1)
        out = jnp.einsum('bhqk,bhkd->bhqd', attn, V)
        out = out.transpose(0, 2, 1, 3).reshape(B, Nq, EMBED_DIM)
        out = out @ Wo + bo
        x = out + Qp
        mu = jnp.mean(x, axis=-1, keepdims=True)
        var = jnp.mean((x - mu) ** 2, axis=-1, keepdims=True)
        return (x - mu) / jnp.sqrt(var + LN_EPS) * ln_gamma + ln_beta

    def _L1_ffn_ref(x, gate_w, expert_gate, expert_up, expert_down, shared_gate, shared_up, shared_down):
        import jax, jax.numpy as jnp
        import numpy as np
        TOP_K = 2

        def _ffn(x, gw, uw, dw):
            return jax.nn.silu(x @ gw.T) * (x @ uw.T) @ dw.T
        B, S, H = x.shape
        xf = x.reshape(-1, H)
        T = xf.shape[0]
        E = expert_gate.shape[0]
        shared = _ffn(xf, shared_gate, shared_up, shared_down)
        logits = xf @ gate_w.T
        probs = jax.nn.softmax(logits, axis=-1)
        topw, topi = jax.lax.top_k(probs, TOP_K)
        topw = topw / (topw.sum(-1, keepdims=True) + 1e-20)
        comb = jnp.zeros((T, E), xf.dtype).at[jnp.arange(T)[:, None], topi].add(topw)

        def body(acc, ws):
            gw, uw, dw, wcol = ws
            return (acc + _ffn(xf, gw, uw, dw) * wcol[:, None], None)
        routed, _ = jax.lax.scan(body, jnp.zeros_like(xf), (expert_gate, expert_up, expert_down, comb.T))
        return (shared + routed).reshape(B, S, H)
    x = _layernorm(x + _L0_attn_ref(x, L0_attn_ln_g, L0_attn_ln_b, L0_attn_Wq, L0_attn_bq, L0_attn_Wk, L0_attn_bk, L0_attn_Wv, L0_attn_bv, L0_attn_Wo, L0_attn_bo), axis=-1)
    x = _layernorm(x + _L0_xattn_ref(x, ctx_768, L0_xattn_ln_gamma, L0_xattn_ln_beta, L0_xattn_Wq, L0_xattn_Wkv, L0_xattn_Wo, L0_xattn_bo, mask_1x1xSxS2_bk0), axis=-1)
    x = _layernorm(x + _L0_ffn_ref(x, L0_ffn_shared_w1, L0_ffn_shared_b1, L0_ffn_shared_w2, L0_ffn_shared_b2, L0_ffn_router_w, L0_ffn_router_b, L0_ffn_spec_w1, L0_ffn_spec_b1, L0_ffn_spec_w2, L0_ffn_spec_b2), axis=-1)
    x = _layernorm(x + _L1_attn_ref(x, L1_attn_ln_w, L1_attn_ln_b, L1_attn_Wq, L1_attn_Wk, L1_attn_Wv, L1_attn_Wb, L1_attn_o_norm_w, L1_attn_Wo), axis=-1)
    x = _layernorm(x + _L1_xattn_ref(x, ctx_768, ctx_768, L1_xattn_Wq, L1_xattn_bq, L1_xattn_Wk, L1_xattn_bk, L1_xattn_Wv, L1_xattn_bv, L1_xattn_Wo, L1_xattn_bo, L1_xattn_ln_gamma, L1_xattn_ln_beta), axis=-1)
    x = _layernorm(x + _L1_ffn_ref(x, L1_ffn_gate_w, L1_ffn_expert_gate, L1_ffn_expert_up, L1_ffn_expert_down, L1_ffn_shared_gate, L1_ffn_shared_up, L1_ffn_shared_down), axis=-1)
    return x

_drawn_inputs = setup_inputs


def setup_inputs(seed=0):
    import zlib

    import numpy as np

    out = dict(_drawn_inputs(seed))
    spreads = {'L0_attn_ln_g': (1.0, 0.6),
     'L0_attn_ln_b': (0.0, 0.8),
     'L0_attn_bq': (0.0, 0.8),
     'L0_attn_bk': (0.0, 0.8),
     'L0_attn_bv': (0.0, 0.585),
     'L0_attn_bo': (0.0, 0.1),
     'L0_xattn_ln_gamma': (1.0, 0.2),
     'L0_xattn_ln_beta': (0.0, 0.329),
     'L0_xattn_bo': (0.0, 0.1),
     'L0_ffn_shared_b1': (0.0, 0.327),
     'L0_ffn_shared_b2': (0.0, 0.1),
     'L0_ffn_router_b': (0.0, 0.1),
     'L0_ffn_spec_b1': (0.0, 0.409),
     'L0_ffn_spec_b2': (0.0, 0.1),
     'L1_attn_ln_w': (1.0, 0.2),
     'L1_attn_ln_b': (0.0, 0.1),
     'L1_attn_o_norm_w': (1.0, 0.2),
     'L1_xattn_bq': (0.0, 0.1),
     'L1_xattn_bk': (0.0, 0.8),
     'L1_xattn_bv': (0.0, 0.1),
     'L1_xattn_bo': (0.0, 0.1),
     'L1_xattn_ln_gamma': (1.0, 0.2),
     'L1_xattn_ln_beta': (0.0, 0.1)}
    factors = {'L0_attn_Wq': 8.0,
     'L0_attn_Wk': 8.0,
     'L0_attn_Wv': 2.746,
     'L1_xattn_Wk': 8.0,
     'L1_ffn_gate_w': 8.0,
     'L1_ffn_expert_gate': 8.0,
     'L1_ffn_expert_up': 8.0,
     'L1_ffn_expert_down': 8.0,
     'L1_ffn_shared_gate': 5.623,
     'L1_ffn_shared_up': 5.761,
     'L1_ffn_shared_down': 5.43}
    for name, (base, spread) in spreads.items():
        noise = np.random.default_rng([zlib.crc32(name.encode()), seed]).standard_normal(out[name].shape)
        drawn = base * np.exp(spread * noise) if base else spread * noise
        out[name] = jnp.asarray(drawn.astype(out[name].dtype))
    for name, factor in factors.items():
        out[name] = (out[name] * factor).astype(out[name].dtype)
    return out
```

```python
import numpy as np
import concourse.bass as bass
from concourse import mybir
from contextlib import ExitStack

FP = mybir.dt.float32
U32 = mybir.dt.uint32
I32 = mybir.dt.int32
U8 = mybir.dt.uint8
ALU = mybir.AluOpType
ACT = mybir.ActivationFunctionType
AX = mybir.AxisListType

P = 128
B, S, D = 2, 512, 128
HT = S // P
NT = B * HT
CTX, CD = 77, 96
XH, XD = 16, 64
XI = XH * XD
E = 8
NE = E + 1
F0 = 512
C0 = F0 // P
F1 = 352
F1C = [(0, 128), (128, 128), (256, 96)]
GH, GK, GV = 4, 32, 64
CH = 32
NC = S // CH
NM = HT * GH
EH = 16
EP = EH * CTX
EK = (EP + P - 1) // P
ARENA = 17600
MAGIC = float(0x5F3759DF)

COLS = ["a_g", "a_b", "a_bq", "a_bk", "a_bv", "x_g", "x_b", "d_g", "d_b", "e_bq"]
ROWS = [("a_bo", 128), ("x_bo", 128), ("f_b2", 128), ("e_bq", 128), ("e_bk", 128), ("e_bv", 128),
        ("e_bo", 128), ("e_g", 128), ("e_b", 128), ("d_on", 64), ("f_rb", 8)]
ROFF = {}
_o = 0
for _n, _w in ROWS:
    ROFF[_n] = (_o, _w)
    _o += _w
RTOT = _o
TABS = [("ident", 128), ("head8", 128), ("low_neg", 32), ("low_incl", 32), ("eye", 32), ("pair", 32),
        ("blk_neg", 128), ("ehead", EH), ("iota", 8), ("vmask", EK * 144)]
TOFF = {}
_o = 0
for _n, _w in TABS:
    TOFF[_n] = (_o, _w)
    _o += _w
TTOT = _o


def program(nc, a):
    ctx = ExitStack()
    with ctx:
        def sb(name, shape, dt=FP):
            return ctx.enter_context(nc.sbuf_tensor(name, shape, dt))

        def sem(name):
            return ctx.enter_context(nc.semaphore(name))

        ps = ctx.enter_context(nc.psum_tensor("ps", [P, 8, 512], FP))

        tabs = sb("tabs", [P, TTOT])
        cols = sb("cols", [P, len(COLS)])
        rows = sb("rows", [P, RTOT])
        level_mask = sb("level_mask", [P, 4, 32], U32)
        spread = sb("spread", [CTX, EK * P])
        ctxT = sb("ctxT", [CD, B * CTX])
        mask_u8 = sb("mask_u8", [P, HT, CTX], U8)
        mask_f = sb("mask_f", [P, HT, CTX])
        wa = sb("wa", [P, 4, 128])
        wx = sb("wx", [P, 4 * XI])
        wxq, wxkv = wx[:, 0:XI], wx[0:CD, XI:3 * XI]
        wxo = wx[:, 3 * XI:4 * XI].rearrange("p (c d) -> p c d", c=8)
        w1f = sb("w1f", [P, NE * F0])
        w2f = sb("w2f", [P, NE * F0])
        w1 = w1f[:, :].rearrange("p (e f) -> p e f", e=NE)
        w2 = w2f[:, :].rearrange("p (e c d) -> p e c d", e=NE, c=C0)
        fb1 = sb("fb1", [P, NE, C0])
        fb2 = sb("fb2", [E, 128])
        router = sb("router", [P, 2, E])
        wd = sb("wd", [P, 516])
        wdo = sb("wdo", [P, 2, 128])
        we = sb("we", [P, 2, 128])
        wekv = sb("wekv", [CD, 256])

        def tab(n):
            return tabs[:, TOFF[n][0]:TOFF[n][0] + TOFF[n][1]]

        def row(n):
            return rows[:, ROFF[n][0]:ROFF[n][0] + ROFF[n][1]]

        def col(n):
            return cols[:, COLS.index(n):COLS.index(n) + 1]

        ident = tab("ident")

        z = sb("z", [P, NT, D])
        xT = sb("xT", [P, B * S])
        res = sb("res", [P, NT, D])
        pre = sb("pre", [P, NT, D])
        bn6 = sb("bn6", [P, NT, 6])
        bn2 = sb("bn2", [P, NT, 2])
        rt = sb("rt", [P, 3, 64])
        arena = sb("arena", [P, ARENA])
        hid = sb("hid", [P, 2, 4, 512])
        sm = sb("sm", [P, 512])
        idx = sb("idx", [P, HT, 8], U32)
        comb = sb("comb", [P, NT, E])
        combT = sb("combT", [E, 2, 512])

        class Carve:
            def __init__(self):
                self.at = 0

            def __call__(self, *dims):
                n = int(np.prod(dims))
                v = arena[:, self.at:self.at + n]
                self.at += n
                assert self.at <= ARENA, self.at
                names = " ".join(f"d{i}" for i in range(len(dims)))
                if len(dims) > 1:
                    v = v.rearrange(f"p ({names}) -> p {names}", **{f"d{i}": d for i, d in enumerate(dims) if i})
                return v

        cut = Carve()
        a_qkv = cut(3, B * S)
        a_kd, a_vd, a_vs = cut(S), cut(S), cut(S)
        a_prod, a_th, a_o = cut(B * S), cut(B * S), cut(B * S)
        cut = Carve()
        b_q = cut(8, 512)
        b_kT = cut(8, B * CTX)
        b_v = cut(B, XI)
        b_s = cut(3, 4, 4 * CTX)
        b_pT = cut(16, 128)
        b_o = cut(2, XI)
        b_oT = cut(8, 128)
        cut = Carve()
        d_qk = cut(2, HT, 8, GK)
        d_r = cut(2, HT, GH, GV + GK)
        d_u = cut(2, HT, GH, GV)
        d_w = cut(2, HT, GH * GK)
        d_S = cut(NC, 2, GV)
        d_X = cut(2, NM, CH)
        d_Y = cut(2, NM, CH)
        d_P = cut(2, NM, CH)
        pbd = cut(2 * NM, 128)
        d_o = d_r.rearrange("p b t h w -> p (b t h w)")[:, 0:2 * HT * GH * GV].rearrange(
            "p (b t h w) -> p b t h w", b=2, t=HT, h=GH)
        d_sq = d_u
        abd = w1f[:, 0:2 * NM * 128].rearrange("p (m j) -> p m j", j=128)
        ybd = w2f[:, 0:2 * NM * 128].rearrange("p (m j) -> p m j", j=128)
        d_T = wx[:, 0:3072].rearrange("p (b w n) -> p b w n", b=2, w=3)
        d_wT = wx[:, 3072:4096].rearrange("p (b n) -> p b n", b=2)
        e_kT = w1f[:, 0:B * EP].rearrange("p (b n) -> p b n", b=B)
        e_q = w1f[:, B * EP:B * EP + 1024].rearrange("p (b n) -> p b n", b=B)
        e_o = w1f[:, B * EP + 1024:B * EP + 1280].rearrange("p (b n) -> p b n", b=2)
        e_oT = w1f[:, B * EP + 1280:B * EP + 1536].rearrange("p (b n) -> p b n", b=2)
        e_vb = w2f[:, 0:B * EK * 144].rearrange("p (b k n) -> p b k n", b=B, k=EK)
        e_kv = w1f[0:CTX, B * EP:B * EP + B * 272].rearrange("p (b n) -> p b n", b=B)
        e_p = hid[:, :, :, :].rearrange("p a c n -> p (a c n)")[:, 0:2 * EP].rearrange("p (a n) -> p a n", a=2)
        e_pT = w2f[:, B * EK * 144:B * EK * 144 + EK * 128].rearrange("p (k n) -> p k n", k=EK)
        f_gu = arena[:, 0:NE * 2 * F1].rearrange("p (e g f) -> p e g f", e=NE, g=2)
        f_dn = arena[:, NE * 2 * F1:NE * 2 * F1 + NE * 384].rearrange("p (e c d) -> p e c d", e=NE, c=3)

        sems = {}

        def s(name):
            if name not in sems:
                sems[name] = sem(name)
            return sems[name]

        LOADS = [("x", res[:, :, :], a["x"].rearrange("(t p) d -> p t d", p=P)),
                 ("tabs", tabs[:, :], a["tabs"]),
                 ("cols", cols[:, :], a["cols"]),
                 ("wa", wa[:, :, :], a["wa"]),
                 ("rows", rows[:, :], a["rows"].partition_broadcast(P)),
                 ("ctxT", ctxT[:, :], a["ctxT"]),
                 ("wxkv", wxkv, a["wxkv"]),
                 ("wxq", wxq, a["wxq"]),
                 ("mask", mask_u8[:, :, :], a["mask"].rearrange("(t p) k -> p t k", p=P)),
                 ("wxo", wxo, a["wxo"]),
                 ("router", router[:, :, :], a["router"]),
                 ("fb2", fb2[:, :], a["fb2"]),
                 ("fb1", fb1[:, :, :], a["fb1"]),
                 ("w1", w1, a["w1"]),
                 ("w2", w2, a["w2"]),
                 ("lm", level_mask[:, :, :], a["level_mask"]),
                 ("wd", wd[:, :], a["wd"]),
                 ("wdo", wdo[:, :, :], a["wdo"]),
                 ("we", we[:, :, :], a["we"]),
                 ("wekv", wekv[:, :], a["wekv"]),
                 ("spread", spread[:, :], a["spread"])]

        def need(eng, *names):
            for n in names:
                eng.wait_ge(s("in_" + n), 16)

        A, X, F, G, EX, H = range(6)

        def nth(use, half):
            return 2 * use + half + 1

        def tok(half):
            return slice(half * S, half * S + S)

        def til(half):
            return slice(half * HT, half * HT + HT)

        NI = NT + 3
        RING = []
        for i in range(NI):
            if i in (0, HT):
                RING += [("q", i // HT, r) for r in range(8)]
            if 2 <= i < NT + 2:
                RING += [("pT", i - 2, r) for r in range(4)]
            if 3 <= i:
                RING += [("oT", i - 3, r) for r in range(2)] + [("y", i - 3, 0)]
        RAT = {e: n for n, e in enumerate(RING)}

        def ring_free(eng, n):
            if n >= 2:
                kind = RING[n - 2][0]
                if kind == "y":
                    eng.wait_ge(s("b_yadd"), 1 + sum(e[0] == "y" for e in RING[:n - 2]))
                else:
                    eng.wait_ge(s("b_ringed"), 1 + sum(e[0] != "y" for e in RING[:n - 2]))

        def head_at(h):
            return 2 * (h // 8) + h % 2, (h // 2) % 4

        def r_l(half):
            return sm[:, 64 + 32 * half:96 + 32 * half].rearrange("p (t e) -> p t e", e=E)

        def r_e(half):
            return sm[:, 160 + 32 * half:192 + 32 * half].rearrange("p (t e) -> p t e", e=E)

        block = ctx.enter_context(nc.Block())

        @block.sync
        def _(sp):
            for name, dst, src in LOADS:
                sp.dma_start(dst, src).then_inc(s("in_" + name), 16)
            sp.wait_ge(s("z_ready"), nth(EX, 1))
            sp.dma_start(f_gu, a["f_gu"]).then_inc(s("in_f_gu"), 16)
            sp.dma_start(f_dn, a["f_dn"]).then_inc(s("in_f_dn"), 16)
            for half in range(2):
                sp.wait_ge(s("out_ready"), half + 1)
                sp.dma_start(a["out"].rearrange("(t p) d -> p t d", p=P)[:, til(half), :],
                             res[:, til(half), :]).then_inc(s("stored"), 16)
            sp.wait_ge(s("stored"), 32)

        @block.gpsimd
        def _(pool):
            for t in range(NT):
                pool.wait_ge(s("b_max"), t + 1)
                nc.gpsimd.tensor_tensor(
                    b_s[:, t % 3, :, :].rearrange("p i (j k) -> p (i j) k", k=CTX),
                    b_s[:, t % 3, :, :].rearrange("p i (j k) -> p (i j) k", k=CTX),
                    sm[:, 16 * (t % 3):16 * (t % 3) + 16].unsqueeze(2).to_broadcast([P, 16, CTX]),
                    ALU.subtract).then_inc(s("b_sub"), 1)
            pool.wait_ge(s("c_acc"), 2 * NE)
            nc.gpsimd.memset(w1f[:, 0:2 * NM * 128], 0.0)
            nc.gpsimd.memset(w2f[:, 0:2 * NM * 128], 0.0)
            nc.gpsimd.memset(pbd, 0.0)
            nc.gpsimd.memset(d_S[:, 0, :, :], 0.0).then_inc(s("d_zero"), 1)
            pool.wait_ge(s("d_zero"), 1)
            for v in range(5):
                for half in range(2):
                    pool.wait_ge(s("d_inv"), 2 * v + half + 1)
                    for c in (2, 3):
                        q = slice(CH * c, CH * c + CH)
                        ins = nc.gpsimd.tensor_copy(ybd[q, NM * half:NM * half + NM, q], d_Y[q, half, :, :])
                    ins.then_inc(s("d_diag_p"), 1)

        @block.scalar
        def _(act):
            def turn(use, half, g=None, b=None):
                act.wait_ge(s("turned"), nth(use, half))
                kw = dict(scale=col(g), bias=col(b)) if g else {}
                nc.scalar.activation(xT[:, tok(half)], ps[:, 6 + half, :], ACT.Identity, **kw).then_inc(
                    s("xT_ready"), 1)

            need(act, "cols")
            for half in range(2):
                turn(A, half, "a_g", "a_b")
            for half in range(2):
                for j, bias in enumerate(("a_bq", "a_bk", "a_bv")):
                    act.wait_ge(s("a_qkv_ps"), 3 * half + j + 1)
                    nc.scalar.activation(a_qkv[:, j, tok(half)], ps[:, 3 * half + j, :], ACT.Identity,
                                         bias=col(bias)).then_inc(s("a_qkv"), 1)
            for half in range(2):
                act.wait_ge(s("a_gap"), half + 1)
                nc.scalar.activation(a_th[:, tok(half)], ps[:, 3 * half, :], ACT.Tanh,
                                     scale=0.5 * 8.0 ** -0.5).then_inc(s("a_th"), 1)
            act.wait_ge(s("a_o"), 2)
            for g in range(7):
                act.wait_ge(s("b_kv_ps"), g + 1)
                if g < 3:
                    w = min(3, 8 - 3 * g)
                    ins = nc.scalar.activation(
                        b_kT[:, 3 * g:3 * g + w, :],
                        ps[:, 6 + g % 2, 0:w * B * CTX].rearrange("p (c n) -> p c n", c=w), ACT.Copy)
                else:
                    b, n = divmod(g - 3, 2)
                    ins = nc.scalar.activation(b_v[0:CTX, b, 512 * n:512 * n + 512],
                                               ps[0:CTX, 6 + g % 2, :], ACT.Copy)
                ins.then_inc(s("b_kv"), 1)
            for half in range(2):
                turn(X, half, "x_g", "x_b")
            for i in range(NI):
                if i in (0, HT):
                    for r in range(8):
                        act.wait_ge(s("b_ring"), RAT[("q", i // HT, r)] + 1)
                        nc.scalar.activation(b_q[:, r, :], ps[:, 4 + RAT[("q", i // HT, r)] % 2, :], ACT.Copy,
                                             scale=XD ** -0.5).then_inc(s("b_ringed"), 1)
                if 2 <= i < NT + 2:
                    for r in range(4):
                        n = RAT[("pT", i - 2, r)]
                        act.wait_ge(s("b_ring"), n + 1)
                        nc.scalar.activation(
                            b_pT[0:CTX, 4 * r:4 * r + 4, :],
                            ps[0:CTX, 4 + n % 2, :].rearrange("p (j n) -> p j n", j=4),
                            ACT.Copy).then_inc(s("b_ringed"), 1)
                if 3 <= i:
                    for r in range(2):
                        n = RAT[("oT", i - 3, r)]
                        act.wait_ge(s("b_ring"), n + 1)
                        nc.scalar.activation(b_oT[:, 4 * r:4 * r + 4, :],
                                             ps[:, 4 + n % 2, :].rearrange("p (j n) -> p j n", j=4),
                                             ACT.Copy).then_inc(s("b_ringed"), 1)
                if i < NT:
                    act.wait_ge(s("b_sub"), i + 1)
                    nc.scalar.activation(b_s[:, i % 3, :, :], b_s[:, i % 3, :, :], ACT.Exp).then_inc(
                        s("b_exp"), 1)
            for half in range(2):
                turn(F, half)
            for half in range(2):
                act.wait_ge(s("r_shift"), half + 1)
                nc.scalar.activation(r_e(half), r_e(half), ACT.Exp).then_inc(s("r_exp"), 1)
            for half in range(2):
                for e in range(NE):
                    g = NE * half + e
                    for c in range(C0):
                        if g == 0 and c == 0:
                            need(act, "fb1")
                        act.wait_ge(s("c_h_ps"), C0 * g + c + 1)
                        nc.scalar.activation(hid[:, g % 2, c, :], ps[:, c, :], ACT.Gelu_apprx_tanh,
                                             bias=fb1[:, e, c:c + 1]).then_inc(s("c_h"), 1)
                    if e == 1:
                        act.wait_ge(s("c_combT_ps"), half + 1)
                        nc.scalar.activation(combT[:, half, :], ps[0:E, 6 + half, :], ACT.Copy).then_inc(
                            s("c_combT"), 1)
            for half in range(2):
                turn(G, half, "d_g", "d_b")
            for half in range(2):
                for t in range(HT):
                    act.wait_ge(s("d_qkv"), HT * half + t + 1)
                    nc.scalar.activation(hid[:, half, t, :], ps[:, 4 * half + t, :], ACT.Silu).then_inc(
                        s("d_silu"), 1)
                act.wait_ge(s("d_beta_ps"), half + 1)
                nc.scalar.activation(sm[:, 128 + 16 * half:144 + 16 * half], ps[:, 4 * half, 0:16], ACT.Tanh,
                                     scale=0.5).then_inc(s("d_tanh"), 1)
            for half in range(2):
                for w in range(3):
                    act.wait_ge(s("d_turn_ps"), 3 * half + w + 1)
                    nc.scalar.activation(d_T[:, half, w, :], ps[:, 4 * half + w, :], ACT.Copy).then_inc(
                        s("d_turn"), 1)
            act.wait_ge(s("d_zero"), 1)
            for v in range(5):
                for half in range(2):
                    act.wait_ge(s("d_inv"), 2 * v + half + 1)
                    for c in (0, 1):
                        q = slice(CH * c, CH * c + CH)
                        ins = nc.scalar.activation(ybd[q, NM * half:NM * half + NM, q], d_Y[q, half, :, :],
                                                   ACT.Copy)
                    ins.then_inc(s("d_diag_a"), 1)
                    if v < 4:
                        act.wait_ge(s("d_ax"), 2 * v + half + 1)
                        nc.scalar.activation(d_P[:, half, :, :],
                                             ps[:, 4 * half, :].rearrange("p (m j) -> p m j", j=CH),
                                             ACT.Copy).then_inc(s("d_p"), 1)
            for half in range(2):
                act.wait_ge(s("d_uw_ps"), half + 1)
                uw = ps[:, 4 * half:4 * half + 4, 0:384].rearrange("p t (h w) -> p t h w", h=GH)
                for t in range(HT):
                    nc.scalar.activation(d_u[:, half, t, :, :], uw[:, t, :, 0:GV], ACT.Copy)
                    ins = nc.scalar.activation(d_w[:, half, t, :].rearrange("p (h k) -> p h k", h=GH),
                                               uw[:, t, :, GV:96], ACT.Copy)
                ins.then_inc(s("d_uw"), 1)
            for half in range(2):
                act.wait_ge(s("d_wT_ps"), half + 1)
                nc.scalar.activation(d_wT[:, half, :], ps[:, 4 * half, :], ACT.Copy).then_inc(s("d_wT"), 1)
            for half in range(2):
                for w in range(2):
                    act.wait_ge(s("d_oT_ps"), 2 * half + w + 1)
                    nc.scalar.activation(d_T[:, half, w, :], ps[:, 4 * half + w, :], ACT.Copy).then_inc(
                        s("d_oT"), 1)
            for b in range(B):
                act.wait_ge(s("e_kT_ps"), b + 1)
                nc.scalar.activation(d_wT[:, b, 0:CTX], ps[:, b, 0:CTX], ACT.Copy).then_inc(s("e_kT1"), 1)
            for half in range(2):
                turn(EX, half)
            for half in range(2):
                act.wait_ge(s("e_q_ps"), half + 1)
                nc.scalar.activation(e_q[:, half, :], ps[:, 2 * half, :], ACT.Identity,
                                     bias=col("e_bq")).then_inc(s("e_q"), 1)
            for i in range(NT + 2):
                if i < NT:
                    act.wait_ge(s("e_sc"), i + 1)
                    act.wait_ge(s("e_scale"), i // HT + 1)
                    nc.scalar.activation(e_p[:, i % 2, :].rearrange("p (i k) -> p i k", i=4),
                                         ps[:, 0:4, 0:4 * CTX], ACT.Exp,
                                         scale=sm[:, 256 + i:257 + i]).then_inc(s("e_exp"), 1)
                if 1 <= i <= NT:
                    for r in range(3):
                        n = 3 * (i - 1) + r
                        m = 4 if r < 2 else 2
                        act.wait_ge(s("e_pT_ps"), n + 1)
                        if r < 2:
                            ins = nc.scalar.activation(e_pT[:, 4 * r:4 * r + 4, :],
                                                       ps[:, 4 + n % 2, :].rearrange("p (k n) -> p k n", k=4),
                                                       ACT.Copy)
                        else:
                            nc.scalar.activation(e_pT[:, 8, :], ps[:, 4 + n % 2, 0:128], ACT.Copy)
                            ins = nc.scalar.activation(e_pT[0:EP - 9 * 128, 9, :],
                                                       ps[0:EP - 9 * 128, 4 + n % 2, 128:256], ACT.Copy)
                        ins.then_inc(s("e_pT"), 1)
                if 2 <= i:
                    t = i - 2
                    act.wait_ge(s("e_oT_ps"), t + 1)
                    nc.scalar.activation(e_oT[:, t % 2, :], ps[:, 6 + t % 2, 256:384], ACT.Copy).then_inc(
                        s("e_oT"), 1)
            for half in range(2):
                turn(H, half)
            for half in range(2):
                act.wait_ge(s("r_shift"), 2 + half + 1)
                nc.scalar.activation(r_e(half), r_e(half), ACT.Exp).then_inc(s("r_exp"), 1)
            for g in range(2 * NE):
                for c in range(3):
                    n = 3 * g + c
                    w = F1C[c][1]
                    act.wait_ge(s("f_gate_ps"), n + 1)
                    nc.scalar.activation(hid[0:w, g % 2, c, :], ps[0:w, 2 * (n % 2), :], ACT.Silu).then_inc(
                        s("f_silu"), 1)

        @block.vector
        def _(dve):
            done = [0]

            def link(ins):
                done[0] += 1
                ins.then_inc(s("dve_chain"), 1)
                dve.wait_ge(s("dve_chain"), done[0])

            def bc(ap, shape):
                return ap.to_broadcast(shape)

            def inv_sqrt(v, y, w):
                link(nc.vector.tensor_scalar(w.bitcast(U32), v.bitcast(U32), 1, None,
                                             ALU.logical_shift_right))
                link(nc.vector.tensor_scalar(y.bitcast(I32), w.bitcast(I32), -1.0, MAGIC, ALU.mult, ALU.add))
                for _ in range(3):
                    link(nc.vector.tensor_tensor(w, y, y, ALU.mult))
                    link(nc.vector.scalar_tensor_tensor(w, w, -0.5, v, ALU.mult, ALU.mult))
                    link(nc.vector.scalar_tensor_tensor(y, w, 1.5, y, ALU.add, ALU.mult))

            def norm(src, dst, half):
                for t in range(HT * half, HT * half + HT):
                    ins = nc.vector.bn_stats(bn6[:, t, :], src[:, t, :])
                link(ins)
                for t in range(HT * half, HT * half + HT):
                    ins = nc.vector.bn_aggr(bn2[:, t, :], bn6[:, t, :])
                link(ins)
                v, w, y = rt[:, 0, 0:HT], rt[:, 1, 0:HT], rt[:, 2, 0:HT]
                link(nc.vector.tensor_scalar(v, bn2[:, til(half), 1], 1e-5, None, ALU.add))
                inv_sqrt(v, y, w)
                for t in range(HT):
                    ins = nc.vector.tensor_scalar(dst[:, HT * half + t, :], src[:, HT * half + t, :],
                                                  bn2[:, HT * half + t, 0:1], y[:, t:t + 1],
                                                  ALU.subtract, ALU.mult)
                return ins

            def rowb(n, k):
                return row(n).unsqueeze(1).to_broadcast([P, k, ROFF[n][1]])

            def route(which, half, extra, eps):
                L, Ex = r_l(half), r_e(half)
                dve.wait_ge(s("r_logit"), 2 * which + half + 1)
                lp = ps[:, 6 + half, 0:HT * E].rearrange("p (t e) -> p t e", e=E)
                if extra is None:
                    link(nc.vector.tensor_copy(L, lp))
                else:
                    link(nc.vector.tensor_tensor(L, lp, rowb(extra, HT), ALU.add))
                m = sm[:, 300:304]
                link(nc.vector.tensor_reduce(m, L, AX.X, ALU.max))
                nc.vector.tensor_tensor(Ex, L, m.unsqueeze(2).to_broadcast([P, HT, E]),
                                        ALU.subtract).then_inc(s("r_shift"), 1)
                dve.wait_ge(s("r_exp"), 2 * which + half + 1)
                link(nc.vector.tensor_reduce(m, Ex, AX.X, ALU.add))
                link(nc.vector.reciprocal(sm[:, 308:312], m))
                link(nc.vector.tensor_tensor(L, Ex, sm[:, 308:312].unsqueeze(2).to_broadcast([P, HT, E]),
                                             ALU.mult))
                top = sm[:, 320:352].rearrange("p (t e) -> p t e", e=E)
                for t in range(HT):
                    ins = nc.vector.max(top[:, t, :], L[:, t, :])
                link(ins)
                for t in range(HT):
                    ins = nc.vector.max_index(idx[:, t, :], top[:, t, :], L[:, t, :])
                link(ins)
                at = sm[:, 352:384].rearrange("p (t e) -> p t e", e=E)
                link(nc.vector.tensor_copy(at, idx[:, :, :]))
                link(nc.vector.tensor_tensor(sm[:, 312:316], top[:, :, 0], top[:, :, 1], ALU.add))
                if eps:
                    link(nc.vector.tensor_scalar(sm[:, 312:316], sm[:, 312:316], eps, None, ALU.add))
                link(nc.vector.reciprocal(sm[:, 316:320], sm[:, 312:316]))
                link(nc.vector.tensor_tensor(top[:, :, 0:2], top[:, :, 0:2],
                                             sm[:, 316:320].unsqueeze(2).to_broadcast([P, HT, 2]), ALU.mult))
                iota = tab("iota").unsqueeze(1).to_broadcast([P, HT, E])
                hit = [sm[:, 384:416].rearrange("p (t e) -> p t e", e=E),
                       sm[:, 416:448].rearrange("p (t e) -> p t e", e=E)]
                for k in range(2):
                    link(nc.vector.tensor_tensor(hit[k], iota,
                                                 at[:, :, k:k + 1].to_broadcast([P, HT, E]), ALU.is_equal))
                    link(nc.vector.tensor_tensor(hit[k], hit[k],
                                                 top[:, :, k:k + 1].to_broadcast([P, HT, E]), ALU.mult))
                nc.vector.tensor_tensor(comb[:, til(half), :], hit[0], hit[1], ALU.add).then_inc(
                    s("r_comb"), 1)
                dve.wait_ge(s("r_comb"), 2 * which + half + 1)

            need(dve, "x")
            for half in range(2):
                norm(res, z, half).then_inc(s("z_ready"), 1)
            need(dve, "rows")
            for half in range(2):
                nc.vector.scalar_tensor_tensor(pre[:, til(half), :], res[:, til(half), :], 2.0,
                                               rowb("a_bo", HT), ALU.mult, ALU.add)
            need(dve, "mask")
            link(nc.vector.tensor_copy(mask_f[:, :, :], mask_u8[:, :, :]))
            link(nc.vector.tensor_scalar(mask_f[:, :, :], mask_f[:, :, :], 1.0, 1e30, ALU.subtract, ALU.mult))
            dve.wait_ge(s("a_qkv"), 6)
            link(nc.vector.tensor_tensor(a_kd, a_qkv[:, 1, tok(0)], a_qkv[:, 1, tok(1)], ALU.subtract))
            for half in range(2):
                nc.vector.tensor_tensor(a_prod[:, tok(half)], a_qkv[:, 0, tok(half)], a_kd, ALU.mult).then_inc(
                    s("a_prod"), 1)
            nc.vector.tensor_tensor(a_vd, a_qkv[:, 2, tok(0)], a_qkv[:, 2, tok(1)], ALU.subtract)
            link(nc.vector.tensor_tensor(a_vs, a_qkv[:, 2, tok(0)], a_qkv[:, 2, tok(1)], ALU.add))
            for half in range(2):
                dve.wait_ge(s("a_th"), half + 1)
                link(nc.vector.scalar_tensor_tensor(a_th[:, tok(half)], a_th[:, tok(half)], 0.5, a_vd,
                                                    ALU.mult, ALU.mult))
                nc.vector.scalar_tensor_tensor(a_o[:, tok(half)], a_vs, 0.5, a_th[:, tok(half)],
                                               ALU.mult, ALU.add).then_inc(s("a_o"), 1)

            def join(half, bank, name, n):
                dve.wait_ge(s(name), n)
                link(nc.vector.tensor_tensor(pre[:, til(half), :],
                                             ps[:, bank, :].rearrange("p (t d) -> p t d", t=HT),
                                             pre[:, til(half), :], ALU.add))

            for half in range(2):
                join(half, 3 * half + 1, "a_y", half + 1)
                link(norm(pre, res, half))
                norm(res, z, half).then_inc(s("z_ready"), 1)
                link(nc.vector.tensor_tensor(pre[:, til(half), :], res[:, til(half), :], rowb("x_bo", HT),
                                             ALU.add))

            rs = [sm[:, 48:64], sm[:, 448:464], sm[:, 464:480]]
            for i in range(NI):
                if i < NT:
                    dve.wait_ge(s("b_sc"), i + 1)
                    link(nc.vector.tensor_tensor(
                        b_s[:, i % 3, :, :].rearrange("p i (j k) -> p i j k", k=CTX),
                        ps[:, 0:4, 0:4 * CTX].rearrange("p i (j k) -> p i j k", k=CTX),
                        mask_f[:, i % HT, :].unsqueeze(1).unsqueeze(1).to_broadcast([P, 4, 4, CTX]), ALU.add))
                    nc.vector.tensor_reduce(sm[:, 16 * (i % 3):16 * (i % 3) + 16],
                                            b_s[:, i % 3, :, :].rearrange("p i (j k) -> p (i j) k", k=CTX),
                                            AX.X, ALU.max).then_inc(s("b_max"), 1)
                if 1 <= i <= NT:
                    t = i - 1
                    dve.wait_ge(s("b_exp"), t + 1)
                    link(nc.vector.tensor_reduce(sm[:, 480:496],
                                                 b_s[:, t % 3, :, :].rearrange("p i (j k) -> p (i j) k", k=CTX),
                                                 AX.X, ALU.add))
                    link(nc.vector.reciprocal(rs[t % 3].rearrange("p (a j q) -> p a q j", a=2, q=2),
                                              sm[:, 480:496].rearrange("p (a q j) -> p a q j", a=2, q=2)))
                if 2 <= i < NT + 2:
                    t = i - 2
                    dve.wait_ge(s("b_pv"), t + 1)
                    nc.vector.tensor_tensor(
                        b_o[:, t % 2, :].rearrange("p (h d) -> p h d", d=XD),
                        ps[:, 6:8, :].rearrange("p b (h d) -> p (b h) d", d=XD),
                        rs[t % 3].unsqueeze(2).to_broadcast([P, XH, XD]), ALU.mult).then_inc(s("b_o"), 1)
                if 3 <= i:
                    t = i - 3
                    n = RAT[("y", t, 0)]
                    dve.wait_ge(s("b_ring"), n + 1)
                    nc.vector.tensor_tensor(pre[:, t, :], ps[:, 4 + n % 2, 0:128], pre[:, t, :],
                                            ALU.add).then_inc(s("b_yadd"), 1)
                    if t % HT == HT - 1:
                        dve.wait_ge(s("b_yadd"), t + 1)
                        half = t // HT
                        link(norm(pre, res, half))
                        nc.vector.tensor_tensor(pre[:, til(half), :], res[:, til(half), :],
                                                rowb("f_b2", HT), ALU.add).then_inc(s("z_ready"), 1)

            need(dve, "tabs")
            for half in range(2):
                route(0, half, "f_rb", None)

            def gather(which, half, e, bank):
                for t in range(HT * half, HT * half + HT):
                    y = ps[:, bank, 128 * (t % HT):128 * (t % HT) + 128]
                    if e == 0:
                        ins = nc.vector.tensor_tensor(pre[:, t, :], y, pre[:, t, :], ALU.add)
                    else:
                        ins = nc.vector.scalar_tensor_tensor(pre[:, t, :], y, comb[:, t, e - 1:e],
                                                             pre[:, t, :], ALU.mult, ALU.add)
                return ins

            for half in range(2):
                for e in range(NE):
                    g = NE * half + e
                    dve.wait_ge(s("c_y"), g + 1)
                    gather(0, half, e, 4 + g % 2).then_inc(s("c_acc"), 1)
                    dve.wait_ge(s("c_acc"), g + 1)
                    if e == 1:
                        join(half, 6 + half, "c_b2", half + 1)
                link(norm(pre, res, half))
                norm(res, z, half).then_inc(s("z_ready"), 1)
                nc.vector.tensor_tensor(pre[:, til(half), :], res[:, til(half), :], res[:, til(half), :],
                                        ALU.add)

            for half in range(2):
                v = hid[:, half, :, :]
                qk = v[:, :, 0:256].rearrange("p t (h k) -> p t h k", k=GK)
                beta = sm[:, 128 + 16 * half:144 + 16 * half]
                dve.wait_ge(s("d_silu"), HT * half + HT)
                sq = d_sq[:, half, :, :, :].rearrange("p t h w -> p (t h w)").rearrange(
                    "p (t h k) -> p t h k", t=HT, h=8)
                link(nc.vector.tensor_tensor(sq, qk, qk, ALU.mult))
                vv, ww, yy = rt[:, 0, 0:32], rt[:, 1, 0:32], rt[:, 2, 0:32]
                link(nc.vector.tensor_reduce(vv.rearrange("p (t h) -> p t h", t=HT), sq, AX.X, ALU.add))
                link(nc.vector.tensor_scalar(vv, vv, 1e-6, None, ALU.add))
                inv_sqrt(vv, yy, ww)
                y3 = yy.rearrange("p (t h) -> p t h", t=HT)
                link(nc.vector.tensor_scalar(y3[:, :, 0:GH], y3[:, :, 0:GH], GK ** -0.5, None, ALU.mult))
                link(nc.vector.tensor_tensor(d_qk[:, half, :, :, :], qk,
                                             y3.unsqueeze(3).to_broadcast([P, HT, 8, GK]), ALU.mult))
                dve.wait_ge(s("d_tanh"), half + 1)
                link(nc.vector.tensor_scalar(beta, beta, 0.5, 0.5, ALU.mult, ALU.add))
                b3 = beta.rearrange("p (t h) -> p t h", t=HT)
                nc.vector.tensor_tensor(d_r[:, half, :, :, 0:GV],
                                        v[:, :, 256:512].rearrange("p t (h w) -> p t h w", w=GV),
                                        b3.unsqueeze(3).to_broadcast([P, HT, GH, GV]), ALU.mult)
                nc.vector.tensor_tensor(d_P[:, half, :, :].rearrange("p (t h) k -> p t h k", t=HT),
                                        d_qk[:, half, :, 4:8, :],
                                        b3.unsqueeze(3).to_broadcast([P, HT, GH, GK]), ALU.mult)
                nc.vector.tensor_tensor(d_r[:, half, :, :, GV:96], d_qk[:, half, :, 4:8, :],
                                        b3.unsqueeze(3).to_broadcast([P, HT, GH, GK]), ALU.mult).then_inc(
                    s("d_norm"), 1)
            dve.wait_ge(s("d_zero"), 1)
            for half in range(2):
                dve.wait_ge(s("d_gram"), half + 1)
                mm = slice(NM * half, NM * half + NM)
                gr = ps[:, 4 * half:4 * half + 4, 0:256].rearrange("p h (t w i) -> p h t w i", t=HT, w=2)
                for c in range(4):
                    q = slice(CH * c, CH * c + CH)
                    for dst, w, tb in ((abd, 0, "low_neg"), (pbd, 1, "low_incl")):
                        nc.vector.tensor_tensor(
                            dst[q, mm, q].rearrange("p (h t) i -> p h t i", h=GH), gr[q, :, :, w, :],
                            tab(tb)[q, :].unsqueeze(1).unsqueeze(1).to_broadcast([CH, GH, HT, CH]), ALU.mult)
                link(nc.vector.tensor_tensor(
                    d_Y[:, half, :, :].rearrange("p (h t) i -> p h t i", h=GH), gr[:, :, :, 0, :],
                    tab("pair").unsqueeze(1).unsqueeze(1).to_broadcast([P, GH, HT, CH]), ALU.mult))
                link(nc.vector.tensor_tensor(d_Y[:, half, :, :], d_Y[:, half, :, :],
                                             tab("eye").unsqueeze(1).to_broadcast([P, NM, CH]), ALU.add))
                nc.vector.transpose(d_X[:, half, :, :].rearrange("p m i -> p (m i)"),
                                    d_Y[:, half, :, :].rearrange("p m i -> p (m i)")).then_inc(s("d_inv"), 1)
            need(dve, "lm")
            for v in range(4):
                for half in range(2):
                    dve.wait_ge(s("d_xax"), 2 * v + half + 1)
                    link(nc.vector.copy_predicated(
                        d_X[:, half, :, :], level_mask[:, v, :].unsqueeze(1).to_broadcast([P, NM, CH]),
                        ps[:, 4 * half + 1, :].rearrange("p (m j) -> p m j", j=CH)))
                    nc.vector.transpose(d_Y[:, half, :, :].rearrange("p m i -> p (m i)"),
                                        d_X[:, half, :, :].rearrange("p m i -> p (m i)")).then_inc(
                        s("d_inv"), 1)
            for half in range(2):
                dve.wait_ge(s("d_mt"), half + 1)
                nc.vector.tensor_tensor(abd[:, NM * half:NM * half + NM, :],
                                        ps[:, 4 * half:4 * half + 4, :].rearrange("p c (t j) -> p (c t) j", j=128),
                                        tab("blk_neg").unsqueeze(1).to_broadcast([P, NM, 128]),
                                        ALU.mult).then_inc(s("d_mbd"), 1)
            for n in range(NC - 1):
                dve.wait_ge(s("d_step"), n + 1)
                nc.vector.tensor_tensor(d_S[:, n + 1, :, :], ps[:, 2 * (n % 4):2 * (n % 4) + 2, 0:GV], d_S[:, n, :, :],
                                        ALU.add).then_inc(s("d_state"), 1)
                dve.wait_ge(s("d_state"), n + 1)
            for half in range(2):
                dve.wait_ge(s("d_ws"), half + 1)
                nc.vector.tensor_tensor(d_u[:, half, :, :, :], d_u[:, half, :, :, :],
                                        ps[:, 4 * half:4 * half + 4, 0:256].rearrange("p h (t w) -> p t h w", t=HT),
                                        ALU.subtract).then_inc(s("d_u"), 1)
            for half in range(2):
                dve.wait_ge(s("d_o_ps"), half + 1)
                o = d_o[:, half, :, :, :]
                link(nc.vector.tensor_copy(
                    o, ps[:, 4 * half:4 * half + 4, 0:256].rearrange("p h (t w) -> p t h w", t=HT)))
                link(nc.vector.tensor_tensor(d_sq[:, half, :, :, :], o, o, ALU.mult))
                vv, ww, yy = rt[:, 0, 0:16], rt[:, 1, 0:16], rt[:, 2, 0:16]
                link(nc.vector.tensor_reduce(vv.rearrange("p (t h) -> p t h", t=HT),
                                             d_sq[:, half, :, :, :], AX.X, ALU.add))
                link(nc.vector.tensor_scalar(vv, vv, 1.0 / GV, 1e-5, ALU.mult, ALU.add))
                inv_sqrt(vv, yy, ww)
                link(nc.vector.tensor_tensor(
                    o, o, yy.rearrange("p (t h) -> p t h", t=HT).unsqueeze(3).to_broadcast([P, HT, GH, GV]),
                    ALU.mult))
                nc.vector.tensor_tensor(
                    o, o, row("d_on").unsqueeze(1).unsqueeze(1).to_broadcast([P, HT, GH, GV]),
                    ALU.mult).then_inc(s("d_on"), 1)
            for half in range(2):
                join(half, 4 * half + 2, "d_y", half + 1)
                norm(pre, res, half).then_inc(s("z_ready"), 1)

            ones = e_kv[:, :, 256:272]
            dve.wait_ge(s("z_ready"), nth(EX, 1))
            link(nc.vector.memset(ones, 1.0))
            for b in range(B):
                dve.wait_ge(s("e_kv_ps"), b + 1)
                o = ROFF["e_bk"][0]
                link(nc.vector.tensor_tensor(e_kv[:, b, 0:256], ps[0:CTX, 2 + b, 0:256],
                                             rows[0:CTX, o:o + 256], ALU.add))
                link(nc.vector.tensor_tensor(e_kT[0:CTX, b, 0:128], e_kv[:, b, 0:128], e_kv[:, b, 0:128],
                                             ALU.mult))
                vv, ww, yy = rt[0:CTX, 0, 0:1], rt[0:CTX, 1, 0:1], rt[0:CTX, 2, 0:1]
                link(nc.vector.tensor_reduce(vv, e_kT[0:CTX, b, 0:128], AX.X, ALU.add))
                link(nc.vector.tensor_scalar(vv, vv, 1e-24, None, ALU.max))
                inv_sqrt(vv, yy, ww)
                nc.vector.tensor_scalar(e_kv[:, b, 0:128], e_kv[:, b, 0:128], yy, None, ALU.mult).then_inc(
                    s("e_kn"), 1)
            for b in range(B):
                dve.wait_ge(s("e_kT1"), b + 1)
                nc.vector.tensor_tensor(e_kT[:, b, :].rearrange("p (h k) -> p h k", k=CTX),
                                        d_wT[:, b, 0:CTX].unsqueeze(1).to_broadcast([P, EH, CTX]),
                                        tab("ehead").unsqueeze(2).to_broadcast([P, EH, CTX]),
                                        ALU.mult).then_inc(s("e_kT"), 1)
            vm = tab("vmask").rearrange("p (k n) -> p k n", k=EK)
            for b in range(B):
                for g in range(4):
                    n = 4 * b + g
                    w = min(3, EK - 3 * g)
                    dve.wait_ge(s("e_vb_ps"), n + 1)
                    nc.vector.tensor_tensor(e_vb[:, b, 3 * g:3 * g + w, :],
                                            ps[:, 4 + n % 2, 0:144 * w].rearrange("p (k n) -> p k n", k=w),
                                            vm[:, 3 * g:3 * g + w, :], ALU.mult).then_inc(s("e_vb"), 1)
            for half in range(2):
                dve.wait_ge(s("e_qt_ps"), half + 1)
                qp = z[:, til(half), :]
                link(nc.vector.tensor_tensor(qp, ps[:, 2 * half + 1, :].rearrange("p (t d) -> p t d", t=HT),
                                             rowb("e_bq", HT), ALU.add))
                link(nc.vector.tensor_tensor(pre[:, til(half), :], qp, qp, ALU.mult))
                vv, ww, yy = rt[:, 0, 0:HT], rt[:, 1, 0:HT], rt[:, 2, 0:HT]
                link(nc.vector.tensor_reduce(vv, pre[:, til(half), :], AX.X, ALU.add))
                link(nc.vector.tensor_scalar(vv, vv, 1e-24, None, ALU.max))
                inv_sqrt(vv, yy, ww)
                nc.vector.tensor_scalar(sm[:, 256 + HT * half:260 + HT * half], yy, 8.0 ** -0.5, None,
                                        ALU.mult).then_inc(s("e_scale"), 1)
                link(nc.vector.tensor_tensor(pre[:, til(half), :], qp, rowb("e_bo", HT), ALU.add))
            for i in range(NT + 2):
                if 1 <= i <= NT:
                    t = i - 1
                    dve.wait_ge(s("e_pv"), t + 1)
                    den = rt[:, t % 2, 16:32]
                    link(nc.vector.reciprocal(den, ps[:, 6 + t % 2, 128:144]))
                    nc.vector.tensor_tensor(e_o[:, t % 2, :].rearrange("p (h d) -> p h d", h=EH),
                                            ps[:, 6 + t % 2, 0:128].rearrange("p (h d) -> p h d", h=EH),
                                            den.unsqueeze(2).to_broadcast([P, EH, 8]),
                                            ALU.mult).then_inc(s("e_o"), 1)
                if 2 <= i:
                    t = i - 2
                    dve.wait_ge(s("e_y"), t + 1)
                    nc.vector.tensor_tensor(pre[:, t, :], ps[:, 6 + t % 2, 384:512], pre[:, t, :],
                                            ALU.add).then_inc(s("e_yadd"), 1)
                    dve.wait_ge(s("e_yadd"), t + 1)
                    if t % HT == HT - 1:
                        half = t // HT
                        hs = til(half)
                        link(norm(pre, z, half))
                        link(nc.vector.tensor_tensor(z[:, hs, :], z[:, hs, :], rowb("e_g", HT), ALU.mult))
                        link(nc.vector.tensor_tensor(z[:, hs, :], z[:, hs, :], rowb("e_b", HT), ALU.add))
                        link(nc.vector.tensor_tensor(pre[:, hs, :], z[:, hs, :], res[:, hs, :], ALU.add))
                        link(norm(pre, res, half))
                        nc.vector.tensor_copy(pre[:, hs, :], res[:, hs, :]).then_inc(s("z_ready"), 1)

            for half in range(2):
                route(1, half, None, 1e-20)

            def f_acc(g):
                dve.wait_ge(s("f_y"), g + 1)
                gather(1, g // NE, g % NE, 4 + g % 2).then_inc(s("f_acc"), 1)
                dve.wait_ge(s("f_acc"), g + 1)
                if g % NE == NE - 1:
                    half = g // NE
                    norm(pre, res, half).then_inc(s("out_ready"), 1)

            for g in range(2 * NE):
                for c in range(3):
                    n = 3 * g + c
                    w = F1C[c][1]
                    dve.wait_ge(s("f_silu"), n + 1)
                    dve.wait_ge(s("f_up_ps"), n + 1)
                    nc.vector.tensor_tensor(hid[0:w, g % 2, c, :], hid[0:w, g % 2, c, :],
                                            ps[0:w, 2 * (n % 2) + 1, :], ALU.mult).then_inc(s("f_h"), 1)
                if g >= 1:
                    f_acc(g - 1)
            f_acc(2 * NE - 1)

        @block.tensor
        def _(pe):
            mm = nc.tensor.matmul

            def turn(use, half, src):
                pe.wait_ge(s("z_ready"), nth(use, half))
                for t in range(HT):
                    ins = nc.tensor.transpose(ps[:, 6 + half, 128 * t:128 * t + 128], src[:, HT * half + t, :],
                                              ident)
                ins.then_inc(s("turned"), 1)

            need(pe, "tabs")
            for half in range(2):
                turn(A, half, z)
            need(pe, "wa")
            for half in range(2):
                pe.wait_ge(s("xT_ready"), nth(A, half))
                for j in range(3):
                    mm(ps[:, 3 * half + j, :], wa[:, j, :], xT[:, tok(half)], start=True, stop=True).then_inc(
                        s("a_qkv_ps"), 1)
            for half in range(2):
                pe.wait_ge(s("a_prod"), half + 1)
                mm(ps[:, 3 * half, :], tab("head8"), a_prod[:, tok(half)], start=True, stop=True).then_inc(
                    s("a_gap"), 1)
            need(pe, "ctxT", "wxkv")
            for g in range(7):
                if g >= 2:
                    pe.wait_ge(s("b_kv"), g - 1)
                if g < 3:
                    for c in range(3 * g, min(3 * g + 3, 8)):
                        ins = mm(ps[:, 6 + g % 2, B * CTX * (c - 3 * g):B * CTX * (c - 3 * g + 1)],
                                 wxkv[:, 128 * c:128 * c + 128], ctxT[:, :], start=True, stop=True)
                else:
                    b, n = divmod(g - 3, 2)
                    ins = mm(ps[0:CTX, 6 + g % 2, :], ctxT[:, CTX * b:CTX * b + CTX],
                             wxkv[:, XI + 512 * n:XI + 512 * n + 512], start=True, stop=True)
                ins.then_inc(s("b_kv_ps"), 1)
                if g == 1:
                    for half in range(2):
                        pe.wait_ge(s("a_o"), half + 1)
                        for t in range(HT):
                            ins = mm(ps[:, 3 * half + 1, 128 * t:128 * t + 128],
                                     a_o[:, S * half + 128 * t:S * half + 128 * t + 128], wa[:, 3, :],
                                     start=True, stop=True)
                        ins.then_inc(s("a_y"), 1)

            need(pe, "wxq")
            pe.wait_ge(s("b_kv"), 7)
            for half in range(2):
                turn(X, half, z)

            def b_queries(half):
                if half == 0:
                    pe.wait_ge(s("xT_ready"), nth(X, 0))
                for r in range(8):
                    n = RAT[("q", half, r)]
                    ring_free(pe, n)
                    mm(ps[:, 4 + n % 2, :], wxq[:, 128 * r:128 * r + 128], xT[:, tok(half)],
                       start=True, stop=True).then_inc(s("b_ring"), 1)

            def b_scores(t):
                if t % HT == 0:
                    pe.wait_ge(s("b_ringed"), 1 + sum(e[0] != "y" for e in RING[:RAT[("q", t // HT, 7)]]))
                if t >= 1:
                    pe.wait_ge(s("b_max"), t)
                else:
                    pe.wait_ge(s("z_ready"), nth(X, 1))
                for h in range(XH):
                    i, j = head_at(h)
                    q = slice(64 * (h % 2), 64 * (h % 2) + 64)
                    ins = mm(ps[:, i, CTX * j:CTX * j + CTX],
                             b_q[q, h // 2, 128 * (t % HT):128 * (t % HT) + 128],
                             b_kT[q, h // 2, CTX * (t // HT):CTX * (t // HT) + CTX], start=True, stop=True)
                ins.then_inc(s("b_sc"), 1)

            def b_turn_p(t):
                pe.wait_ge(s("b_exp"), t + 1)
                for r in range(4):
                    n = RAT[("pT", t, r)]
                    ring_free(pe, n)
                    for j in range(4):
                        ins = nc.tensor.transpose(ps[0:CTX, 4 + n % 2, 128 * j:128 * j + 128],
                                                  b_s[:, t % 3, r, CTX * j:CTX * j + CTX], ident)
                    ins.then_inc(s("b_ring"), 1)

            def b_values(t):
                pe.wait_ge(s("b_ringed"), 1 + sum(e[0] != "y" for e in RING[:RAT[("pT", t, 3)]]))
                if t >= 1:
                    pe.wait_ge(s("b_o"), t)
                else:
                    pe.wait_ge(s("xT_ready"), nth(X, 1))
                for h in range(XH):
                    i, j = head_at(h)
                    ins = mm(ps[:, 6 + h // 8, XD * (h % 8):XD * (h % 8) + XD], b_pT[0:CTX, 4 * i + j, :],
                             b_v[0:CTX, t // HT, XD * h:XD * h + XD], start=True, stop=True)
                ins.then_inc(s("b_pv"), 1)

            def b_out(t):
                pe.wait_ge(s("b_o"), t + 1)
                for r in range(2):
                    n = RAT[("oT", t, r)]
                    ring_free(pe, n)
                    for j in range(4):
                        k = 128 * (4 * r + j)
                        ins = nc.tensor.transpose(ps[:, 4 + n % 2, 128 * j:128 * j + 128],
                                                  b_o[:, t % 2, k:k + 128], ident)
                    ins.then_inc(s("b_ring"), 1)
                n = RAT[("y", t, 0)]
                if t == 0:
                    need(pe, "wxo")
                ring_free(pe, n)
                pe.wait_ge(s("b_ringed"), 1 + sum(e[0] != "y" for e in RING[:RAT[("oT", t, 1)]]))
                for k in range(8):
                    ins = mm(ps[:, 4 + n % 2, 0:128], b_oT[:, k, :], wxo[:, k, :], start=(k == 0), stop=(k == 7))
                ins.then_inc(s("b_ring"), 1)

            for i in range(NI):
                if i in (0, HT):
                    b_queries(i // HT)
                if i < NT:
                    b_scores(i)
                if 2 <= i < NT + 2:
                    b_turn_p(i - 2)
                    b_values(i - 2)
                if 3 <= i:
                    b_out(i - 3)

            def logits(which, half):
                pe.wait_ge(s("xT_ready"), nth(H if which else F, half))
                for t in range(HT):
                    ins = mm(ps[:, 6 + half, E * t:E * t + E],
                             xT[:, S * half + 128 * t:S * half + 128 * t + 128], router[:, which, :],
                             start=True, stop=True)
                ins.then_inc(s("r_logit"), 1)

            need(pe, "router", "w1", "w2", "fb2")
            pe.wait_ge(s("b_o"), NT)
            for half in range(2):
                turn(F, half, res)
                logits(0, half)

            def c_hidden(g):
                half, e = divmod(g, NE)
                for c in range(C0):
                    if g >= 1:
                        pe.wait_ge(s("c_h"), C0 * (g - 1) + c + 1)
                    mm(ps[:, c, :], w1[:, e, 128 * c:128 * c + 128], xT[:, tok(half)],
                       start=True, stop=True).then_inc(s("c_h_ps"), 1)

            def c_out(g):
                half, e = divmod(g, NE)
                pe.wait_ge(s("c_h"), C0 * (g + 1))
                if g >= 2:
                    pe.wait_ge(s("c_acc"), g - 1)
                for t in range(HT):
                    for c in range(C0):
                        ins = mm(ps[:, 4 + g % 2, 128 * t:128 * t + 128],
                                 hid[:, g % 2, c, 128 * t:128 * t + 128], w2[:, e, c, :],
                                 start=(c == 0), stop=(c == C0 - 1))
                ins.then_inc(s("c_y"), 1)

            for g in range(2 * NE + 1):
                if g < 2 * NE:
                    c_hidden(g)
                if g >= 1:
                    c_out(g - 1)
                if g % NE == 1:
                    half = g // NE
                    if half < 2:
                        pe.wait_ge(s("r_comb"), half + 1)
                        for t in range(HT):
                            ins = nc.tensor.transpose(ps[0:E, 6 + half, 128 * t:128 * t + 128],
                                                      comb[:, HT * half + t, :], ident)
                        ins.then_inc(s("c_combT_ps"), 1)
                        pe.wait_ge(s("c_combT"), half + 1)
                        for t in range(HT):
                            ins = mm(ps[:, 6 + half, 128 * t:128 * t + 128],
                                     combT[:, half, 128 * t:128 * t + 128], fb2[:, :], start=True, stop=True)
                        ins.then_inc(s("c_b2"), 1)

            need(pe, "wd", "wdo")
            for half in range(2):
                turn(G, half, z)
            for half in range(2):
                pe.wait_ge(s("xT_ready"), nth(G, half))
                if half == 1:
                    pe.wait_ge(s("xT_ready"), nth(G, 1))
                for t in range(HT):
                    x = xT[:, S * half + 128 * t:S * half + 128 * t + 128]
                    mm(ps[:, 4 * half + t, :], x, wd[:, 0:512], start=True, stop=True).then_inc(s("d_qkv"), 1)
                pe.wait_ge(s("d_silu"), HT * half + 1)
                for t in range(HT):
                    x = xT[:, S * half + 128 * t:S * half + 128 * t + 128]
                    ins = mm(ps[:, 4 * half, 4 * t:4 * t + 4], x, wd[:, 512:516], start=True, stop=True)
                ins.then_inc(s("d_beta_ps"), 1)
            for half in range(2):
                pe.wait_ge(s("d_norm"), half + 1)
                for w in range(3):
                    for t in range(HT):
                        src = (d_qk[:, half, t, 4:8, :], d_P[:, half, GH * t:GH * t + GH, :], d_qk[:, half, t, 0:4, :])[w]
                        ins = nc.tensor.transpose(ps[:, 4 * half + w, 128 * t:128 * t + 128], src, ident)
                    ins.then_inc(s("d_turn_ps"), 1)
            for half in range(2):
                pe.wait_ge(s("d_turn"), 3 * half + 3)
                for h in range(GH):
                    q = slice(GK * h, GK * h + GK)
                    for t in range(HT):
                        for c in range(4):
                            n = 128 * t + CH * c
                            ins = mm(ps[CH * c:CH * c + CH, 4 * half + h, 64 * t:64 * t + 64],
                                     d_T[q, half, 0, n:n + CH], d_T[q, half, 1:3, n:n + CH],
                                     start=True, stop=True, tile_position=(GK * h, CH * c))
                ins.then_inc(s("d_gram"), 1)
            for v in range(4):
                for half in range(2):
                    pe.wait_ge(s("d_inv"), 2 * v + half + 1)
                    for m in range(NM):
                        ins = mm(ps[:, 4 * half, CH * m:CH * m + CH], abd[:, NM * half + m, :],
                                 d_X[:, half, m, :], start=True, stop=True)
                    ins.then_inc(s("d_ax"), 1)
                for half in range(2):
                    pe.wait_ge(s("d_p"), 2 * v + half + 1)
                    pe.wait_ge(s("d_diag_a"), 2 * v + half + 1)
                    pe.wait_ge(s("d_diag_p"), 2 * v + half + 1)
                    for m in range(NM):
                        ins = mm(ps[:, 4 * half + 1, CH * m:CH * m + CH], ybd[:, NM * half + m, :],
                                 d_P[:, half, m, :], start=True, stop=True)
                    ins.then_inc(s("d_xax"), 1)
            for half in range(2):
                pe.wait_ge(s("d_diag_a"), 8 + half + 1)
                pe.wait_ge(s("d_diag_p"), 8 + half + 1)
                for t in range(HT):
                    for h in range(GH):
                        ins = mm(ps[:, 4 * half + t, 96 * h:96 * h + 96], ybd[:, NM * half + HT * h + t, :],
                                 d_r[:, half, t, h, :], start=True, stop=True)
                ins.then_inc(s("d_uw_ps"), 1)
            for half in range(2):
                pe.wait_ge(s("d_uw"), half + 1)
                for c in range(4):
                    q = slice(CH * c, CH * c + CH)
                    for t in range(HT):
                        ins = mm(ps[:, 4 * half + c, 128 * t:128 * t + 128], d_w[q, half, t, :],
                                 d_qk[q, half, t, 4:8, :], start=True, stop=True, tile_position=(CH * c, 0))
                ins.then_inc(s("d_mt"), 1)
            for half in range(2):
                pe.wait_ge(s("d_mbd"), half + 1)
                for t in range(HT):
                    ins = nc.tensor.transpose(ps[:, 4 * half, 128 * t:128 * t + 128], d_w[:, half, t, :], ident)
                ins.then_inc(s("d_wT_ps"), 1)

            def d_new(n):
                t, c = divmod(n, 4)
                q = slice(CH * c, CH * c + CH)
                if n >= 4:
                    pe.wait_ge(s("d_state"), n - 3)
                for b in range(2):
                    for h in range(GH):
                        mm(ps[GK * h:GK * h + GK, 2 * (n % 4) + b, 0:GV], d_qk[q, b, t, 4 + h, :],
                           d_u[q, b, t, h, :], start=True, stop=False, tile_position=(CH * c, GK * h),
                           skip_group_check=True)

            pe.wait_ge(s("d_wT"), 2)
            d_new(0)
            for n in range(NC - 1):
                if n + 1 < NC - 1:
                    d_new(n + 1)
                if n >= 1:
                    pe.wait_ge(s("d_state"), n)
                t, c = divmod(n, 4)
                for b in range(2):
                    ins = mm(ps[:, 2 * (n % 4) + b, 0:GV], abd[:, NM * b + HT * c + t, :], d_S[:, n, b, :],
                             start=False, stop=True, skip_group_check=True)
                ins.then_inc(s("d_step"), 1)
            pe.wait_ge(s("d_state"), NC - 1)
            for half in range(2):
                for h in range(GH):
                    q = slice(GK * h, GK * h + GK)
                    for t in range(HT):
                        for c in range(4):
                            n = 128 * t + CH * c
                            ins = mm(ps[CH * c:CH * c + CH, 4 * half + h, GV * t:GV * t + GV],
                                     d_wT[q, half, n:n + CH], d_S[q, 4 * t + c, half, :],
                                     start=True, stop=True, tile_position=(GK * h, CH * c))
                ins.then_inc(s("d_ws"), 1)
            for half in range(2):
                pe.wait_ge(s("d_u"), half + 1)
                for h in range(GH):
                    q = slice(GK * h, GK * h + GK)
                    for t in range(HT):
                        mm(ps[:, 4 * half + h, GV * t:GV * t + GV], pbd[:, NM * half + HT * h + t, :],
                           d_u[:, half, t, h, :], start=True, stop=False, skip_group_check=True)
                        for c in range(4):
                            n = 128 * t + CH * c
                            ins = mm(ps[CH * c:CH * c + CH, 4 * half + h, GV * t:GV * t + GV],
                                     d_T[q, half, 2, n:n + CH], d_S[q, 4 * t + c, half, :],
                                     start=False, stop=True, tile_position=(GK * h, CH * c),
                                     skip_group_check=True)
                ins.then_inc(s("d_o_ps"), 1)
            for half in range(2):
                pe.wait_ge(s("d_on"), half + 1)
                for w in range(2):
                    for t in range(HT):
                        ins = nc.tensor.transpose(
                            ps[:, 4 * half + w, 128 * t:128 * t + 128],
                            d_o[:, half, t, 2 * w:2 * w + 2, :].rearrange("p h d -> p (h d)"), ident)
                    ins.then_inc(s("d_oT_ps"), 1)
                pe.wait_ge(s("d_oT"), 2 * half + 2)
                for t in range(HT):
                    for w in range(2):
                        ins = mm(ps[:, 4 * half + 2, 128 * t:128 * t + 128],
                                 d_T[:, half, w, 128 * t:128 * t + 128], wdo[:, w, :],
                                 start=(w == 0), stop=(w == 1))
                ins.then_inc(s("d_y"), 1)

            need(pe, "we", "wekv", "spread")
            pe.wait_ge(s("z_ready"), nth(EX, 0))
            for b in range(B):
                mm(ps[0:CTX, 2 + b, 0:256], ctxT[:, CTX * b:CTX * b + CTX], wekv[:, :],
                   start=True, stop=True).then_inc(s("e_kv_ps"), 1)
            for b in range(B):
                pe.wait_ge(s("e_kn"), b + 1)
                nc.tensor.transpose(ps[:, b, 0:CTX], e_kv[:, b, 0:128], ident[0:CTX, 0:CTX]).then_inc(
                    s("e_kT_ps"), 1)
            for half in range(2):
                turn(EX, half, res)
            for b in range(B):
                for g in range(4):
                    n = 4 * b + g
                    if n >= 2:
                        pe.wait_ge(s("e_vb"), n - 1)
                    for k in range(3 * g, min(3 * g + 3, EK)):
                        ins = mm(ps[:, 4 + n % 2, 144 * (k - 3 * g):144 * (k - 3 * g) + 144],
                                 spread[:, 128 * k:128 * k + 128], e_kv[:, b, 128:272], start=True, stop=True)
                    ins.then_inc(s("e_vb_ps"), 1)
            pe.wait_ge(s("e_vb"), 8)
            pe.wait_ge(s("e_kT"), 2)
            for half in range(2):
                pe.wait_ge(s("xT_ready"), nth(EX, half))
                mm(ps[:, 2 * half, :], we[:, 0, :], xT[:, tok(half)], start=True, stop=True).then_inc(
                    s("e_q_ps"), 1)
                for t in range(HT):
                    ins = mm(ps[:, 2 * half + 1, 128 * t:128 * t + 128],
                             xT[:, S * half + 128 * t:S * half + 128 * t + 128], we[:, 0, :],
                             start=True, stop=True)
                ins.then_inc(s("e_qt_ps"), 1)
            pe.wait_ge(s("e_q"), 2)
            pe.wait_ge(s("e_scale"), 2)
            for i in range(NT + 2):
                if i < NT:
                    if i >= 1:
                        pe.wait_ge(s("e_exp"), i)
                    half, t = divmod(i, HT)
                    for k in range(4):
                        ins = mm(ps[:, k, 0:4 * CTX], e_q[:, half, 128 * t:128 * t + 128],
                                 e_kT[:, half, 4 * CTX * k:4 * CTX * (k + 1)], start=True, stop=True)
                    ins.then_inc(s("e_sc"), 1)
                if 1 <= i <= NT:
                    t = i - 1
                    pe.wait_ge(s("e_exp"), t + 1)
                    for r in range(3):
                        n = 3 * t + r
                        if n >= 2:
                            pe.wait_ge(s("e_pT"), n - 1)
                        for k in range(4 * r, min(4 * r + 4, EK)):
                            w = min(128, EP - 128 * k)
                            ins = nc.tensor.transpose(ps[0:w, 4 + n % 2, 128 * (k - 4 * r):128 * (k - 4 * r) + 128],
                                                      e_p[:, t % 2, 128 * k:128 * k + w], ident)
                        ins.then_inc(s("e_pT_ps"), 1)
                    pe.wait_ge(s("e_pT"), 3 * t + 3)
                    if t >= 2:
                        pe.wait_ge(s("e_yadd"), t - 1)
                    for k in range(EK):
                        w = min(128, EP - 128 * k)
                        ins = mm(ps[:, 6 + t % 2, 0:144], e_pT[0:w, k, :], e_vb[0:w, t // HT, k, :],
                                 start=(k == 0), stop=(k == EK - 1))
                    ins.then_inc(s("e_pv"), 1)
                if 2 <= i:
                    t = i - 2
                    pe.wait_ge(s("e_o"), t + 1)
                    nc.tensor.transpose(ps[:, 6 + t % 2, 256:384], e_o[:, t % 2, :], ident).then_inc(
                        s("e_oT_ps"), 1)
                    pe.wait_ge(s("e_oT"), t + 1)
                    mm(ps[:, 6 + t % 2, 384:512], e_oT[:, t % 2, :], we[:, 1, :], start=True,
                       stop=True).then_inc(s("e_y"), 1)

            need(pe, "f_gu", "f_dn")
            pe.wait_ge(s("e_yadd"), NT)
            for half in range(2):
                turn(H, half, res)
                logits(1, half)

            def f_hidden(g):
                half, e = divmod(g, NE)
                for c, (f, w) in enumerate(F1C):
                    n = 3 * g + c
                    if n >= 2:
                        pe.wait_ge(s("f_silu"), n - 1)
                    mm(ps[0:w, 2 * (n % 2), :], f_gu[:, e, 0, f:f + w], xT[:, tok(half)],
                       start=True, stop=True).then_inc(s("f_gate_ps"), 1)
                    if n >= 2:
                        pe.wait_ge(s("f_h"), n - 1)
                    mm(ps[0:w, 2 * (n % 2) + 1, :], f_gu[:, e, 1, f:f + w], xT[:, tok(half)],
                       start=True, stop=True).then_inc(s("f_up_ps"), 1)

            def f_out(g):
                half, e = divmod(g, NE)
                pe.wait_ge(s("f_h"), 3 * (g + 1))
                if g >= 2:
                    pe.wait_ge(s("f_acc"), g - 1)
                for t in range(HT):
                    for c, (f, w) in enumerate(F1C):
                        ins = mm(ps[:, 4 + g % 2, 128 * t:128 * t + 128],
                                 hid[0:w, g % 2, c, 128 * t:128 * t + 128], f_dn[0:w, e, c, :],
                                 start=(c == 0), stop=(c == 2))
                ins.then_inc(s("f_y"), 1)

            pe.wait_ge(s("e_exp"), NT)
            for g in range(2 * NE + 1):
                if g < 2 * NE:
                    f_hidden(g)
                if g >= 1:
                    f_out(g - 1)


def tables():
    p = np.arange(P)
    k = np.arange(CH)
    j = p % CH
    t = {}
    t["ident"] = np.eye(P)
    t["head8"] = p[:, None] // 8 == p[None, :] // 8
    t["low_neg"] = -1.0 * (j[:, None] < k[None, :])
    t["low_incl"] = j[:, None] <= k[None, :]
    t["eye"] = j[:, None] == k[None, :]
    t["pair"] = -1.0 * ((j[:, None] + 1 == k[None, :]) & (j[:, None] % 2 == 0))
    t["blk_neg"] = -1.0 * (p[:, None] // CH == p[None, :] // CH)
    t["ehead"] = p[:, None] // 8 == np.arange(EH)[None, :]
    t["iota"] = np.broadcast_to(np.arange(E), (P, E))
    r = np.arange(EK * P)
    h = np.concatenate([np.arange(P) // 8, np.arange(EH)])
    vm = (r[:, None] // CTX == h[None, :]) & (r[:, None] < EP)
    t["vmask"] = vm.reshape(EK, P, 144).transpose(1, 0, 2).reshape(P, EK * 144)
    tabs = np.concatenate([np.asarray(t[n], np.float32) for n, _ in TABS], 1)
    i = j[:, None]
    level = np.stack([(i // (2 * b) == k // (2 * b)) & ((i // b) % 2 == 1) & ((k // b) % 2 == 0)
                      for b in (2, 4, 8, 16)], 1)
    spread = (np.arange(CTX)[:, None] == r[None, :] % CTX) & (r[None, :] < EP)
    return tabs, level.astype(np.uint32), spread.astype(np.float32)


def kernel(**inputs):
    import concourse.bacc as bacc
    from concourse.bass_utils import run_bass_kernel_spmd as run

    i = {k: np.asarray(v) for k, v in inputs.items()}
    tabs, level, spread = tables()
    L0, L1 = "L0_", "L1_"
    cat = np.concatenate
    a = {
        "x": i["x"].reshape(B * S, D),
        "tabs": tabs, "level_mask": level, "spread": spread,
        "cols": np.stack([i[n] for n in ("L0_attn_ln_g", "L0_attn_ln_b", "L0_attn_bq", "L0_attn_bk",
                                         "L0_attn_bv", "L0_xattn_ln_gamma", "L0_xattn_ln_beta",
                                         "L1_attn_ln_w", "L1_attn_ln_b", "L1_xattn_bq")], 1),
        "rows": cat([i["L0_attn_bo"], i["L0_xattn_bo"], i["L0_ffn_shared_b2"], i["L1_xattn_bq"],
                     i["L1_xattn_bk"], i["L1_xattn_bv"], i["L1_xattn_bo"], i["L1_xattn_ln_gamma"],
                     i["L1_xattn_ln_beta"], i["L1_attn_o_norm_w"], i["L0_ffn_router_b"]]),
        "ctxT": i["ctx_768"].reshape(B * CTX, CD).T,
        "mask": i["mask_1x1xSxS2_bk0"].reshape(S, CTX),
        "wa": np.stack([i["L0_attn_W" + w] for w in "qkvo"], 1),
        "wxq": i["L0_xattn_Wq"],
        "wxkv": i["L0_xattn_Wkv"],
        "wxo": i["L0_xattn_Wo"].reshape(8, P, D).transpose(1, 0, 2),
        "router": np.stack([i["L0_ffn_router_w"].T, i["L1_ffn_gate_w"].T], 1),
        "w1": cat([i["L0_ffn_shared_w1"][None], i["L0_ffn_spec_w1"]]).transpose(2, 0, 1),
        "w2": cat([i["L0_ffn_shared_w2"][None], i["L0_ffn_spec_w2"]]).reshape(NE, D, C0, P).transpose(3, 0, 2, 1),
        "fb1": cat([i["L0_ffn_shared_b1"][None], i["L0_ffn_spec_b1"]]).reshape(NE, C0, P).transpose(2, 0, 1),
        "fb2": i["L0_ffn_spec_b2"],
        "wd": cat([i["L1_attn_W" + w] for w in "qkvb"], 1),
        "wdo": i["L1_attn_Wo"].reshape(2, P, D).transpose(1, 0, 2),
        "we": np.stack([i["L1_xattn_Wq"], i["L1_xattn_Wo"]], 1),
        "wekv": cat([i["L1_xattn_Wk"], i["L1_xattn_Wv"]], 1),
        "f_gu": np.stack([cat([i["L1_ffn_shared_gate"][None], i["L1_ffn_expert_gate"]]),
                          cat([i["L1_ffn_shared_up"][None], i["L1_ffn_expert_up"]])], 1).transpose(3, 0, 1, 2),
    }
    dn = cat([i["L1_ffn_shared_down"][None], i["L1_ffn_expert_down"]]).transpose(2, 0, 1)
    pad = np.zeros((3 * P - F1, NE, D), dn.dtype)
    a["f_dn"] = cat([dn, pad]).reshape(3, P, NE, D).transpose(1, 2, 0, 3)

    nc = bacc.Bacc("TRN2", target_bir_lowering=False, num_devices=1)
    arrays, args = {}, {}
    for name, v in a.items():
        v = np.ascontiguousarray(v)
        arrays["in_" + name] = v
        args[name] = nc.dram_tensor("in_" + name, v.shape, mybir.dt.from_np(v.dtype), kind="ExternalInput").ap()
    args["out"] = nc.dram_tensor("out_x", (B * S, D), FP, kind="ExternalOutput").ap()
    program(nc, args)
    r = run(nc, [arrays], core_ids=[0])
    return r.results[0]["out_x"].reshape(B, S, D)
```

```python
import numpy as np
import concourse.bass as bass
from concourse import mybir
from contextlib import ExitStack

FP = mybir.dt.float32
U32 = mybir.dt.uint32
I32 = mybir.dt.int32
U8 = mybir.dt.uint8
F16 = mybir.dt.float16
ALU = mybir.AluOpType
ACT = mybir.ActivationFunctionType
AX = mybir.AxisListType

P = 128
B, S, D = 2, 512, 128
HT = S // P
NT = B * HT
CTX, CD = 77, 96
XH, XD = 16, 64
XI = XH * XD
E = 8
NE = E + 1
F0 = 512
C0 = F0 // P
F1 = 352
F1C = [(0, 128), (128, 128), (256, 96)]
GH, GK, GV = 4, 32, 64
CH = 32
NC = S // CH
NM = HT * GH
EH = 16
EP = EH * CTX
EK = (EP + P - 1) // P
ARENA = 17600
XS, WS, HS = 2.0 ** 10, 2.0 ** 6, 2.0 ** 4
PASSES = ((0, 0), (0, 1), (1, 0))
WG = 3
MAGIC = float(0x5F3759DF)

COLS = ["a_g", "a_b", "a_bq", "a_bk", "a_bv", "x_g", "x_b", "d_g", "d_b", "e_bq", "d_on"]
ROWS = [("a_bo", 128), ("x_bo", 128), ("f_b2", 128), ("e_bq", 128), ("e_bk", 128), ("e_bv", 128),
        ("e_bo", 128), ("e_g", 128), ("e_b", 128), ("f_rb", 8)]
ROFF = {}
_o = 0
for _n, _w in ROWS:
    ROFF[_n] = (_o, _w)
    _o += _w
RTOT = _o
TABS = [("ident", 128), ("head8", 128), ("low_incl", 32),
        ("blk_neg", 128), ("head4", GH), ("ehead", EH), ("iota", 8), ("vmask", EK * 144)]
TOFF = {}
_o = 0
for _n, _w in TABS:
    TOFF[_n] = (_o, _w)
    _o += _w
TTOT = _o


def program(nc, a):
    ctx = ExitStack()
    with ctx:
        def sb(name, shape, dt=FP):
            return ctx.enter_context(nc.sbuf_tensor(name, shape, dt))

        def sem(name):
            return ctx.enter_context(nc.semaphore(name))

        ps = ctx.enter_context(nc.psum_tensor("ps", [P, 8, 512], FP))

        tabs = sb("tabs", [P, TTOT])
        cols = sb("cols", [P, len(COLS)])
        rows = sb("rows", [P, RTOT])
        spread = sb("spread", [CTX, EK * P])
        ctxT = sb("ctxT", [CD, B * CTX])
        mask_u8 = sb("mask_u8", [P, HT, CTX], U8)
        mask_f = sb("mask_f", [P, HT, CTX])
        wa = sb("wa", [P, 4, 128])
        wx = sb("wx", [P, 4 * XI])
        wxq, wxkv = wx[:, 0:XI], wx[0:CD, XI:3 * XI]
        wxo = wx[:, 3 * XI:4 * XI].rearrange("p (c d) -> p c d", c=8)
        w1f = sb("w1f", [P, NE * F0])
        w2f = sb("w2f", [P, NE * F0])
        w1 = w1f[:, :].bitcast(F16).rearrange("p (s e f) -> p s e f", s=2, e=NE)
        w2 = w2f[:, :].bitcast(F16).rearrange("p (s e f) -> p s e f", s=2, e=NE)
        fb1 = sb("fb1", [P, NE, C0])
        fb2 = sb("fb2", [E, 128])
        router = sb("router", [P, 2, E])
        wd = sb("wd", [P, 516])
        wdo = sb("wdo", [P, 2, 128])
        we = sb("we", [P, 2, 128])
        wekv = sb("wekv", [CD, 256])

        def tab(n):
            return tabs[:, TOFF[n][0]:TOFF[n][0] + TOFF[n][1]]

        def row(n):
            return rows[:, ROFF[n][0]:ROFF[n][0] + ROFF[n][1]]

        def col(n):
            return cols[:, COLS.index(n):COLS.index(n) + 1]

        ident = tab("ident")

        z = sb("z", [P, NT, D])
        xT = sb("xT", [P, B * S])
        res = sb("res", [P, NT, D])
        pre = sb("pre", [P, NT, D])
        bn6 = sb("bn6", [P, NT, 6])
        bn2 = sb("bn2", [P, NT, 2])
        rt = sb("rt", [P, 3, 64])
        arena = sb("arena", [P, ARENA])
        hid = sb("hid", [P, 2, 4, 512])
        sm = sb("sm", [P, 512])
        idx = sb("idx", [P, HT, 8], U32)
        comb = sb("comb", [P, NT, E])
        wscale = sb("wscale", [P, 1])
        combT = sb("combT", [E, 2, 512])

        class Carve:
            def __init__(self):
                self.at = 0

            def __call__(self, *dims):
                n = int(np.prod(dims))
                v = arena[:, self.at:self.at + n]
                self.at += n
                assert self.at <= ARENA, self.at
                names = " ".join(f"d{i}" for i in range(len(dims)))
                if len(dims) > 1:
                    v = v.rearrange(f"p ({names}) -> p {names}", **{f"d{i}": d for i, d in enumerate(dims) if i})
                return v

        cut = Carve()
        a_qkv = cut(3, B * S)
        a_kd, a_vd, a_vs = cut(S), cut(S), cut(S)
        a_prod, a_th, a_o = cut(B * S), cut(B * S), cut(B * S)
        cut = Carve()
        b_q = cut(8, 512)
        b_s = cut(3, XH * CTX)
        assert cut.at >= 3 * B * S + 3 * S + 3 * B * S
        b_kT = cut(8, B, 2, CTX)
        b_v = cut(B, XI)
        b_pT = cut(16, 128)
        b_o = cut(2, XI)
        b_oT = cut(8, 128)
        cut = Carve()
        d_qk = cut(2, HT, 8, GK)
        d_r = cut(2, HT, GH, GV + GK)
        d_u = cut(2, HT, GH, GV)
        d_w = cut(2, HT, GH * GK)
        d_S = cut(NC, 2, GV)
        d_P = cut(2 * NM, CH)
        pbd = cut(2 * NM, 128)
        sbd = cut(2, 2, GH * GV)
        d_o = d_r.rearrange("p b t h w -> p (b t h w)")[:, 0:2 * HT * GH * GV].rearrange(
            "p (b t h w) -> p b t h w", b=2, t=HT, h=GH)
        d_sq = d_u
        inv_a = sb("inv_a", [P, CH * CH])
        inv_x = sb("inv_x", [P, CH * CH])
        inv_t = sb("inv_t", [P, 256])
        mbd = w1f[:, 0:2 * NM * 128].rearrange("p (m j) -> p m j", j=128)
        ybd = w2f[:, 0:2 * NM * 128].rearrange("p (m j) -> p m j", j=128)
        d_T = wx[:, 0:3072].rearrange("p (b w n) -> p b w n", b=2, w=3)
        d_wT = wx[:, 3072:4096].rearrange("p (b n) -> p b n", b=2)
        e_kv = z[0:CTX, :, :].rearrange("p t d -> p (t d)")[:, 0:B * 272].rearrange(
            "p (b n) -> p b n", b=B)
        e_k1 = xT[:, 0:B * CTX].rearrange("p (b k) -> p b k", b=B)
        flat = hid[:, :, :, :].rearrange("p a c n -> p (a c n)")
        e_sq = flat[0:CTX, 0:B * 128].rearrange("p (b n) -> p b n", b=B)
        e_kT = flat[:, 0:B * EP].rearrange("p (b n) -> p b n", b=B)
        e_p = w1f[:, 0:2 * EP].rearrange("p (a n) -> p a n", a=2)
        e_q = w1f[:, B * EP:B * EP + 1024].rearrange("p (b n) -> p b n", b=B)
        e_o = w1f[:, B * EP + 1024:B * EP + 1280].rearrange("p (b n) -> p b n", b=2)
        e_oT = w1f[:, B * EP + 1280:B * EP + 1536].rearrange("p (b n) -> p b n", b=2)
        e_vb = w2f[:, 0:B * EK * 144].rearrange("p (b k n) -> p b k n", b=B, k=EK)
        e_pT = w2f[:, B * EK * 144:B * EK * 144 + EK * 128].rearrange("p (k n) -> p k n", k=EK)
        VG = [(b, k, min(k + 3, EK)) for b in range(B) for k in range(0, EK, 3)]
        FD = NE * 2 * F1
        FW = FD + NE * 3 * D
        f_gu = arena[:, 0:FD].bitcast(F16).rearrange("p (s e f) -> p s e f", s=2, e=NE)
        f_dn = arena[:, FD:FW].bitcast(F16).rearrange("p (s e f) -> p s e f", s=2, e=NE)
        xs, hp = [], []
        for at0 in (0, FW):
            n = at0 + B * S
            xs.append(arena[:, at0:n].bitcast(F16).rearrange("p (b s n) -> p b s n", b=B, s=2))
            hp.append(arena[:, n:n + 4096 if not at0 else n + 3072].bitcast(F16).rearrange(
                "p (a s c n) -> p a s c n", a=2, s=2, n=512))
        SPLITS = []
        for name, dst, w in (("w1", w1, F0), ("w2", w2, F0), ("f_gu", f_gu, 2 * F1), ("f_dn", f_dn, 3 * D)):
            for k in range(0, NE, WG):
                n = len(SPLITS)
                if name in ("w1", "w2"):
                    stage = hid[:, n % 2, :, :].rearrange("p c n -> p (c n)")[:, 0:WG * w]
                else:
                    o = FW + (n - 6) % 3 * WG * 2 * F1
                    stage = arena[:, o:o + WG * w]
                SPLITS.append((a[name][:, k:k + WG, :], stage.rearrange("p (e f) -> p e f", e=WG),
                               dst[:, :, k:k + WG, :]))

        sems = {}

        def s(name):
            if name not in sems:
                sems[name] = sem(name)
            return sems[name]

        LOADS = [("x", res[:, :, :], a["x"].rearrange("(t p) d -> p t d", p=P)),
                 ("tabs", tabs[:, :], a["tabs"]),
                 ("cols", cols[:, :], a["cols"]),
                 ("wa", wa[:, :, :], a["wa"]),
                 ("rows", rows[:, :], a["rows"].partition_broadcast(P)),
                 ("ctxT", ctxT[:, :], a["ctxT"]),
                 ("wxkv", wxkv, a["wxkv"]),
                 ("wxq", wxq, a["wxq"]),
                 ("mask", mask_u8[:, :, :], a["mask"].rearrange("(t p) k -> p t k", p=P)),
                 ("wxo", wxo, a["wxo"]),
                 ("router", router[:, :, :], a["router"]),
                 ("fb2", fb2[:, :], a["fb2"]),
                 ("fb1", fb1[:, :, :], a["fb1"]),
                 ("wd", wd[:, :], a["wd"]),
                 ("wdo", wdo[:, :, :], a["wdo"]),
                 ("we", we[:, :, :], a["we"]),
                 ("wekv", wekv[:, :], a["wekv"]),
                 ("spread", spread[:, :], a["spread"])]

        def need(eng, *names):
            for n in names:
                eng.wait_ge(s("in_" + n), 16)

        A, X, F, G, EX, H = range(6)

        def turn_bank(use, half):
            return 4 * half + 3 if use == EX else 6 + half

        def nth(use, half):
            return 2 * use + half + 1

        def tok(half):
            return slice(half * S, half * S + S)

        def til(half):
            return slice(half * HT, half * HT + HT)

        NI = NT + 3
        RING = []
        for i in range(NI):
            if i in (0, HT):
                RING += [("q", i // HT, r) for r in range(8)]
            if 2 <= i < NT + 2:
                RING += [("pT", i - 2, r) for r in range(4)]
            if 3 <= i:
                RING += [("oT", i - 3, r) for r in range(2)] + [("y", i - 3, 0)]
        RAT = {e: n for n, e in enumerate(RING)}

        def ring(n):
            return 3 + n % 3

        def ringed(kind, i, r):
            return 1 + sum(e[0] != "y" for e in RING[:RAT[(kind, i, r)]])

        def ring_free(eng, n):
            if n >= 3:
                kind, i, r = RING[n - 3]
                if kind == "y":
                    eng.wait_ge(s("b_yadd"), i + 1)
                else:
                    eng.wait_ge(s("b_ringed"), ringed(kind, i, r))

        def r_l(half):
            return sm[:, 64 + 32 * half:96 + 32 * half].rearrange("p (t e) -> p t e", e=E)

        def r_e(half):
            return sm[:, 160 + 32 * half:192 + 32 * half].rearrange("p (t e) -> p t e", e=E)

        block = ctx.enter_context(nc.Block())

        @block.sync
        def _(sp):
            for name, dst, src in LOADS:
                sp.dma_start(dst, src).then_inc(s("in_" + name), 16)
            for n, (src, stage, _) in enumerate(SPLITS):
                if n in (2, 3, 4, 5, 9, 10, 11):
                    sp.wait_ge(s("w_split"), n - 1 if n < 6 else n - 2)
                if n == 6:
                    sp.wait_ge(s("z_ready"), nth(EX, 1))
                sp.dma_start(stage, src).then_inc(s("in_split%d" % n), 16)
            for half in range(2):
                sp.wait_ge(s("out_ready"), half + 1)
                sp.dma_start(a["out"].rearrange("(t p) d -> p t d", p=P)[:, til(half), :],
                             res[:, til(half), :]).then_inc(s("stored"), 16)
            sp.wait_ge(s("stored"), 32)

        @block.gpsimd
        def _(pool):
            nc.gpsimd.memset(wscale[:, :], WS).then_inc(s("w_scale"), 1)
            nc.gpsimd.memset(b_kT, 0.0).then_inc(s("b_zero"), 1)
            pool.wait_ge(s("w_scale"), 1)

            def split(n):
                _, stage, dst = SPLITS[n]
                pool.wait_ge(s("in_split%d" % n), 16)
                scale = wscale[:, 0:1].unsqueeze(1).to_broadcast(list(stage.shape))
                nc.gpsimd.tensor_tensor(dst[:, 0], stage, scale, ALU.mult)
                nc.gpsimd.tensor_tensor(stage, stage, scale, ALU.mult).then_inc(s("w_high"), 1)
                pool.wait_ge(s("w_high"), n + 1)
                nc.gpsimd.tensor_tensor(dst[:, 1], stage, dst[:, 0], ALU.subtract).then_inc(s("w_split"), 1)

            split(0)
            split(1)
            for t in range(NT):
                pool.wait_ge(s("b_max"), t + 1)
                nc.gpsimd.tensor_tensor(
                    b_s[:, t % 3, :].rearrange("p (h k) -> p h k", k=CTX),
                    b_s[:, t % 3, :].rearrange("p (h k) -> p h k", k=CTX),
                    sm[:, 16 * (t % 3):16 * (t % 3) + 16].unsqueeze(2).to_broadcast([P, 16, CTX]),
                    ALU.subtract).then_inc(s("b_sub"), 1)
                if t < 4:
                    split(t + 2)
            pool.wait_ge(s("c_acc"), 2 * NE)
            nc.gpsimd.memset(inv_x[:, :], 0.0).then_inc(s("d_zero"), 1)
            pool.wait_ge(s("d_zero"), 1)
            nc.gpsimd.memset(inv_x[:, 0:CH * CH:CH + 1], 1.0).then_inc(s("d_zero"), 1)
            nc.gpsimd.memset(w2f[:, 0:2 * NM * 128], 0.0)
            nc.gpsimd.memset(pbd, 0.0)
            nc.gpsimd.memset(d_S[:, 0, :, :], 0.0).then_inc(s("d_zero"), 1)
            need(pool, "wdo", "cols")
            nc.gpsimd.tensor_tensor(wdo[:, :, :], wdo[:, :, :],
                                    col("d_on").unsqueeze(1).to_broadcast([P, 2, 128]), ALU.mult).then_inc(
                s("d_wdo"), 1)
            pool.wait_ge(s("d_wdo"), 1)
            pool.wait_ge(s("d_zero"), 3)
            pool.wait_ge(s("d_pt"), 1)
            for c in range(4):
                q = slice(CH * c, CH * c + CH)
                ins = nc.gpsimd.tensor_tensor(pbd[q, :, q], d_P[q, :, :],
                                              tab("low_incl")[q, :].unsqueeze(1).to_broadcast([CH, 2 * NM, CH]),
                                              ALU.mult)
            ins.then_inc(s("d_pbd"), 1)
            pool.wait_ge(s("e_k1"), 1)
            pool.wait_ge(s("d_ybd"), 1)
            pool.wait_ge(s("d_pbd"), 1)
            for b in range(B):
                nc.gpsimd.tensor_tensor(e_kT[:, b, :].rearrange("p (h k) -> p h k", k=CTX),
                                        e_k1[:, b, :].unsqueeze(1).to_broadcast([P, EH, CTX]),
                                        tab("ehead").unsqueeze(2).to_broadcast([P, EH, CTX]),
                                        ALU.mult).then_inc(s("e_kT"), 1)
            for n in range(NC):
                if n >= 1:
                    pool.wait_ge(s("d_state"), n)
                if n >= 2:
                    pool.wait_ge(s("d_against"), n - 1)
                nc.gpsimd.tensor_tensor(sbd[:, n % 2, :, :].rearrange("p b (h w) -> p b h w", h=GH),
                                        d_S[:, n, :, :].unsqueeze(2).to_broadcast([P, 2, GH, GV]),
                                        tab("head4").unsqueeze(1).unsqueeze(3).to_broadcast([P, 2, GH, GV]),
                                        ALU.mult).then_inc(s("d_diag"), 1)
            vm = tab("vmask").rearrange("p (k n) -> p k n", k=EK)
            for n, (b, k0, k1) in enumerate(VG):
                pool.wait_ge(s("e_spread"), n + 1)
                nc.gpsimd.tensor_tensor(e_vb[:, b, k0:k1, :], e_vb[:, b, k0:k1, :], vm[:, k0:k1, :],
                                        ALU.mult).then_inc(s("e_vb"), 1)
            for n in range(6, 12):
                split(n)
            for n in range(6 * NE):
                g, c = divmod(n, 3)
                w = F1C[c][1]
                pool.wait_ge(s("f_high"), n + 1)
                nc.gpsimd.tensor_tensor(hp[1][0:w, g % 2, 1, c, :], hid[0:w, g % 2, c, :],
                                        hp[1][0:w, g % 2, 0, c, :], ALU.subtract).then_inc(s("f_low"), 1)

        @block.scalar
        def _(act):
            def turn(use, half, g=None, b=None):
                act.wait_ge(s("turned"), nth(use, half))
                kw = dict(scale=col(g), bias=col(b)) if g else {}
                nc.scalar.activation(xT[:, tok(half)], ps[:, turn_bank(use, half), :], ACT.Identity, **kw).then_inc(
                    s("xT_ready"), 1)

            need(act, "cols")
            for half in range(2):
                turn(A, half, "a_g", "a_b")
            for half in range(2):
                for j, bias in enumerate(("a_bq", "a_bk", "a_bv")):
                    act.wait_ge(s("a_qkv_ps"), 3 * half + j + 1)
                    nc.scalar.activation(a_qkv[:, j, tok(half)], ps[:, 3 * half + j, :], ACT.Identity,
                                         bias=col(bias)).then_inc(s("a_qkv"), 1)
            for half in range(2):
                act.wait_ge(s("a_gap"), half + 1)
                nc.scalar.activation(a_th[:, tok(half)], ps[:, 3 * half, :], ACT.Tanh,
                                     scale=0.5 * 8.0 ** -0.5).then_inc(s("a_th"), 1)
            act.wait_ge(s("b_zero"), 1)
            for g in range(7):
                act.wait_ge(s("b_kv_ps"), g + 1)
                if g < 3:
                    w = min(3, 8 - 3 * g)
                    for k in range(2):
                        q = slice(XD * k, XD * k + XD)
                        ins = nc.scalar.activation(
                            b_kT[q, 3 * g:3 * g + w, :, k, :],
                            ps[q, 6 + g % 2, 0:w * B * CTX].rearrange("p (c b n) -> p c b n", c=w, b=B),
                            ACT.Copy)
                else:
                    b, n = divmod(g - 3, 2)
                    ins = nc.scalar.activation(b_v[0:CTX, b, 512 * n:512 * n + 512],
                                               ps[0:CTX, 6 + g % 2, :], ACT.Copy)
                ins.then_inc(s("b_kv"), 1)
            turn(X, 0, "x_g", "x_b")
            for i in range(NI):
                if i == 1:
                    turn(X, 1, "x_g", "x_b")
                if i in (0, HT):
                    for r in range(8):
                        act.wait_ge(s("b_ring"), RAT[("q", i // HT, r)] + 1)
                        nc.scalar.activation(b_q[:, r, :], ps[:, ring(RAT[("q", i // HT, r)]), :], ACT.Copy,
                                             scale=XD ** -0.5).then_inc(s("b_ringed"), 1)
                if 2 <= i < NT + 2:
                    for r in range(4):
                        n = RAT[("pT", i - 2, r)]
                        act.wait_ge(s("b_ring"), n + 1)
                        nc.scalar.activation(
                            b_pT[0:CTX, 4 * r:4 * r + 4, :],
                            ps[0:CTX, ring(n), :].rearrange("p (j n) -> p j n", j=4),
                            ACT.Copy).then_inc(s("b_ringed"), 1)
                if 3 <= i:
                    for r in range(2):
                        n = RAT[("oT", i - 3, r)]
                        act.wait_ge(s("b_ring"), n + 1)
                        nc.scalar.activation(b_oT[:, 4 * r:4 * r + 4, :],
                                             ps[:, ring(n), :].rearrange("p (j n) -> p j n", j=4),
                                             ACT.Copy).then_inc(s("b_ringed"), 1)
                if i < NT:
                    act.wait_ge(s("b_sub"), i + 1)
                    nc.scalar.activation(b_s[:, i % 3, :], b_s[:, i % 3, :], ACT.Exp).then_inc(
                        s("b_exp"), 1)
            def split_x(which, half):
                use = (F, H)[which]
                turn(use, half)
                act.wait_ge(s("xT_ready"), nth(use, half))
                if which:
                    act.wait_ge(s("w_split"), 12)
                nc.scalar.activation(xs[which][:, half, 0, :], xT[:, tok(half)], ACT.Copy, scale=XS).then_inc(
                    s("x_high"), 1)

            def r_exp(which, half):
                act.wait_ge(s("r_shift"), 2 * which + half + 1)
                nc.scalar.activation(r_e(half), r_e(half), ACT.Exp).then_inc(s("r_exp"), 1)

            split_x(0, 0)
            r_exp(0, 0)
            for half in range(2):
                for e in range(NE):
                    g = NE * half + e
                    if g == 0:
                        need(act, "fb1")
                        act.wait_ge(s("w_split"), 6)
                    if g >= 2:
                        act.wait_ge(s("c_y"), g - 1)
                    for c in range(C0 + 1):
                        if c < C0:
                            if g >= 2:
                                act.wait_ge(s("c_low"), C0 * (g - 2) + c + 1)
                            act.wait_ge(s("c_h_ps"), C0 * g + c + 1)
                            nc.scalar.activation(hid[:, g % 2, c, :], ps[:, c, :], ACT.Gelu_apprx_tanh,
                                                 bias=fb1[:, e, c:c + 1], scale=1.0 / (XS * WS)).then_inc(
                                s("c_h"), 1)
                        if c >= 1:
                            act.wait_ge(s("c_h"), C0 * g + c)
                            nc.scalar.activation(hp[0][:, g % 2, 0, c - 1, :], hid[:, g % 2, c - 1, :], ACT.Copy,
                                                 scale=HS).then_inc(s("c_high"), 1)
                    if g == 3:
                        split_x(0, 1)
                        r_exp(0, 1)
                    if g == 2 * NE - 3:
                        turn(G, 0, "d_g", "d_b")
                    if e == 1:
                        act.wait_ge(s("c_combT_ps"), half + 1)
                        nc.scalar.activation(combT[:, half, :], ps[0:E, 6 + half, :], ACT.Copy,
                                             scale=WS * HS).then_inc(s("c_combT"), 1)
            for half in range(2):
                if half == 1:
                    turn(G, 1, "d_g", "d_b")
                act.wait_ge(s("c_low"), C0 * (2 * NE - 1 + half))
                for t in range(HT):
                    act.wait_ge(s("d_qkv"), HT * half + t + 1)
                    nc.scalar.activation(hid[:, half, t, :], ps[:, 4 * half + t, :], ACT.Silu).then_inc(
                        s("d_silu"), 1)
                act.wait_ge(s("d_beta_ps"), half + 1)
                nc.scalar.activation(sm[:, 128 + 16 * half:144 + 16 * half], ps[:, 4 * half, 0:16], ACT.Tanh,
                                     scale=0.5).then_inc(s("d_tanh"), 1)
            for half in range(2):
                for w in range(3):
                    act.wait_ge(s("d_turn_ps"), 3 * half + w + 1)
                    nc.scalar.activation(d_T[:, half, w, :], ps[:, 4 * half + w, :], ACT.Copy).then_inc(
                        s("d_turn"), 1)
            act.wait_ge(s("d_ab"), 1)
            nc.scalar.activation(d_P.rearrange("p (b t) i -> p b t i", b=8),
                                 ps[:, :, 0:256].rearrange("p b (t w i) -> p b t w i", t=HT, w=2)[:, :, :, 1, :],
                                 ACT.Copy).then_inc(s("d_pt"), 1)
            act.wait_ge(s("e_kT_ps"), 1)
            nc.scalar.activation(e_k1, ps[:, 0, 0:B * CTX].rearrange("p (b k) -> p b k", b=B),
                                 ACT.Copy).then_inc(s("e_k1"), 1)
            for half in range(2):
                act.wait_ge(s("d_uw_ps"), half + 1)
                uw = ps[:, 4 * half:4 * half + 4, 0:384].rearrange("p t (h w) -> p t h w", h=GH)
                for t in range(HT):
                    nc.scalar.activation(d_u[:, half, t, :, :], uw[:, t, :, 0:GV], ACT.Copy)
                    ins = nc.scalar.activation(d_w[:, half, t, :].rearrange("p (h k) -> p h k", h=GH),
                                               uw[:, t, :, GV:96], ACT.Copy)
                ins.then_inc(s("d_uw"), 1)
            for half in range(2):
                act.wait_ge(s("d_wT_ps"), half + 1)
                nc.scalar.activation(d_wT[:, half, :], ps[:, 4 * half, :], ACT.Copy).then_inc(s("d_wT"), 1)
            for t in range(HT):
                act.wait_ge(s("d_o_ps"), t + 1)
                o = ps[:, 6 + t % 2, :].rearrange("p (b n) -> p b n", b=2)
                nc.scalar.activation(d_o[:, :, t, :, :].rearrange("p b h w -> p b (h w)"), o, ACT.Copy)
                nc.scalar.activation(d_sq[:, :, t, :, :].rearrange("p b h w -> p b (h w)"), o,
                                     ACT.Square).then_inc(s("d_sq"), 1)
            for n, (b, k0, k1) in enumerate(VG):
                act.wait_ge(s("e_vb_ps"), n + 1)
                nc.scalar.activation(e_vb[:, b, k0:k1, :],
                                     ps[:, 4 + n % 2, 0:144 * (k1 - k0)].rearrange("p (k n) -> p k n", n=144),
                                     ACT.Copy).then_inc(s("e_spread"), 1)
            for half in range(2):
                for w in range(2):
                    act.wait_ge(s("d_oT_ps"), 2 * half + w + 1)
                    nc.scalar.activation(d_T[:, half, w, :], ps[:, 4 * half + w, :], ACT.Copy).then_inc(
                        s("d_oT"), 1)
            act.wait_ge(s("e_kT"), 2)
            for half in range(2):
                turn(EX, half)
                act.wait_ge(s("e_q_ps"), half + 1)
                nc.scalar.activation(e_q[:, half, :], ps[:, 2 * half, :], ACT.Identity,
                                     bias=col("e_bq")).then_inc(s("e_q"), 1)
            for i in range(NT + 2):
                if i < NT:
                    act.wait_ge(s("e_sc"), i + 1)
                    act.wait_ge(s("e_scale"), i // HT + 1)
                    nc.scalar.activation(e_p[:, i % 2, :].rearrange("p (i k) -> p i k", i=4),
                                         ps[:, 0:4, 0:4 * CTX], ACT.Exp,
                                         scale=sm[:, 256 + i:257 + i]).then_inc(s("e_exp"), 1)
                if 1 <= i <= NT:
                    for r in range(3):
                        n = 3 * (i - 1) + r
                        m = 4 if r < 2 else 2
                        act.wait_ge(s("e_pT_ps"), n + 1)
                        if r < 2:
                            ins = nc.scalar.activation(e_pT[:, 4 * r:4 * r + 4, :],
                                                       ps[:, 4 + n % 2, :].rearrange("p (k n) -> p k n", k=4),
                                                       ACT.Copy)
                        else:
                            nc.scalar.activation(e_pT[:, 8, :], ps[:, 4 + n % 2, 0:128], ACT.Copy)
                            ins = nc.scalar.activation(e_pT[0:EP - 9 * 128, 9, :],
                                                       ps[0:EP - 9 * 128, 4 + n % 2, 128:256], ACT.Copy)
                        ins.then_inc(s("e_pT"), 1)
                if 2 <= i:
                    t = i - 2
                    act.wait_ge(s("e_oT_ps"), t + 1)
                    nc.scalar.activation(e_oT[:, t % 2, :], ps[:, 6 + t % 2, 256:384], ACT.Copy).then_inc(
                        s("e_oT"), 1)
            split_x(1, 0)
            r_exp(1, 0)

            def f_high(n):
                g, c = divmod(n, 3)
                w = F1C[c][1]
                act.wait_ge(s("f_h"), n + 1)
                if g >= 2:
                    act.wait_ge(s("f_y"), g - 1)
                nc.scalar.activation(hp[1][0:w, g % 2, 0, c, :], hid[0:w, g % 2, c, :], ACT.Copy).then_inc(
                    s("f_high"), 1)

            for n in range(6 * NE):
                g, c = divmod(n, 3)
                w = F1C[c][1]
                if g >= 2:
                    act.wait_ge(s("f_low"), n - 5)
                act.wait_ge(s("f_gate_ps"), n + 1)
                nc.scalar.activation(hid[0:w, g % 2, c, :], ps[0:w, 2 * (n % 2), :], ACT.Silu,
                                     scale=1.0 / (XS * WS)).then_inc(s("f_silu"), 1)
                if n >= 1:
                    f_high(n - 1)
                if n == 3 * 6 - 1:
                    split_x(1, 1)
                    r_exp(1, 1)
            f_high(6 * NE - 1)

        @block.vector
        def _(dve):
            done = [0]

            def link(ins):
                done[0] += 1
                ins.then_inc(s("dve_chain"), 1)
                dve.wait_ge(s("dve_chain"), done[0])

            def bc(ap, shape):
                return ap.to_broadcast(shape)

            def inv_sqrt(v, y, w):
                link(nc.vector.tensor_scalar(w.bitcast(U32), v.bitcast(U32), 1, None,
                                             ALU.logical_shift_right))
                link(nc.vector.tensor_scalar(y.bitcast(I32), w.bitcast(I32), -1.0, MAGIC, ALU.mult, ALU.add))
                for _ in range(3):
                    link(nc.vector.tensor_tensor(w, y, y, ALU.mult))
                    link(nc.vector.scalar_tensor_tensor(w, w, -0.5, v, ALU.mult, ALU.mult))
                    link(nc.vector.scalar_tensor_tensor(y, w, 1.5, y, ALU.add, ALU.mult))

            def norm(src, dst, half):
                for t in range(HT * half, HT * half + HT):
                    ins = nc.vector.bn_stats(bn6[:, t, :], src[:, t, :])
                link(ins)
                for t in range(HT * half, HT * half + HT):
                    ins = nc.vector.bn_aggr(bn2[:, t, :], bn6[:, t, :])
                link(ins)
                v, w, y = rt[:, 0, 0:HT], rt[:, 1, 0:HT], rt[:, 2, 0:HT]
                link(nc.vector.tensor_scalar(v, bn2[:, til(half), 1], 1e-5, None, ALU.add))
                inv_sqrt(v, y, w)
                for t in range(HT):
                    ins = nc.vector.tensor_scalar(dst[:, HT * half + t, :], src[:, HT * half + t, :],
                                                  bn2[:, HT * half + t, 0:1], y[:, t:t + 1],
                                                  ALU.subtract, ALU.mult)
                return ins

            def rowb(n, k):
                return row(n).unsqueeze(1).to_broadcast([P, k, ROFF[n][1]])

            def shift(which, half, extra):
                L, Ex = r_l(half), r_e(half)
                dve.wait_ge(s("r_logit"), 2 * which + half + 1)
                lp = ps[:, 6 + half, 0:HT * E].rearrange("p (t e) -> p t e", e=E)
                if extra is None:
                    link(nc.vector.tensor_copy(L, lp))
                else:
                    link(nc.vector.tensor_tensor(L, lp, rowb(extra, HT), ALU.add))
                m = sm[:, 300:304]
                link(nc.vector.tensor_reduce(m, L, AX.X, ALU.max))
                nc.vector.tensor_tensor(Ex, L, m.unsqueeze(2).to_broadcast([P, HT, E]),
                                        ALU.subtract).then_inc(s("r_shift"), 1)

            def route(which, half, eps):
                L, Ex, m = r_l(half), r_e(half), sm[:, 300:304]
                dve.wait_ge(s("r_exp"), 2 * which + half + 1)
                link(nc.vector.tensor_reduce(m, Ex, AX.X, ALU.add))
                link(nc.vector.reciprocal(sm[:, 308:312], m))
                link(nc.vector.tensor_tensor(L, Ex, sm[:, 308:312].unsqueeze(2).to_broadcast([P, HT, E]),
                                             ALU.mult))
                top = sm[:, 320:352].rearrange("p (t e) -> p t e", e=E)
                for t in range(HT):
                    ins = nc.vector.max(top[:, t, :], L[:, t, :])
                link(ins)
                for t in range(HT):
                    ins = nc.vector.max_index(idx[:, t, :], top[:, t, :], L[:, t, :])
                link(ins)
                at = sm[:, 352:384].rearrange("p (t e) -> p t e", e=E)
                link(nc.vector.tensor_copy(at, idx[:, :, :]))
                link(nc.vector.tensor_tensor(sm[:, 312:316], top[:, :, 0], top[:, :, 1], ALU.add))
                link(nc.vector.tensor_scalar(sm[:, 312:316], sm[:, 312:316], eps, WS * HS, ALU.add, ALU.mult))
                link(nc.vector.reciprocal(sm[:, 316:320], sm[:, 312:316]))
                link(nc.vector.tensor_tensor(top[:, :, 0:2], top[:, :, 0:2],
                                             sm[:, 316:320].unsqueeze(2).to_broadcast([P, HT, 2]), ALU.mult))
                iota = tab("iota").unsqueeze(1).to_broadcast([P, HT, E])
                hit = [sm[:, 384:416].rearrange("p (t e) -> p t e", e=E),
                       sm[:, 416:448].rearrange("p (t e) -> p t e", e=E)]
                for k in range(2):
                    link(nc.vector.tensor_tensor(hit[k], iota,
                                                 at[:, :, k:k + 1].to_broadcast([P, HT, E]), ALU.is_equal))
                    link(nc.vector.tensor_tensor(hit[k], hit[k],
                                                 top[:, :, k:k + 1].to_broadcast([P, HT, E]), ALU.mult))
                nc.vector.tensor_tensor(comb[:, til(half), :], hit[0], hit[1], ALU.add).then_inc(
                    s("r_comb"), 1)
                dve.wait_ge(s("r_comb"), 2 * which + half + 1)

            need(dve, "x")
            for half in range(2):
                norm(res, z, half).then_inc(s("z_ready"), 1)
            need(dve, "rows")
            for half in range(2):
                nc.vector.scalar_tensor_tensor(pre[:, til(half), :], res[:, til(half), :], 2.0,
                                               rowb("a_bo", HT), ALU.mult, ALU.add)
            need(dve, "mask")
            link(nc.vector.tensor_copy(mask_f[:, :, :], mask_u8[:, :, :]))
            link(nc.vector.tensor_scalar(mask_f[:, :, :], mask_f[:, :, :], 1.0, 1e30, ALU.subtract, ALU.mult))
            dve.wait_ge(s("a_qkv"), 6)
            link(nc.vector.tensor_tensor(a_kd, a_qkv[:, 1, tok(0)], a_qkv[:, 1, tok(1)], ALU.subtract))
            for half in range(2):
                nc.vector.tensor_tensor(a_prod[:, tok(half)], a_qkv[:, 0, tok(half)], a_kd, ALU.mult).then_inc(
                    s("a_prod"), 1)
            nc.vector.tensor_tensor(a_vd, a_qkv[:, 2, tok(0)], a_qkv[:, 2, tok(1)], ALU.subtract)
            link(nc.vector.tensor_tensor(a_vs, a_qkv[:, 2, tok(0)], a_qkv[:, 2, tok(1)], ALU.add))
            for half in range(2):
                dve.wait_ge(s("a_th"), half + 1)
                link(nc.vector.scalar_tensor_tensor(a_th[:, tok(half)], a_th[:, tok(half)], 0.5, a_vd,
                                                    ALU.mult, ALU.mult))
                nc.vector.scalar_tensor_tensor(a_o[:, tok(half)], a_vs, 0.5, a_th[:, tok(half)],
                                               ALU.mult, ALU.add).then_inc(s("a_o"), 1)

            def join(half, bank, name, n):
                dve.wait_ge(s(name), n)
                link(nc.vector.tensor_tensor(pre[:, til(half), :],
                                             ps[:, bank, :].rearrange("p (t d) -> p t d", t=HT),
                                             pre[:, til(half), :], ALU.add))

            for half in range(2):
                join(half, 3 * half + 1, "a_y", half + 1)
            for half in range(2):
                link(norm(pre, res, half))
                norm(res, z, half).then_inc(s("z_ready"), 1)
                link(nc.vector.tensor_tensor(pre[:, til(half), :], res[:, til(half), :], rowb("x_bo", HT),
                                             ALU.add))

            def low_x(which, half):
                dve.wait_ge(s("x_high"), 2 * which + half + 1)
                nc.vector.scalar_tensor_tensor(xs[which][:, half, 1, :], xT[:, tok(half)], XS,
                                               xs[which][:, half, 0, :], ALU.mult, ALU.subtract).then_inc(
                    s("x_low"), 1)

            def to_experts(half):
                norm(pre, res, half).then_inc(s("z_ready"), 1)
                dve.wait_ge(s("z_ready"), nth(F, half))
                link(nc.vector.tensor_tensor(pre[:, til(half), :], res[:, til(half), :],
                                             rowb("f_b2", HT), ALU.add))

            rs = [sm[:, 48:64], sm[:, 448:464], sm[:, 464:480]]
            for i in range(NI):
                if i < NT:
                    dve.wait_ge(s("b_sc"), i + 1)
                    sc = b_s[:, i % 3, :].rearrange("p (h k) -> p h k", k=CTX)
                    m3 = mask_f[:, i % HT, :].unsqueeze(1)
                    nc.vector.tensor_tensor(
                        b_s[:, i % 3, 0:12 * CTX].rearrange("p (i j k) -> p i j k", i=2, k=CTX),
                        ps[:, 0:2, 0:6 * CTX].rearrange("p i (j k) -> p i j k", k=CTX),
                        m3.unsqueeze(1).to_broadcast([P, 2, 6, CTX]), ALU.add)
                    link(nc.vector.tensor_tensor(
                        sc[:, 12:16, :], ps[:, 2, 0:4 * CTX].rearrange("p (j k) -> p j k", k=CTX),
                        m3.to_broadcast([P, 4, CTX]), ALU.add))
                    nc.vector.tensor_reduce(sm[:, 16 * (i % 3):16 * (i % 3) + 16], sc, AX.X,
                                            ALU.max).then_inc(s("b_max"), 1)
                if 1 <= i <= NT:
                    t = i - 1
                    dve.wait_ge(s("b_exp"), t + 1)
                    link(nc.vector.tensor_reduce(sm[:, 480:496],
                                                 b_s[:, t % 3, :].rearrange("p (h k) -> p h k", k=CTX),
                                                 AX.X, ALU.add))
                    link(nc.vector.reciprocal(rs[t % 3], sm[:, 480:496]))
                if 2 <= i < NT + 2:
                    t = i - 2
                    dve.wait_ge(s("b_pv"), t + 1)
                    nc.vector.tensor_tensor(
                        b_o[:, t % 2, :].rearrange("p (h d) -> p h d", d=XD),
                        ps[:, 6:8, :].rearrange("p b (h d) -> p (b h) d", d=XD),
                        rs[t % 3].unsqueeze(2).to_broadcast([P, XH, XD]), ALU.mult).then_inc(s("b_o"), 1)
                if 3 <= i:
                    t = i - 3
                    n = RAT[("y", t, 0)]
                    dve.wait_ge(s("b_ring"), n + 1)
                    nc.vector.tensor_tensor(pre[:, t, :], ps[:, ring(n), 0:128], pre[:, t, :],
                                            ALU.add).then_inc(s("b_yadd"), 1)
                    if t % HT == HT - 1:
                        dve.wait_ge(s("b_yadd"), t + 1)
                        half = t // HT
                        if half == 1:
                            low_x(0, 0)
                            need(dve, "tabs")
                            shift(0, 0, "f_rb")
                        else:
                            to_experts(half)


            def gather(which, half, e, bank):
                for t in range(HT * half, HT * half + HT):
                    y = ps[:, bank, 128 * (t % HT):128 * (t % HT) + 128]
                    if e == 0:
                        ins = nc.vector.scalar_tensor_tensor(pre[:, t, :], y, 1.0 / (WS * HS), pre[:, t, :],
                                                             ALU.mult, ALU.add)
                    else:
                        ins = nc.vector.scalar_tensor_tensor(pre[:, t, :], y, comb[:, t, e - 1:e],
                                                             pre[:, t, :], ALU.mult, ALU.add)
                return ins

            def c_low(g):
                for c in range(C0):
                    dve.wait_ge(s("c_high"), C0 * g + c + 1)
                    nc.vector.scalar_tensor_tensor(hp[0][:, g % 2, 1, c, :], hid[:, g % 2, c, :], HS,
                                                   hp[0][:, g % 2, 0, c, :], ALU.mult,
                                                   ALU.subtract).then_inc(s("c_low"), 1)

            route(0, 0, 0.0)
            def twice(half):
                nc.vector.tensor_tensor(pre[:, til(half), :], res[:, til(half), :], res[:, til(half), :],
                                        ALU.add)

            c_low(0)
            for half in range(2):
                for e in range(NE):
                    g = NE * half + e
                    if g + 1 < 2 * NE:
                        c_low(g + 1)
                    dve.wait_ge(s("c_y"), g + 1)
                    gather(0, half, e, 4 + g % 2).then_inc(s("c_acc"), 1)
                    dve.wait_ge(s("c_acc"), g + 1)
                    if e == 1:
                        join(half, 6 + half, "c_b2", half + 1)
                    if g == 0:
                        to_experts(1)
                    if g == 2:
                        low_x(0, 1)
                        shift(0, 1, "f_rb")
                    if g == 4:
                        route(0, 1, 0.0)
                    if g == NE:
                        link(norm(pre, res, 0))
                    if g == NE + 2:
                        norm(res, z, 0).then_inc(s("z_ready"), 1)
                    if g == NE + 3:
                        twice(0)
            link(norm(pre, res, 1))
            norm(res, z, 1).then_inc(s("z_ready"), 1)
            twice(1)

            for half in range(2):
                v = hid[:, half, :, :]
                qk = v[:, :, 0:256].rearrange("p t (h k) -> p t h k", k=GK)
                beta = sm[:, 128 + 16 * half:144 + 16 * half]
                dve.wait_ge(s("d_silu"), HT * half + HT)
                sq = d_sq[:, half, :, :, :].rearrange("p t h w -> p (t h w)").rearrange(
                    "p (t h k) -> p t h k", t=HT, h=8)
                link(nc.vector.tensor_tensor(sq, qk, qk, ALU.mult))
                vv, ww, yy = rt[:, 0, 0:32], rt[:, 1, 0:32], rt[:, 2, 0:32]
                link(nc.vector.tensor_reduce(vv.rearrange("p (t h) -> p t h", t=HT), sq, AX.X, ALU.add))
                link(nc.vector.tensor_scalar(vv, vv, 1e-6, None, ALU.add))
                inv_sqrt(vv, yy, ww)
                y3 = yy.rearrange("p (t h) -> p t h", t=HT)
                link(nc.vector.tensor_scalar(y3[:, :, 0:GH], y3[:, :, 0:GH], GK ** -0.5, None, ALU.mult))
                link(nc.vector.tensor_tensor(d_qk[:, half, :, :, :], qk,
                                             y3.unsqueeze(3).to_broadcast([P, HT, 8, GK]), ALU.mult))
                dve.wait_ge(s("d_tanh"), half + 1)
                link(nc.vector.tensor_scalar(beta, beta, 0.5, 0.5, ALU.mult, ALU.add))
                b3 = beta.rearrange("p (t h) -> p t h", t=HT)
                nc.vector.tensor_tensor(d_r[:, half, :, :, 0:GV],
                                        v[:, :, 256:512].rearrange("p t (h w) -> p t h w", w=GV),
                                        b3.unsqueeze(3).to_broadcast([P, HT, GH, GV]), ALU.mult)
                nc.vector.tensor_tensor(d_P[:, NM * half:NM * half + NM, :].rearrange("p (t h) k -> p t h k", t=HT),
                                        d_qk[:, half, :, 4:8, :],
                                        b3.unsqueeze(3).to_broadcast([P, HT, GH, GK]), ALU.mult)
                nc.vector.tensor_tensor(d_r[:, half, :, :, GV:96], d_qk[:, half, :, 4:8, :],
                                        b3.unsqueeze(3).to_broadcast([P, HT, GH, GK]), ALU.mult).then_inc(
                    s("d_norm"), 1)
            link(nc.vector.memset(e_kv[:, :, 256:272], 1.0))
            dve.wait_ge(s("e_kv_ps"), 1)
            o = ROFF["e_bk"][0]
            nc.vector.tensor_tensor(e_kv[:, :, 0:256], ps[0:CTX, 3, :].rearrange("p (b n) -> p b n", b=B),
                                    rows[0:CTX, o:o + 256].unsqueeze(1).to_broadcast([CTX, B, 256]),
                                    ALU.add).then_inc(s("e_kv"), 1)
            dve.wait_ge(s("e_kv"), 1)
            link(nc.vector.tensor_tensor(e_sq, e_kv[:, :, 0:128], e_kv[:, :, 0:128], ALU.mult))
            vv, ww, yy = rt[0:CTX, 0, 0:B], rt[0:CTX, 1, 0:B], rt[0:CTX, 2, 0:B]
            link(nc.vector.tensor_reduce(vv, e_sq, AX.X, ALU.add))
            link(nc.vector.tensor_scalar(vv, vv, 1e-24, None, ALU.max))
            inv_sqrt(vv, yy, ww)
            nc.vector.tensor_tensor(e_kv[:, :, 0:128], e_kv[:, :, 0:128],
                                    yy.unsqueeze(2).to_broadcast([CTX, B, 128]), ALU.mult).then_inc(s("e_kn"), 1)
            dve.wait_ge(s("d_gram"), 2)
            nc.vector.transpose(inv_a[:, :],
                                ps[:, :, 0:256].rearrange("p b (t w i) -> p i b t w", t=HT, w=2)[:, :, :, :, 0]
                                ).then_inc(s("d_ab"), 1)
            dve.wait_ge(s("d_ab"), 1)
            dve.wait_ge(s("d_zero"), 2)
            link(nc.vector.tensor_scalar(inv_x[:, CH:CH * CH:2 * CH + 2], inv_a[:, CH:CH * CH:2 * CH + 2], -1.0,
                                         None, ALU.mult))

            def at(buf, off, *dims):
                row_len = int(np.prod(buf.shape[1:]))
                return bass.AP(tensor=buf[:, :].tensor, offset=off,
                               ap=[[row_len, P]] + [list(d) for d in dims])

            for sz in (2, 4, 8, 16):
                g, step = CH // (2 * sz), 2 * sz * (CH + 1)
                parts = {16: 4, 8: 2}.get(sz, 1)
                w = sz // parts
                for second in range(2):
                    todo, off = [], 0
                    for p0 in range(0, sz, w):
                        if second:
                            ni, nk, nj = w, sz, p0 + w
                            left = inv_x, sz * (CH + 1) + CH * p0, CH, 0, 1, step
                            right = inv_t, 0, 0, 1, sz, sz * sz
                            out = at(inv_x, sz * CH + CH * p0, (step, g), (CH, ni), (1, nk))
                        else:
                            ni, nk, nj = sz, w, sz - p0
                            left = inv_a, sz * CH + p0, CH, 0, 1, step
                            right = inv_x, (CH + 1) * p0, 0, 1, CH, step
                            out = at(inv_t, p0, (sz * sz, g), (sz, ni), (1, nk))
                        prod = hid, off, nk * nj, nj, 1, ni * nk * nj

                        def piece(v, n):
                            buf, o, si, sk, sj, sg = v
                            if g > ni:
                                return at(buf, o + si * n, (sg, g), (sk, nk), (sj, nj))
                            return at(buf, o + sg * n, (si, ni), (sk, nk), (sj, nj))

                        for n in range(min(g, ni)):
                            ins = nc.vector.tensor_tensor(piece(prod, n), piece(left, n), piece(right, n),
                                                          ALU.mult)
                        todo.append((out, at(hid, off, (nj, g * ni * nk), (1, nj))))
                        off += g * ni * nk * nj
                    link(ins)
                    for out, prod in todo:
                        ins = nc.vector.tensor_reduce(out, prod, AX.X, ALU.add, negate=bool(second))
                    link(ins)
            dve.wait_ge(s("d_zero"), 3)
            for c in range(4):
                q = slice(CH * c, CH * c + CH)
                ins = nc.vector.transpose(ybd[q, :, q].rearrange("p m i -> p i m"), inv_x[q, :])
            ins.then_inc(s("d_ybd"), 1)
            for half in range(2):
                dve.wait_ge(s("d_mt"), half + 1)
                nc.vector.tensor_tensor(mbd[:, NM * half:NM * half + NM, :],
                                        ps[:, 4 * half:4 * half + 4, :].rearrange("p c (t j) -> p (c t) j", j=128),
                                        tab("blk_neg").unsqueeze(1).to_broadcast([P, NM, 128]),
                                        ALU.mult).then_inc(s("d_mbd"), 1)
            vv, ww, yy = rt[:, 0, 0:32], rt[:, 1, 0:32], rt[:, 2, 0:32]

            def d_square_sums(t):
                dve.wait_ge(s("d_sq"), t + 1)
                return nc.vector.tensor_reduce(vv.rearrange("p (b t h) -> p b t h", b=2, t=HT)[:, :, t, :],
                                               d_sq[:, :, t, :, :], AX.X, ALU.add)

            def d_less_ws(t):
                dve.wait_ge(s("d_ws"), t + 1)
                u = d_u[:, :, t, :, :].rearrange("p b h w -> p b (h w)")
                nc.vector.tensor_tensor(u, u, ps[:, 4 + t % 2, :].rearrange("p (b n) -> p b n", b=2),
                                        ALU.subtract).then_inc(s("d_u"), 1)

            for n in range(NC - 1):
                dve.wait_ge(s("d_step"), n + 1)
                nc.vector.tensor_tensor(d_S[:, n + 1, :, :], ps[:, 2 * (n % 2):2 * (n % 2) + 2, 0:GV],
                                        d_S[:, n, :, :], ALU.add).then_inc(s("d_state"), 1)
                dve.wait_ge(s("d_state"), n + 1)
                t, c = divmod(n, 4)
                if c == 0 and t >= 1:
                    d_less_ws(t - 1)
                if c == 3 and t >= 1:
                    d_square_sums(t - 1)
            d_less_ws(HT - 1)
            d_square_sums(HT - 2)
            link(d_square_sums(HT - 1))
            link(nc.vector.tensor_scalar(vv, vv, 1.0 / GV, 1e-5, ALU.mult, ALU.add))
            inv_sqrt(vv, yy, ww)
            for half in range(2):
                o = d_o[:, half, :, :, :].rearrange("p t h w -> p (t h) w")
                nc.vector.tensor_tensor(
                    o, o, yy[:, NM * half:NM * half + NM].unsqueeze(2).to_broadcast([P, NM, GV]),
                    ALU.mult).then_inc(s("d_on"), 1)
            for half in range(2):
                join(half, 4 * half + 2, "d_y", half + 1)
                norm(pre, res, half).then_inc(s("z_ready"), 1)

            for half in range(2):
                dve.wait_ge(s("e_qt_ps"), half + 1)
                nc.vector.tensor_tensor(z[:, til(half), :],
                                        ps[:, 2 * half + 1, :].rearrange("p (t d) -> p t d", t=HT),
                                        rowb("e_bq", HT), ALU.add).then_inc(s("e_qt"), 1)
            dve.wait_ge(s("e_qt"), 2)
            for half in range(2):
                qp = z[:, til(half), :]
                link(nc.vector.tensor_tensor(pre[:, til(half), :], qp, qp, ALU.mult))
                vv, ww, yy = rt[:, 0, 0:HT], rt[:, 1, 0:HT], rt[:, 2, 0:HT]
                link(nc.vector.tensor_reduce(vv, pre[:, til(half), :], AX.X, ALU.add))
                link(nc.vector.tensor_scalar(vv, vv, 1e-24, None, ALU.max))
                inv_sqrt(vv, yy, ww)
                nc.vector.tensor_scalar(sm[:, 256 + HT * half:260 + HT * half], yy, 8.0 ** -0.5, None,
                                        ALU.mult).then_inc(s("e_scale"), 1)
                link(nc.vector.tensor_tensor(pre[:, til(half), :], qp, rowb("e_bo", HT), ALU.add))

            def e_tail(half, step):
                hs = til(half)
                if step == 0:
                    link(norm(pre, z, half))
                elif step == 1:
                    link(nc.vector.tensor_tensor(z[:, hs, :], z[:, hs, :], rowb("e_g", HT), ALU.mult))
                    link(nc.vector.tensor_tensor(z[:, hs, :], z[:, hs, :], rowb("e_b", HT), ALU.add))
                    link(nc.vector.tensor_tensor(pre[:, hs, :], z[:, hs, :], res[:, hs, :], ALU.add))
                else:
                    norm(pre, res, half).then_inc(s("z_ready"), 1)
                    dve.wait_ge(s("z_ready"), nth(H, half))
                    link(nc.vector.tensor_copy(pre[:, hs, :], res[:, hs, :]))

            for i in range(NT + 2):
                if 1 <= i <= NT:
                    t = i - 1
                    dve.wait_ge(s("e_pv"), t + 1)
                    den = rt[:, t % 2, 16:32]
                    link(nc.vector.reciprocal(den, ps[:, 6 + t % 2, 128:144]))
                    nc.vector.tensor_tensor(e_o[:, t % 2, :].rearrange("p (h d) -> p h d", h=EH),
                                            ps[:, 6 + t % 2, 0:128].rearrange("p (h d) -> p h d", h=EH),
                                            den.unsqueeze(2).to_broadcast([P, EH, 8]),
                                            ALU.mult).then_inc(s("e_o"), 1)
                if 2 <= i:
                    t = i - 2
                    dve.wait_ge(s("e_y"), t + 1)
                    nc.vector.tensor_tensor(pre[:, t, :], ps[:, 6 + t % 2, 384:512], pre[:, t, :],
                                            ALU.add).then_inc(s("e_yadd"), 1)
                    dve.wait_ge(s("e_yadd"), t + 1)
                    if HT <= i - 1 < HT + 3:
                        e_tail(0, i - 1 - HT)

            low_x(1, 0)
            shift(1, 0, None)

            def f_acc(g):
                dve.wait_ge(s("f_y"), g + 1)
                gather(1, g // NE, g % NE, 4 + g % 2).then_inc(s("f_acc"), 1)
                dve.wait_ge(s("f_acc"), g + 1)
                if g == NE or g == 2 * NE - 1:
                    norm(pre, res, g // NE if g > NE else 0).then_inc(s("out_ready"), 1)

            for g in range(2 * NE):
                for c in range(3):
                    n = 3 * g + c
                    w = F1C[c][1]
                    dve.wait_ge(s("f_silu"), n + 1)
                    dve.wait_ge(s("f_up_ps"), n + 1)
                    nc.vector.scalar_tensor_tensor(hid[0:w, g % 2, c, :], ps[0:w, 2 * (n % 2) + 1, :],
                                                   HS / (XS * WS), hid[0:w, g % 2, c, :], ALU.mult,
                                                   ALU.mult).then_inc(s("f_h"), 1)
                if g == 0:
                    route(1, 0, 1e-20)
                if g >= 1:
                    f_acc(g - 1)
                if 1 <= g <= 3:
                    e_tail(1, g - 1)
                if g == 5:
                    low_x(1, 1)
                    shift(1, 1, None)
                if g == 6:
                    route(1, 1, 1e-20)
            f_acc(2 * NE - 1)

        @block.tensor
        def _(pe):
            mm = nc.tensor.matmul

            def turn(use, half, src):
                pe.wait_ge(s("z_ready"), nth(use, half))
                for t in range(HT):
                    ins = nc.tensor.transpose(ps[:, turn_bank(use, half), 128 * t:128 * t + 128],
                                              src[:, HT * half + t, :], ident)
                ins.then_inc(s("turned"), 1)

            need(pe, "tabs")
            for half in range(2):
                turn(A, half, z)
            need(pe, "wa")
            for half in range(2):
                pe.wait_ge(s("xT_ready"), nth(A, half))
                for j in range(3):
                    mm(ps[:, 3 * half + j, :], wa[:, j, :], xT[:, tok(half)], start=True, stop=True).then_inc(
                        s("a_qkv_ps"), 1)
            for half in range(2):
                pe.wait_ge(s("a_prod"), half + 1)
                mm(ps[:, 3 * half, :], tab("head8"), a_prod[:, tok(half)], start=True, stop=True).then_inc(
                    s("a_gap"), 1)
            need(pe, "ctxT", "wxkv")
            for g in range(7):
                if g >= 2:
                    pe.wait_ge(s("b_kv"), g - 1)
                if g < 3:
                    for c in range(3 * g, min(3 * g + 3, 8)):
                        ins = mm(ps[:, 6 + g % 2, B * CTX * (c - 3 * g):B * CTX * (c - 3 * g + 1)],
                                 wxkv[:, 128 * c:128 * c + 128], ctxT[:, :], start=True, stop=True)
                else:
                    b, n = divmod(g - 3, 2)
                    ins = mm(ps[0:CTX, 6 + g % 2, :], ctxT[:, CTX * b:CTX * b + CTX],
                             wxkv[:, XI + 512 * n:XI + 512 * n + 512], start=True, stop=True)
                ins.then_inc(s("b_kv_ps"), 1)
                if g == 1:
                    for half in range(2):
                        pe.wait_ge(s("a_o"), half + 1)
                        for t in range(HT):
                            ins = mm(ps[:, 3 * half + 1, 128 * t:128 * t + 128],
                                     a_o[:, S * half + 128 * t:S * half + 128 * t + 128], wa[:, 3, :],
                                     start=True, stop=True)
                        ins.then_inc(s("a_y"), 1)

            need(pe, "wxq")
            pe.wait_ge(s("b_kv"), 7)
            turn(X, 0, z)

            def b_queries(half):
                if half == 0:
                    pe.wait_ge(s("xT_ready"), nth(X, 0))
                for r in range(8):
                    n = RAT[("q", half, r)]
                    ring_free(pe, n)
                    mm(ps[:, ring(n), :], wxq[:, 128 * r:128 * r + 128], xT[:, tok(half)],
                       start=True, stop=True).then_inc(s("b_ring"), 1)

            def b_scores(t):
                if t % HT == 0:
                    pe.wait_ge(s("b_ringed"), ringed("q", t // HT, 7))
                if t >= 1:
                    pe.wait_ge(s("b_max"), t)
                for r in range(8):
                    ins = mm(ps[:, r // 3, 2 * CTX * (r % 3):2 * CTX * (r % 3 + 1)],
                             b_q[:, r, 128 * (t % HT):128 * (t % HT) + 128],
                             b_kT[:, r, t // HT, :, :].rearrange("p a k -> p (a k)"), start=True, stop=True)
                ins.then_inc(s("b_sc"), 1)

            def b_turn_p(t):
                pe.wait_ge(s("b_exp"), t + 1)
                for r in range(4):
                    n = RAT[("pT", t, r)]
                    ring_free(pe, n)
                    for j in range(4):
                        h = 4 * r + j
                        ins = nc.tensor.transpose(ps[0:CTX, ring(n), 128 * j:128 * j + 128],
                                                  b_s[:, t % 3, CTX * h:CTX * h + CTX], ident)
                    ins.then_inc(s("b_ring"), 1)

            def b_values(t):
                pe.wait_ge(s("b_ringed"), ringed("pT", t, 3))
                if t >= 1:
                    pe.wait_ge(s("b_o"), t)
                else:
                    pe.wait_ge(s("xT_ready"), nth(X, 1))
                for h in range(XH):
                    ins = mm(ps[:, 6 + h // 8, XD * (h % 8):XD * (h % 8) + XD], b_pT[0:CTX, h, :],
                             b_v[0:CTX, t // HT, XD * h:XD * h + XD], start=True, stop=True)
                ins.then_inc(s("b_pv"), 1)

            def b_turn_o(t):
                pe.wait_ge(s("b_o"), t + 1)
                for r in range(2):
                    n = RAT[("oT", t, r)]
                    ring_free(pe, n)
                    for j in range(4):
                        k = 128 * (4 * r + j)
                        ins = nc.tensor.transpose(ps[:, ring(n), 128 * j:128 * j + 128],
                                                  b_o[:, t % 2, k:k + 128], ident)
                    ins.then_inc(s("b_ring"), 1)

            def b_project(t):
                n = RAT[("y", t, 0)]
                if t == 0:
                    need(pe, "wxo")
                ring_free(pe, n)
                pe.wait_ge(s("b_ringed"), ringed("oT", t, 1))
                for k in range(8):
                    ins = mm(ps[:, ring(n), 0:128], b_oT[:, k, :], wxo[:, k, :], start=(k == 0), stop=(k == 7))
                ins.then_inc(s("b_ring"), 1)

            for i in range(NI):
                if i in (0, HT):
                    b_queries(i // HT)
                if i == 1:
                    turn(X, 1, z)
                if i < NT:
                    b_scores(i)
                if 2 <= i < NT + 2:
                    b_turn_p(i - 2)
                if 3 <= i:
                    b_turn_o(i - 3)
                if i == NI - 1:
                    turn(F, 0, res)
                if 2 <= i < NT + 2:
                    b_values(i - 2)
                if 3 <= i:
                    b_project(i - 3)

            def logits(which, half):
                pe.wait_ge(s("xT_ready"), nth(H if which else F, half))
                for t in range(HT):
                    ins = mm(ps[:, 6 + half, E * t:E * t + E],
                             xT[:, S * half + 128 * t:S * half + 128 * t + 128], router[:, which, :],
                             start=True, stop=True)
                ins.then_inc(s("r_logit"), 1)

            need(pe, "router", "fb2")
            logits(0, 0)

            def c_hidden(g):
                half, e = divmod(g, NE)
                if e == 0:
                    pe.wait_ge(s("x_low"), half + 1)
                    pe.wait_ge(s("w_split"), 6)
                for c in range(C0):
                    if g >= 1:
                        pe.wait_ge(s("c_h"), C0 * (g - 1) + c + 1)
                    for i, (p, q) in enumerate(PASSES):
                        ins = mm(ps[:, c, :], w1[:, p, e, 128 * c:128 * c + 128], xs[0][:, half, q, :],
                                 start=(i == 0), stop=(i == 2))
                    ins.then_inc(s("c_h_ps"), 1)

            def c_out(g):
                half, e = divmod(g, NE)
                pe.wait_ge(s("c_low"), C0 * (g + 1))
                if g >= 2:
                    pe.wait_ge(s("c_acc"), g - 1)
                for t in range(HT):
                    for c in range(C0):
                        for i, (p, q) in enumerate(PASSES):
                            ins = mm(ps[:, 4 + g % 2, 128 * t:128 * t + 128],
                                     hp[0][:, g % 2, p, c, 128 * t:128 * t + 128],
                                     w2[:, q, e, D * c:D * c + D],
                                     start=(c == 0 and i == 0), stop=(c == C0 - 1 and i == 2))
                ins.then_inc(s("c_y"), 1)

            def d_project(half):
                pe.wait_ge(s("xT_ready"), nth(G, half))
                if half == 0:
                    need(pe, "wd")
                    pe.wait_ge(s("c_h"), C0 * 2 * NE)
                for t in range(HT):
                    mm(ps[:, 4 * half + t, :], xT[:, S * half + 128 * t:S * half + 128 * t + 128],
                       wd[:, 0:512], start=True, stop=True).then_inc(s("d_qkv"), 1)

            def d_betas(half):
                pe.wait_ge(s("d_silu"), HT * half + 1)
                for t in range(HT):
                    ins = mm(ps[:, 4 * half, 4 * t:4 * t + 4],
                             xT[:, S * half + 128 * t:S * half + 128 * t + 128], wd[:, 512:516],
                             start=True, stop=True)
                ins.then_inc(s("d_beta_ps"), 1)

            for g in range(2 * NE + 1):
                if g < 2 * NE:
                    c_hidden(g)
                if g == 2 * NE:
                    d_project(0)
                if g >= 1:
                    c_out(g - 1)
                if g == 3:
                    turn(F, 1, res)
                    logits(0, 1)
                if g == 2 * NE - 4:
                    turn(G, 0, z)
                if g % NE == 1:
                    half = g // NE
                    if half < 2:
                        pe.wait_ge(s("r_comb"), half + 1)
                        for t in range(HT):
                            ins = nc.tensor.transpose(ps[0:E, 6 + half, 128 * t:128 * t + 128],
                                                      comb[:, HT * half + t, :], ident)
                        ins.then_inc(s("c_combT_ps"), 1)
                        pe.wait_ge(s("c_combT"), half + 1)
                        for t in range(HT):
                            ins = mm(ps[:, 6 + half, 128 * t:128 * t + 128],
                                     combT[:, half, 128 * t:128 * t + 128], fb2[:, :], start=True, stop=True)
                        ins.then_inc(s("c_b2"), 1)

            need(pe, "wdo")
            d_betas(0)
            turn(G, 1, z)
            d_project(1)
            d_betas(1)
            need(pe, "wekv", "spread")
            for b in range(B):
                ins = mm(ps[0:CTX, 3, 256 * b:256 * b + 256], ctxT[:, CTX * b:CTX * b + CTX], wekv[:, :],
                         start=True, stop=True)
            ins.then_inc(s("e_kv_ps"), 1)
            for half in range(2):
                pe.wait_ge(s("d_norm"), half + 1)
                for w in range(3):
                    for t in range(HT):
                        src = (d_qk[:, half, t, 4:8, :], d_P[:, NM * half + GH * t:NM * half + GH * t + GH, :], d_qk[:, half, t, 0:4, :])[w]
                        ins = nc.tensor.transpose(ps[:, 4 * half + w, 128 * t:128 * t + 128], src, ident)
                    ins.then_inc(s("d_turn_ps"), 1)
            for half in range(2):
                pe.wait_ge(s("d_turn"), 3 * half + 3)
                if half == 0:
                    pe.wait_ge(s("e_kv"), 1)
                for h in range(GH):
                    q = slice(GK * h, GK * h + GK)
                    for t in range(HT):
                        for c in range(4):
                            n = 128 * t + CH * c
                            ins = mm(ps[CH * c:CH * c + CH, 4 * half + h, 64 * t:64 * t + 64],
                                     d_T[q, half, 0, n:n + CH], d_T[q, half, 1:3, n:n + CH],
                                     start=True, stop=True, tile_position=(GK * h, CH * c))
                ins.then_inc(s("d_gram"), 1)
            pe.wait_ge(s("e_kn"), 1)
            pe.wait_ge(s("d_ab"), 1)
            pe.wait_ge(s("d_pt"), 1)
            for b in range(B):
                ins = nc.tensor.transpose(ps[:, 0, CTX * b:CTX * b + CTX], e_kv[:, b, 0:128], ident[0:CTX, 0:CTX])
            ins.then_inc(s("e_kT_ps"), 1)
            pe.wait_ge(s("e_k1"), 1)
            pe.wait_ge(s("d_ybd"), 1)
            for half in range(2):
                for t in range(HT):
                    for h in range(GH):
                        ins = mm(ps[:, 4 * half + t, 96 * h:96 * h + 96], ybd[:, NM * half + HT * h + t, :],
                                 d_r[:, half, t, h, :], start=True, stop=True)
                ins.then_inc(s("d_uw_ps"), 1)
            for half in range(2):
                pe.wait_ge(s("d_uw"), half + 1)
                for c in range(4):
                    q = slice(CH * c, CH * c + CH)
                    for t in range(HT):
                        ins = mm(ps[:, 4 * half + c, 128 * t:128 * t + 128], d_w[q, half, t, :],
                                 d_qk[q, half, t, 4:8, :], start=True, stop=True, tile_position=(CH * c, 0))
                ins.then_inc(s("d_mt"), 1)
            for half in range(2):
                pe.wait_ge(s("d_mbd"), half + 1)
                for t in range(HT):
                    ins = nc.tensor.transpose(ps[:, 4 * half, 128 * t:128 * t + 128], d_w[:, half, t, :], ident)
                ins.then_inc(s("d_wT_ps"), 1)

            def d_new(n):
                t, c = divmod(n, 4)
                q = slice(CH * c, CH * c + CH)
                if n >= 2:
                    pe.wait_ge(s("d_state"), n - 1)
                for b in range(2):
                    for h in range(GH):
                        mm(ps[GK * h:GK * h + GK, 2 * (n % 2) + b, 0:GV], d_qk[q, b, t, 4 + h, :],
                           d_u[q, b, t, h, :], start=True, stop=False, tile_position=(CH * c, GK * h),
                           skip_group_check=True)

            def d_against_state(n):
                t, c = divmod(n, 4)
                if c == 0 and t >= 2:
                    pe.wait_ge(s("d_u"), t - 1)
                    pe.wait_ge(s("d_sq"), t - 1)
                pe.wait_ge(s("d_diag"), n + 1)
                for b in range(2):
                    ins = mm(ps[CH * c:CH * c + CH, 4 + t % 2, 256 * b:256 * b + 256],
                             d_wT[:, b, CH * n:CH * n + CH], sbd[:, n % 2, b, :],
                             start=(b == 0), stop=True, tile_position=(0, CH * c), skip_group_check=True)
                if c == 3:
                    ins.then_inc(s("d_ws"), 1)
                for b in range(2):
                    ins = mm(ps[CH * c:CH * c + CH, 6 + t % 2, 256 * b:256 * b + 256],
                             d_T[:, b, 2, CH * n:CH * n + CH], sbd[:, n % 2, b, :],
                             start=(b == 0), stop=False, tile_position=(0, CH * c), skip_group_check=True)
                ins.then_inc(s("d_against"), 1)

            def d_within(t):
                if t == 0:
                    pe.wait_ge(s("d_pbd"), 1)
                pe.wait_ge(s("d_u"), t + 1)
                for b in range(2):
                    for h in range(GH):
                        k = GV * (GH * b + h)
                        ins = mm(ps[:, 6 + t % 2, k:k + GV], pbd[:, NM * b + HT * h + t, :], d_u[:, b, t, h, :],
                                 start=False, stop=True, skip_group_check=True)
                ins.then_inc(s("d_o_ps"), 1)

            pe.wait_ge(s("d_wT"), 2)
            d_new(0)
            for n in range(NC - 1):
                t, c = divmod(n, 4)
                if n >= 1:
                    pe.wait_ge(s("d_state"), n)
                for b in range(2):
                    ins = mm(ps[:, 2 * (n % 2) + b, 0:GV], mbd[:, NM * b + HT * c + t, :], d_S[:, n, b, :],
                             start=False, stop=True, skip_group_check=True)
                ins.then_inc(s("d_step"), 1)
                if n + 1 < NC - 1:
                    d_new(n + 1)
                if n >= 1:
                    d_against_state(n - 1)
                if n >= 6 and c == 2:
                    d_within(t - 1)
            d_against_state(NC - 2)
            d_against_state(NC - 1)
            d_within(HT - 1)
            for n, (b, k0, k1) in enumerate(VG):
                if n >= 2:
                    pe.wait_ge(s("e_spread"), n - 1)
                for k in range(k0, k1):
                    ins = mm(ps[:, 4 + n % 2, 144 * (k - k0):144 * (k - k0) + 144],
                             spread[:, 128 * k:128 * k + 128], e_kv[:, b, 128:272], start=True, stop=True)
                ins.then_inc(s("e_vb_ps"), 1)
            pe.wait_ge(s("d_wdo"), 1)
            for half in range(2):
                pe.wait_ge(s("d_on"), half + 1)
                if half == 1:
                    pe.wait_ge(s("e_spread"), len(VG))
                for w in range(2):
                    for t in range(HT):
                        ins = nc.tensor.transpose(
                            ps[:, 4 * half + w, 128 * t:128 * t + 128],
                            d_o[:, half, t, 2 * w:2 * w + 2, :].rearrange("p h d -> p (h d)"), ident)
                    ins.then_inc(s("d_oT_ps"), 1)
                pe.wait_ge(s("d_oT"), 2 * half + 2)
                for t in range(HT):
                    for w in range(2):
                        ins = mm(ps[:, 4 * half + 2, 128 * t:128 * t + 128],
                                 d_T[:, half, w, 128 * t:128 * t + 128], wdo[:, w, :],
                                 start=(w == 0), stop=(w == 1))
                ins.then_inc(s("d_y"), 1)

            need(pe, "we")
            for half in range(2):
                turn(EX, half, res)
                pe.wait_ge(s("xT_ready"), nth(EX, half))
                mm(ps[:, 2 * half, :], we[:, 0, :], xT[:, tok(half)], start=True, stop=True).then_inc(
                    s("e_q_ps"), 1)
                for t in range(HT):
                    ins = mm(ps[:, 2 * half + 1, 128 * t:128 * t + 128],
                             xT[:, S * half + 128 * t:S * half + 128 * t + 128], we[:, 0, :],
                             start=True, stop=True)
                ins.then_inc(s("e_qt_ps"), 1)
            pe.wait_ge(s("e_q"), 2)
            pe.wait_ge(s("e_qt"), 2)
            pe.wait_ge(s("e_kT"), 2)
            pe.wait_ge(s("e_vb"), len(VG))
            for i in range(NT + 2):
                if i < NT:
                    if i >= 1:
                        pe.wait_ge(s("e_exp"), i)
                    half, t = divmod(i, HT)
                    for k in range(4):
                        ins = mm(ps[:, k, 0:4 * CTX], e_q[:, half, 128 * t:128 * t + 128],
                                 e_kT[:, half, 4 * CTX * k:4 * CTX * (k + 1)], start=True, stop=True)
                    ins.then_inc(s("e_sc"), 1)
                if 1 <= i <= NT:
                    t = i - 1
                    pe.wait_ge(s("e_exp"), t + 1)
                    for r in range(3):
                        n = 3 * t + r
                        if n >= 2:
                            pe.wait_ge(s("e_pT"), n - 1)
                        for k in range(4 * r, min(4 * r + 4, EK)):
                            w = min(128, EP - 128 * k)
                            ins = nc.tensor.transpose(ps[0:w, 4 + n % 2, 128 * (k - 4 * r):128 * (k - 4 * r) + 128],
                                                      e_p[:, t % 2, 128 * k:128 * k + w], ident)
                        ins.then_inc(s("e_pT_ps"), 1)
                if 2 <= i:
                    t = i - 2
                    pe.wait_ge(s("e_o"), t + 1)
                    nc.tensor.transpose(ps[:, 6 + t % 2, 256:384], e_o[:, t % 2, :], ident).then_inc(
                        s("e_oT_ps"), 1)
                if 1 <= i <= NT:
                    t = i - 1
                    pe.wait_ge(s("e_pT"), 3 * t + 3)
                    if t >= 2:
                        pe.wait_ge(s("e_yadd"), t - 1)
                    for k in range(EK):
                        w = min(128, EP - 128 * k)
                        ins = mm(ps[:, 6 + t % 2, 0:144], e_pT[0:w, k, :], e_vb[0:w, t // HT, k, :],
                                 start=(k == 0), stop=(k == EK - 1))
                    ins.then_inc(s("e_pv"), 1)
                if 2 <= i:
                    t = i - 2
                    pe.wait_ge(s("e_oT"), t + 1)
                    mm(ps[:, 6 + t % 2, 384:512], e_oT[:, t % 2, :], we[:, 1, :], start=True,
                       stop=True).then_inc(s("e_y"), 1)

            pe.wait_ge(s("e_yadd"), NT)
            turn(H, 0, res)
            logits(1, 0)

            def f_hidden(g):
                half, e = divmod(g, NE)
                if e == 0:
                    pe.wait_ge(s("x_low"), 2 + half + 1)
                for c, (f, w) in enumerate(F1C):
                    n = 3 * g + c
                    for up, free, full in ((0, "f_silu", "f_gate_ps"), (1, "f_h", "f_up_ps")):
                        if n >= 2:
                            pe.wait_ge(s(free), n - 1)
                        for i, (p, q) in enumerate(PASSES):
                            ins = mm(ps[0:w, 2 * (n % 2) + up, :], f_gu[:, p, e, F1 * up + f:F1 * up + f + w],
                                     xs[1][:, half, q, :], start=(i == 0), stop=(i == 2))
                        ins.then_inc(s(full), 1)

            def f_out(g):
                half, e = divmod(g, NE)
                pe.wait_ge(s("f_low"), 3 * (g + 1))
                if g >= 2:
                    pe.wait_ge(s("f_acc"), g - 1)
                for t in range(HT):
                    for c, (f, w) in enumerate(F1C):
                        for i, (p, q) in enumerate(PASSES):
                            ins = mm(ps[:, 4 + g % 2, 128 * t:128 * t + 128],
                                     hp[1][0:w, g % 2, p, c, 128 * t:128 * t + 128],
                                     f_dn[0:w, q, e, D * c:D * c + D],
                                     start=(c == 0 and i == 0), stop=(c == 2 and i == 2))
                ins.then_inc(s("f_y"), 1)

            pe.wait_ge(s("e_exp"), NT)
            for g in range(2 * NE + 1):
                if g < 2 * NE:
                    f_hidden(g)
                if g >= 1:
                    f_out(g - 1)
                if g == 5:
                    turn(H, 1, res)
                    logits(1, 1)


def tables():
    p = np.arange(P)
    k = np.arange(CH)
    j = p % CH
    t = {}
    t["ident"] = np.eye(P)
    t["head8"] = p[:, None] // 8 == p[None, :] // 8
    t["low_incl"] = j[:, None] <= k[None, :]
    t["blk_neg"] = -1.0 * (p[:, None] // CH == p[None, :] // CH)
    t["head4"] = p[:, None] // GK == np.arange(GH)[None, :]
    t["ehead"] = p[:, None] // 8 == np.arange(EH)[None, :]
    t["iota"] = np.broadcast_to(np.arange(E), (P, E))
    r = np.arange(EK * P)
    h = np.concatenate([np.arange(P) // 8, np.arange(EH)])
    vm = (r[:, None] // CTX == h[None, :]) & (r[:, None] < EP)
    t["vmask"] = vm.reshape(EK, P, 144).transpose(1, 0, 2).reshape(P, EK * 144)
    tabs = np.concatenate([np.asarray(t[n], np.float32) for n, _ in TABS], 1)
    spread = (np.arange(CTX)[:, None] == r[None, :] % CTX) & (r[None, :] < EP)
    return tabs, spread.astype(np.float32)


def kernel(**inputs):
    import concourse.bacc as bacc
    from concourse.bass_utils import run_bass_kernel_spmd as run

    i = {k: np.asarray(v) for k, v in inputs.items()}
    tabs, spread = tables()
    cat = np.concatenate
    a = {
        "x": i["x"].reshape(B * S, D),
        "tabs": tabs, "spread": spread,
        "cols": np.stack([i[n] for n in ("L0_attn_ln_g", "L0_attn_ln_b", "L0_attn_bq", "L0_attn_bk",
                                         "L0_attn_bv", "L0_xattn_ln_gamma", "L0_xattn_ln_beta",
                                         "L1_attn_ln_w", "L1_attn_ln_b", "L1_xattn_bq")]
                         + [cat([i["L1_attn_o_norm_w"]] * (P // GV))], 1),
        "rows": cat([i["L0_attn_bo"], i["L0_xattn_bo"], i["L0_ffn_shared_b2"], i["L1_xattn_bq"],
                     i["L1_xattn_bk"], i["L1_xattn_bv"], i["L1_xattn_bo"], i["L1_xattn_ln_gamma"],
                     i["L1_xattn_ln_beta"], i["L0_ffn_router_b"]]),
        "ctxT": i["ctx_768"].reshape(B * CTX, CD).T,
        "mask": i["mask_1x1xSxS2_bk0"].reshape(S, CTX),
        "wa": np.stack([i["L0_attn_W" + w] for w in "qkvo"], 1),
        "wxq": i["L0_xattn_Wq"],
        "wxkv": i["L0_xattn_Wkv"],
        "wxo": i["L0_xattn_Wo"].reshape(8, P, D).transpose(1, 0, 2),
        "router": np.stack([i["L0_ffn_router_w"].T, i["L1_ffn_gate_w"].T], 1),
        "w1": cat([i["L0_ffn_shared_w1"][None], i["L0_ffn_spec_w1"]]).transpose(2, 0, 1),
        "w2": cat([i["L0_ffn_shared_w2"][None], i["L0_ffn_spec_w2"]]).reshape(NE, D, C0, P).transpose(3, 0, 2, 1)
        .reshape(P, NE, F0),
        "fb1": cat([i["L0_ffn_shared_b1"][None], i["L0_ffn_spec_b1"]]).reshape(NE, C0, P).transpose(2, 0, 1),
        "fb2": i["L0_ffn_spec_b2"],
        "wd": cat([i["L1_attn_W" + w] for w in "qkvb"], 1),
        "wdo": i["L1_attn_Wo"].reshape(2, P, D).transpose(1, 0, 2),
        "we": np.stack([i["L1_xattn_Wq"], i["L1_xattn_Wo"]], 1),
        "wekv": cat([i["L1_xattn_Wk"], i["L1_xattn_Wv"]], 1),
        "f_gu": np.stack([cat([i["L1_ffn_shared_gate"][None], i["L1_ffn_expert_gate"]]),
                          cat([i["L1_ffn_shared_up"][None], i["L1_ffn_expert_up"]])], 1).transpose(3, 0, 1, 2).reshape(P, NE, 2 * F1),
    }
    dn = cat([i["L1_ffn_shared_down"][None], i["L1_ffn_expert_down"]]).transpose(2, 0, 1)
    pad = np.zeros((3 * P - F1, NE, D), dn.dtype)
    a["f_dn"] = cat([dn, pad]).reshape(3, P, NE, D).transpose(1, 2, 0, 3).reshape(P, NE, 3 * D)

    nc = bacc.Bacc("TRN2", target_bir_lowering=False, num_devices=1)
    arrays, args = {}, {}
    for name, v in a.items():
        v = np.ascontiguousarray(v)
        arrays["in_" + name] = v
        args[name] = nc.dram_tensor("in_" + name, v.shape, mybir.dt.from_np(v.dtype), kind="ExternalInput").ap()
    args["out"] = nc.dram_tensor("out_x", (B * S, D), FP, kind="ExternalOutput").ap()
    program(nc, args)
    r = run(nc, [arrays], core_ids=[0])
    return r.results[0]["out_x"].reshape(B, S, D)
```

```python
import numpy as np
import concourse.bass as bass
from concourse import mybir
from contextlib import ExitStack

FP = mybir.dt.float32
U32 = mybir.dt.uint32
I32 = mybir.dt.int32
U8 = mybir.dt.uint8
F16 = mybir.dt.float16
ALU = mybir.AluOpType
ACT = mybir.ActivationFunctionType
AX = mybir.AxisListType

P = 128
B, S, D = 2, 512, 128
HT = S // P
NT = B * HT
CTX, CD = 77, 96
XH, XD = 16, 64
XI = XH * XD
E = 8
NE = E + 1
F0 = 512
C0 = F0 // P
F1 = 352
F1C = [(0, 128), (128, 128), (256, 96)]
GH, GK, GV = 4, 32, 64
CH = 32
NC = S // CH
NM = HT * GH
EH = 16
EP = EH * CTX
EK = (EP + P - 1) // P
ARENA = 17600
XS, WS, HS = 2.0 ** 10, 2.0 ** 6, 2.0 ** 4
PASSES = ((0, 0), (0, 1), (1, 0))
WG = 3
MAGIC = float(0x5F3759DF)

COLS = ["a_g", "a_b", "a_bq", "a_bk", "a_bv", "x_g", "x_b", "d_g", "d_b", "e_bq", "d_on"]
ROWS = [("a_bo", 128), ("x_bo", 128), ("f_b2", 128), ("e_bq", 128), ("e_bk", 128), ("e_bv", 128),
        ("e_bo", 128), ("e_g", 128), ("e_b", 128), ("f_rb", 8)]
ROFF = {}
_o = 0
for _n, _w in ROWS:
    ROFF[_n] = (_o, _w)
    _o += _w
RTOT = _o
TABS = [("ident", 128), ("head8", 128), ("low_incl", 32),
        ("blk_neg", 128), ("head4", GH), ("ehead", EH), ("iota", 8), ("vmask", EK * 144)]
TOFF = {}
_o = 0
for _n, _w in TABS:
    TOFF[_n] = (_o, _w)
    _o += _w
TTOT = _o


def program(nc, a):
    ctx = ExitStack()
    with ctx:
        def sb(name, shape, dt=FP):
            return ctx.enter_context(nc.sbuf_tensor(name, shape, dt))

        def sem(name):
            return ctx.enter_context(nc.semaphore(name))

        ps = ctx.enter_context(nc.psum_tensor("ps", [P, 8, 512], FP))

        tabs = sb("tabs", [P, TTOT])
        cols = sb("cols", [P, len(COLS)])
        rows = sb("rows", [P, RTOT])
        spread = sb("spread", [CTX, EK * P])
        ctxT = sb("ctxT", [CD, B * CTX])
        mask_u8 = sb("mask_u8", [P, HT, CTX], U8)
        mask_f = sb("mask_f", [P, HT, CTX])
        wa = sb("wa", [P, 4, 128])
        wx = sb("wx", [P, 4 * XI])
        wxq, wxkv = wx[:, 0:XI], wx[0:CD, XI:3 * XI]
        wxo = wx[:, 3 * XI:4 * XI].rearrange("p (c d) -> p c d", c=8)
        w1f = sb("w1f", [P, NE * F0])
        w2f = sb("w2f", [P, NE * F0])
        w1 = w1f[:, :].bitcast(F16).rearrange("p (s e f) -> p s e f", s=2, e=NE)
        w2 = w2f[:, :].bitcast(F16).rearrange("p (s e f) -> p s e f", s=2, e=NE)
        fb1 = sb("fb1", [P, NE, C0])
        fb2 = sb("fb2", [E, 128])
        router = sb("router", [P, 2, E])
        wd = sb("wd", [P, 516])
        wdo = sb("wdo", [P, 2, 128])
        we = sb("we", [P, 2, 128])
        wekv = sb("wekv", [CD, 256])

        def tab(n):
            return tabs[:, TOFF[n][0]:TOFF[n][0] + TOFF[n][1]]

        def row(n):
            return rows[:, ROFF[n][0]:ROFF[n][0] + ROFF[n][1]]

        def col(n):
            return cols[:, COLS.index(n):COLS.index(n) + 1]

        ident = tab("ident")

        z = sb("z", [P, NT, D])
        xT = sb("xT", [P, B * S])
        res = sb("res", [P, NT, D])
        pre = sb("pre", [P, NT, D])
        bn6 = sb("bn6", [P, NT, 6])
        bn2 = sb("bn2", [P, NT, 2])
        rt = sb("rt", [P, 3, 64])
        arena = sb("arena", [P, ARENA])
        hid = sb("hid", [P, 2, 4, 512])
        sm = sb("sm", [P, 512])
        idx = sb("idx", [P, HT, 8], U32)
        comb = sb("comb", [P, NT, E])
        wscale = sb("wscale", [P, 1])
        combT = sb("combT", [E, 2, 512])

        class Carve:
            def __init__(self):
                self.at = 0

            def __call__(self, *dims):
                n = int(np.prod(dims))
                v = arena[:, self.at:self.at + n]
                self.at += n
                assert self.at <= ARENA, self.at
                names = " ".join(f"d{i}" for i in range(len(dims)))
                if len(dims) > 1:
                    v = v.rearrange(f"p ({names}) -> p {names}", **{f"d{i}": d for i, d in enumerate(dims) if i})
                return v

        cut = Carve()
        a_qkv = cut(3, B * S)
        a_kd, a_vd, a_vs = cut(S), cut(S), cut(S)
        a_prod, a_th, a_o = cut(B * S), cut(B * S), cut(B * S)
        cut = Carve()
        b_q = cut(8, 512)
        b_s = cut(3, XH * CTX)
        assert cut.at >= 3 * B * S + 3 * S + 3 * B * S
        b_kT = cut(8, B, 2, CTX)
        b_v = cut(B, XI)
        b_pT = cut(16, 128)
        b_oT = cut(2, XI).bitcast(F16).rearrange("p a (s c n) -> p a s c n", s=2, c=8)
        b_wo = cut(XI).bitcast(F16).rearrange("p (s c d) -> p s c d", s=2, c=8)
        cut = Carve()
        d_qk = cut(2, HT, 8, GK)
        d_r = cut(2, HT, GH, GV + GK)
        d_u = cut(2, HT, GH, GV)
        d_w = cut(2, HT, GH * GK)
        d_S = cut(NC, 2, GV)
        d_P = cut(2 * NM, CH)
        pbd = cut(2 * NM, 128)
        sbd = cut(2, 2, GH * GV)
        d_o = d_r.rearrange("p b t h w -> p (b t h w)")[:, 0:2 * HT * GH * GV].rearrange(
            "p (b t h w) -> p b t h w", b=2, t=HT, h=GH)
        d_sq = d_u
        inv_a = sb("inv_a", [P, CH * CH])
        inv_x = sb("inv_x", [P, CH * CH])
        inv_t = sb("inv_t", [P, 256])
        mbd = w1f[:, 0:2 * NM * 128].rearrange("p (m j) -> p m j", j=128)
        ybd = w2f[:, 0:2 * NM * 128].rearrange("p (m j) -> p m j", j=128)
        d_T = wx[:, 0:3072].rearrange("p (b w n) -> p b w n", b=2, w=3)
        d_wT = wx[:, 3072:4096].rearrange("p (b n) -> p b n", b=2)
        e_kv = sb("e_kv", [CTX, B, 272])
        e_k1 = xT[:, 0:B * CTX].rearrange("p (b k) -> p b k", b=B)
        flat = hid[:, :, :, :].rearrange("p a c n -> p (a c n)")
        e_sq = flat[0:CTX, 0:B * 128].rearrange("p (b n) -> p b n", b=B)
        e_kT = flat[:, 0:B * EP].rearrange("p (b n) -> p b n", b=B)
        e_p = w1f[:, 0:2 * EP].rearrange("p (a n) -> p a n", a=2)
        e_q = w1f[:, B * EP:B * EP + 1024].rearrange("p (b n) -> p b n", b=B)
        e_o = w1f[:, B * EP + 1024:B * EP + 1280].rearrange("p (b n) -> p b n", b=2)
        e_oT = w1f[:, B * EP + 1280:B * EP + 1536].rearrange("p (b n) -> p b n", b=2)
        e_vb = w2f[:, 0:B * EK * 144].rearrange("p (b k n) -> p b k n", b=B, k=EK)
        e_pT = [v.rearrange("p (k n) -> p k n", k=EK)
                for v in (w2f[:, B * EK * 144:B * EK * 144 + EK * 128],
                          arena[:, ARENA - EK * 128:ARENA])]
        VB = -(-EK // 3)
        VG = [(b, k, min(k + 3, EK)) for b in range(B) for k in range(0, EK, 3)]
        FD = NE * 2 * F1
        FW = FD + NE * 3 * D
        f_gu = arena[:, 0:FD].bitcast(F16).rearrange("p (s e f) -> p s e f", s=2, e=NE)
        f_dn = arena[:, FD:FW].bitcast(F16).rearrange("p (s e f) -> p s e f", s=2, e=NE)
        assert FW + 3 * WG * 2 * F1 <= ARENA - EK * 128
        xs, hp = [], []
        for at0 in (0, FW):
            n = at0 + B * S
            xs.append(arena[:, at0:n].bitcast(F16).rearrange("p (b s n) -> p b s n", b=B, s=2))
            hp.append(arena[:, n:n + 4096 if not at0 else n + 3072].bitcast(F16).rearrange(
                "p (a s c n) -> p a s c n", a=2, s=2, n=512))
        SPLITS = []
        for name, dst, w in (("w1", w1, F0), ("w2", w2, F0), ("f_gu", f_gu, 2 * F1), ("f_dn", f_dn, 3 * D)):
            for k in range(0, NE, WG):
                n = len(SPLITS)
                if name in ("w1", "w2"):
                    stage = hid[:, n % 2, :, :].rearrange("p c n -> p (c n)")[:, 0:WG * w]
                else:
                    o = FW + (n - 6) % 3 * WG * 2 * F1
                    stage = arena[:, o:o + WG * w]
                SPLITS.append((a[name][:, k:k + WG, :], stage.rearrange("p (e f) -> p e f", e=WG),
                               dst[:, :, k:k + WG, :]))

        sems = {}

        def s(name):
            if name not in sems:
                sems[name] = sem(name)
            return sems[name]

        LOADS = [("x", res[:, :, :], a["x"].rearrange("(t p) d -> p t d", p=P)),
                 ("tabs", tabs[:, :], a["tabs"]),
                 ("cols", cols[:, :], a["cols"]),
                 ("wa", wa[:, :, :], a["wa"]),
                 ("rows", rows[:, :], a["rows"].partition_broadcast(P)),
                 ("ctxT", ctxT[:, :], a["ctxT"]),
                 ("wxkv", wxkv, a["wxkv"]),
                 ("wxq", wxq, a["wxq"]),
                 ("mask", mask_u8[:, :, :], a["mask"].rearrange("(t p) k -> p t k", p=P)),
                 ("wxo", wxo, a["wxo"]),
                 ("router", router[:, :, :], a["router"]),
                 ("fb2", fb2[:, :], a["fb2"]),
                 ("fb1", fb1[:, :, :], a["fb1"]),
                 ("wd", wd[:, :], a["wd"]),
                 ("wdo", wdo[:, :, :], a["wdo"]),
                 ("we", we[:, :, :], a["we"]),
                 ("wekv", wekv[:, :], a["wekv"]),
                 ("spread", spread[:, :], a["spread"])]

        def need(eng, *names):
            for n in names:
                eng.wait_ge(s("in_" + n), 16)

        A, X, F, G, EX, H = range(6)

        def turn_bank(use, half):
            return (3, 5)[half] if use == EX else 6 + half

        FB = (0, 2, 6)
        EQ = (0, 6)
        EQT = (1, 7)

        def nth(use, half):
            return 2 * use + half + 1

        def tok(half):
            return slice(half * S, half * S + S)

        def til(half):
            return slice(half * HT, half * HT + HT)

        NI = NT + 3
        RING = []
        for i in range(NI):
            if i in (0, HT):
                RING += [("q", i // HT, r) for r in range(8)]
            if 2 <= i < NT + 2:
                RING += [("pT", i - 2, r) for r in range(4)]
            if 3 <= i:
                RING += [("y", i - 3, 0)]
        RAT = {e: n for n, e in enumerate(RING)}

        def ring(n):
            return 3 + n % 3

        def ringed(kind, i, r):
            return 1 + sum(e[0] != "y" for e in RING[:RAT[(kind, i, r)]])

        def ring_free(eng, n):
            if n >= 3:
                kind, i, r = RING[n - 3]
                if kind == "y":
                    eng.wait_ge(s("b_yadd"), i + 1)
                else:
                    eng.wait_ge(s("b_ringed"), ringed(kind, i, r))

        rs = [sm[:, 48:64], sm[:, 448:464], sm[:, 464:480]]

        def r_l(half):
            return sm[:, 64 + 32 * half:96 + 32 * half].rearrange("p (t e) -> p t e", e=E)

        def r_e(half):
            return sm[:, 160 + 32 * half:192 + 32 * half].rearrange("p (t e) -> p t e", e=E)

        block = ctx.enter_context(nc.Block())

        @block.sync
        def _(sp):
            for name, dst, src in LOADS:
                sp.dma_start(dst, src).then_inc(s("in_" + name), 16)
            for n, (src, stage, _) in enumerate(SPLITS):
                if n in (2, 3, 4, 5, 9, 10, 11):
                    sp.wait_ge(s("w_split"), n - 1 if n < 6 else n - 2)
                if n == 6:
                    sp.wait_ge(s("z_ready"), nth(EX, 1))
                sp.dma_start(stage, src).then_inc(s("in_split%d" % n), 16)
            for half in range(2):
                sp.wait_ge(s("out_ready"), half + 1)
                sp.dma_start(a["out"].rearrange("(t p) d -> p t d", p=P)[:, til(half), :],
                             res[:, til(half), :]).then_inc(s("stored"), 16)
            sp.wait_ge(s("stored"), 32)

        @block.gpsimd
        def _(pool):
            nc.gpsimd.memset(wscale[:, :], WS).then_inc(s("w_scale"), 1)
            nc.gpsimd.memset(b_kT, 0.0).then_inc(s("b_zero"), 1)
            pool.wait_ge(s("w_scale"), 1)

            highs = [0]

            def split_up(stage, high, low, done):
                scale = wscale[:, 0:1].unsqueeze(1).to_broadcast(list(stage.shape))
                nc.gpsimd.tensor_tensor(high, stage, scale, ALU.mult)
                highs[0] += 1
                nc.gpsimd.tensor_tensor(stage, stage, scale, ALU.mult).then_inc(s("w_high"), 1)
                pool.wait_ge(s("w_high"), highs[0])
                nc.gpsimd.tensor_tensor(low, stage, high, ALU.subtract).then_inc(s(done), 1)

            def split(n):
                _, stage, dst = SPLITS[n]
                pool.wait_ge(s("in_split%d" % n), 16)
                split_up(stage, dst[:, 0], dst[:, 1], "w_split")

            need(pool, "wxo")
            split_up(wxo, b_wo[:, 0], b_wo[:, 1], "b_wo")
            for n in range(4):
                split(n)
            def weigh(t):
                pool.wait_ge(s("b_rs"), t + 1)
                sc = b_s[:, t % 3, :].rearrange("p (h k) -> p h k", k=CTX)
                nc.gpsimd.tensor_tensor(sc, sc, rs[t % 3].unsqueeze(2).to_broadcast([P, XH, CTX]),
                                        ALU.mult).then_inc(s("b_prob"), 1)

            for t in range(NT):
                pool.wait_ge(s("b_max"), t + 1)
                nc.gpsimd.tensor_tensor(
                    b_s[:, t % 3, :].rearrange("p (h k) -> p h k", k=CTX),
                    b_s[:, t % 3, :].rearrange("p (h k) -> p h k", k=CTX),
                    sm[:, 16 * (t % 3):16 * (t % 3) + 16].unsqueeze(2).to_broadcast([P, 16, CTX]),
                    ALU.subtract).then_inc(s("b_sub"), 1)
                if t >= 1:
                    weigh(t - 1)
                if t in (2, 4):
                    split(3 + t // 2)
            weigh(NT - 1)
            pool.wait_ge(s("c_acc"), 2 * NE)
            nc.gpsimd.memset(inv_x[:, :], 0.0).then_inc(s("d_zero"), 1)
            pool.wait_ge(s("d_zero"), 1)
            nc.gpsimd.memset(inv_x[:, 0:CH * CH:CH + 1], 1.0).then_inc(s("d_zero"), 1)
            nc.gpsimd.memset(w2f[:, 0:2 * NM * 128], 0.0)
            nc.gpsimd.memset(pbd, 0.0)
            nc.gpsimd.memset(d_S[:, 0, :, :], 0.0).then_inc(s("d_zero"), 1)
            for half in range(2):
                pool.wait_ge(s("d_norm"), half + 1)
                b4 = sm[:, 128 + 16 * half:144 + 16 * half].rearrange("p (t h) -> p t h", t=HT).unsqueeze(3)
                nc.gpsimd.tensor_tensor(d_r[:, half, :, :, 0:GV],
                                        hid[:, half, :, 256:512].rearrange("p t (h w) -> p t h w", w=GV),
                                        b4.to_broadcast([P, HT, GH, GV]), ALU.mult)
                nc.gpsimd.tensor_tensor(d_r[:, half, :, :, GV:96], d_qk[:, half, :, 4:8, :],
                                        b4.to_broadcast([P, HT, GH, GK]), ALU.mult).then_inc(s("d_r"), 1)
            need(pool, "wdo", "cols")
            nc.gpsimd.tensor_tensor(wdo[:, :, :], wdo[:, :, :],
                                    col("d_on").unsqueeze(1).to_broadcast([P, 2, 128]), ALU.mult).then_inc(
                s("d_wdo"), 1)
            pool.wait_ge(s("d_wdo"), 1)
            pool.wait_ge(s("d_zero"), 3)
            pool.wait_ge(s("d_pt"), 1)
            for c in range(4):
                q = slice(CH * c, CH * c + CH)
                ins = nc.gpsimd.tensor_tensor(pbd[q, :, q], d_P[q, :, :],
                                              tab("low_incl")[q, :].unsqueeze(1).to_broadcast([CH, 2 * NM, CH]),
                                              ALU.mult)
            ins.then_inc(s("d_pbd"), 1)
            pool.wait_ge(s("e_k1"), 1)
            pool.wait_ge(s("d_ybd"), 1)
            pool.wait_ge(s("d_pbd"), 1)
            for b in range(B):
                nc.gpsimd.tensor_tensor(e_kT[:, b, :].rearrange("p (h k) -> p h k", k=CTX),
                                        e_k1[:, b, :].unsqueeze(1).to_broadcast([P, EH, CTX]),
                                        tab("ehead").unsqueeze(2).to_broadcast([P, EH, CTX]),
                                        ALU.mult).then_inc(s("e_kT"), 1)
            for n in range(NC):
                if n >= 1:
                    pool.wait_ge(s("d_state"), n)
                if n >= 2:
                    pool.wait_ge(s("d_against"), n - 1)
                nc.gpsimd.tensor_tensor(sbd[:, n % 2, :, :].rearrange("p b (h w) -> p b h w", h=GH),
                                        d_S[:, n, :, :].unsqueeze(2).to_broadcast([P, 2, GH, GV]),
                                        tab("head4").unsqueeze(1).unsqueeze(3).to_broadcast([P, 2, GH, GV]),
                                        ALU.mult).then_inc(s("d_diag"), 1)
            vm = tab("vmask").rearrange("p (k n) -> p k n", k=EK)
            for n, (b, k0, k1) in enumerate(VG):
                pool.wait_ge(s("e_spread"), n + 1)
                nc.gpsimd.tensor_tensor(e_vb[:, b, k0:k1, :], e_vb[:, b, k0:k1, :], vm[:, k0:k1, :],
                                        ALU.mult).then_inc(s("e_vb"), 1)
            for n in range(6, 12):
                split(n)
            for n in range(6 * NE):
                g, c = divmod(n, 3)
                w = F1C[c][1]
                pool.wait_ge(s("f_high"), n + 1)
                nc.gpsimd.tensor_tensor(hp[1][0:w, g % 2, 1, c, :], hid[0:w, g % 2, c, :],
                                        hp[1][0:w, g % 2, 0, c, :], ALU.subtract).then_inc(s("f_low"), 1)

        @block.scalar
        def _(act):
            def turn(use, half, g=None, b=None):
                act.wait_ge(s("turned"), nth(use, half))
                kw = dict(scale=col(g), bias=col(b)) if g else {}
                nc.scalar.activation(xT[:, tok(half)], ps[:, turn_bank(use, half), :], ACT.Identity, **kw).then_inc(
                    s("xT_ready"), 1)

            need(act, "cols")
            for half in range(2):
                turn(A, half, "a_g", "a_b")
                for j, bias in enumerate(("a_bq", "a_bk", "a_bv")):
                    act.wait_ge(s("a_qkv_ps"), 3 * half + j + 1)
                    nc.scalar.activation(a_qkv[:, j, tok(half)], ps[:, 3 * half + j, :], ACT.Identity,
                                         bias=col(bias)).then_inc(s("a_qkv"), 1)
            for half in range(2):
                act.wait_ge(s("a_gap"), half + 1)
                nc.scalar.activation(a_th[:, tok(half)], ps[:, 3 * half, :], ACT.Tanh,
                                     scale=0.5 * 8.0 ** -0.5).then_inc(s("a_th"), 1)
            act.wait_ge(s("b_zero"), 1)
            for g in range(7):
                act.wait_ge(s("b_kv_ps"), g + 1)
                if g < 3:
                    w = min(3, 8 - 3 * g)
                    for k in range(2):
                        q = slice(XD * k, XD * k + XD)
                        ins = nc.scalar.activation(
                            b_kT[q, 3 * g:3 * g + w, :, k, :],
                            ps[q, 6 + g % 2, 0:w * B * CTX].rearrange("p (c b n) -> p c b n", c=w, b=B),
                            ACT.Copy)
                else:
                    b, n = divmod(g - 3, 2)
                    ins = nc.scalar.activation(b_v[0:CTX, b, 512 * n:512 * n + 512],
                                               ps[0:CTX, 6 + g % 2, :], ACT.Copy)
                ins.then_inc(s("b_kv"), 1)
            def b_exp(t):
                act.wait_ge(s("b_sub"), t + 1)
                nc.scalar.activation(b_s[:, t % 3, :], b_s[:, t % 3, :], ACT.Exp).then_inc(s("b_exp"), 1)

            turn(X, 0, "x_g", "x_b")
            for i in range(NI):
                if i == 1:
                    turn(X, 1, "x_g", "x_b")
                if i in (0, HT):
                    for r in range(8):
                        act.wait_ge(s("b_ring"), RAT[("q", i // HT, r)] + 1)
                        nc.scalar.activation(b_q[:, r, :], ps[:, ring(RAT[("q", i // HT, r)]), :], ACT.Copy,
                                             scale=XD ** -0.5).then_inc(s("b_ringed"), 1)
                if i == HT:
                    b_exp(HT - 1)
                if 2 <= i < NT + 2:
                    for r in range(4):
                        n = RAT[("pT", i - 2, r)]
                        act.wait_ge(s("b_ring"), n + 1)
                        nc.scalar.activation(
                            b_pT[0:CTX, 4 * r:4 * r + 4, :],
                            ps[0:CTX, ring(n), :].rearrange("p (j n) -> p j n", j=4),
                            ACT.Copy).then_inc(s("b_ringed"), 1)
                if i < NT and i != HT - 1:
                    b_exp(i)
                if 2 <= i < NT + 2:
                    t = i - 2
                    act.wait_ge(s("b_pv"), t + 1)
                    if t >= 2:
                        act.wait_ge(s("b_yadd"), t - 1)
                    nc.scalar.activation(b_oT[:, t % 2, 0], ps[:, 6:8, :].rearrange("p b (c n) -> p (b c) n", n=128),
                                         ACT.Copy, scale=HS).then_inc(s("b_high"), 1)
            def split_x(which, half):
                use = (F, H)[which]
                turn(use, half)
                act.wait_ge(s("xT_ready"), nth(use, half))
                if which:
                    act.wait_ge(s("w_split"), 12)
                nc.scalar.activation(xs[which][:, half, 0, :], xT[:, tok(half)], ACT.Copy, scale=XS).then_inc(
                    s("x_high"), 1)

            def r_exp(which, half):
                act.wait_ge(s("r_shift"), 2 * which + half + 1)
                nc.scalar.activation(r_e(half), r_e(half), ACT.Exp).then_inc(s("r_exp"), 1)

            split_x(0, 0)
            r_exp(0, 0)
            for half in range(2):
                for e in range(NE):
                    g = NE * half + e
                    if g == 0:
                        need(act, "fb1")
                        act.wait_ge(s("w_split"), 6)
                    if g >= 2:
                        act.wait_ge(s("c_y"), g - 1)
                    for c in range(C0 + 1):
                        if c < C0:
                            if g >= 2:
                                act.wait_ge(s("c_low"), C0 * (g - 2) + c + 1)
                            act.wait_ge(s("c_h_ps"), C0 * g + c + 1)
                            nc.scalar.activation(hid[:, g % 2, c, :], ps[:, c, :], ACT.Gelu_apprx_tanh,
                                                 bias=fb1[:, e, c:c + 1], scale=1.0 / (XS * WS)).then_inc(
                                s("c_h"), 1)
                        if c >= 1:
                            act.wait_ge(s("c_h"), C0 * g + c)
                            nc.scalar.activation(hp[0][:, g % 2, 0, c - 1, :], hid[:, g % 2, c - 1, :], ACT.Copy,
                                                 scale=HS).then_inc(s("c_high"), 1)
                    if g == 3:
                        split_x(0, 1)
                        r_exp(0, 1)
                    if g == 2 * NE - 3:
                        turn(G, 0, "d_g", "d_b")
                    if e == 1:
                        act.wait_ge(s("c_combT_ps"), half + 1)
                        nc.scalar.activation(combT[:, half, :], ps[0:E, 6 + half, :], ACT.Copy,
                                             scale=WS * HS).then_inc(s("c_combT"), 1)
            for half in range(2):
                if half == 1:
                    turn(G, 1, "d_g", "d_b")
                act.wait_ge(s("c_low"), C0 * (2 * NE - 1 + half))
                for t in range(HT):
                    act.wait_ge(s("d_qkv"), HT * half + t + 1)
                    nc.scalar.activation(hid[:, half, t, :], ps[:, 4 * half + t, :], ACT.Silu).then_inc(
                        s("d_silu"), 1)
                act.wait_ge(s("d_silu"), HT * half + HT)
                nc.scalar.activation(d_sq[:, half, :, :, :].rearrange("p t h w -> p t (h w)"),
                                     hid[:, half, :, 0:256], ACT.Square).then_inc(s("d_qksq"), 1)
                act.wait_ge(s("d_beta_ps"), half + 1)
                nc.scalar.activation(sm[:, 128 + 16 * half:144 + 16 * half], ps[:, 4 * half, 0:16], ACT.Tanh,
                                     scale=0.5).then_inc(s("d_tanh"), 1)
            act.wait_ge(s("e_kv_ps"), 1)
            nc.scalar.activation(e_kv[:, :, 0:256], ps[0:CTX, 3, :].rearrange("p (b n) -> p b n", b=B),
                                 ACT.Copy).then_inc(s("e_kv"), 1)
            for half in range(2):
                for w in range(3):
                    act.wait_ge(s("d_turn_ps"), 3 * half + w + 1)
                    nc.scalar.activation(d_T[:, half, w, :], ps[:, 4 * half + w, :], ACT.Copy).then_inc(
                        s("d_turn"), 1)
            act.wait_ge(s("d_ab"), 1)
            nc.scalar.activation(d_P.rearrange("p (b t) i -> p b t i", b=8),
                                 ps[:, :, 0:256].rearrange("p b (t w i) -> p b t w i", t=HT, w=2)[:, :, :, 1, :],
                                 ACT.Copy).then_inc(s("d_pt"), 1)
            act.wait_ge(s("e_kT_ps"), 1)
            nc.scalar.activation(e_k1, ps[:, 0, 0:B * CTX].rearrange("p (b k) -> p b k", b=B),
                                 ACT.Copy).then_inc(s("e_k1"), 1)
            for half in range(2):
                act.wait_ge(s("d_uw_ps"), half + 1)
                uw = ps[:, 4 * half:4 * half + 4, 0:384].rearrange("p t (h w) -> p t h w", h=GH)
                for t in range(HT):
                    nc.scalar.activation(d_u[:, half, t, :, :], uw[:, t, :, 0:GV], ACT.Copy)
                    ins = nc.scalar.activation(d_w[:, half, t, :].rearrange("p (h k) -> p h k", h=GH),
                                               uw[:, t, :, GV:96], ACT.Copy)
                ins.then_inc(s("d_uw"), 1)
            for n, half in enumerate((1, 0)):
                act.wait_ge(s("d_wT_ps"), n + 1)
                nc.scalar.activation(d_wT[:, half, :], ps[:, 4 * half, :], ACT.Copy).then_inc(s("d_wT"), 1)
            for t in range(HT):
                act.wait_ge(s("d_o_ps"), t + 1)
                o = ps[:, 6 + t % 2, :].rearrange("p (b n) -> p b n", b=2)
                nc.scalar.activation(d_o[:, :, t, :, :].rearrange("p b h w -> p b (h w)"), o, ACT.Copy)
                nc.scalar.activation(d_sq[:, :, t, :, :].rearrange("p b h w -> p b (h w)"), o,
                                     ACT.Square).then_inc(s("d_sq"), 1)
            def e_spread(b):
                for n in range(VB * b, VB * b + VB):
                    _, k0, k1 = VG[n]
                    act.wait_ge(s("e_vb_ps"), n + 1)
                    nc.scalar.activation(e_vb[:, b, k0:k1, :],
                                         ps[:, 4 + n % 2, 0:144 * (k1 - k0)].rearrange("p (k n) -> p k n", n=144),
                                         ACT.Copy).then_inc(s("e_spread"), 1)

            e_spread(0)
            for half in range(2):
                for w in range(2):
                    act.wait_ge(s("d_oT_ps"), 2 * half + w + 1)
                    nc.scalar.activation(d_T[:, half, w, :], ps[:, 4 * half + w, :], ACT.Copy).then_inc(
                        s("d_oT"), 1)
            act.wait_ge(s("e_kT"), 2)
            for half in range(2):
                turn(EX, half)
                act.wait_ge(s("e_q_ps"), half + 1)
                nc.scalar.activation(e_q[:, half, :], ps[:, EQ[half], :], ACT.Identity,
                                     bias=col("e_bq")).then_inc(s("e_q"), 1)
            for i in range(NT + 3):
                if i < NT:
                    act.wait_ge(s("e_sc"), i + 1)
                    act.wait_ge(s("e_scale"), i // HT + 1)
                    nc.scalar.activation(e_p[:, i % 2, :].rearrange("p (i k) -> p i k", i=4),
                                         ps[:, 0:4, 0:4 * CTX], ACT.Exp,
                                         scale=sm[:, 256 + i:257 + i]).then_inc(s("e_exp"), 1)
                if i == 0:
                    e_spread(1)
                if 3 <= i:
                    t = i - 3
                    act.wait_ge(s("e_oT_ps"), t + 1)
                    nc.scalar.activation(e_oT[:, t % 2, :], ps[:, 6 + t % 2, 256:384], ACT.Copy).then_inc(
                        s("e_oT"), 1)
                if 1 <= i <= NT:
                    t = i - 1
                    if t >= 2:
                        act.wait_ge(s("e_pv"), t - 1)
                    for r in range(3):
                        n = 3 * t + r
                        act.wait_ge(s("e_pT_ps"), n + 1)
                        if r < 2:
                            ins = nc.scalar.activation(e_pT[t % 2][:, 4 * r:4 * r + 4, :],
                                                       ps[:, 4 + n % 2, :].rearrange("p (k n) -> p k n", k=4),
                                                       ACT.Copy)
                        else:
                            nc.scalar.activation(e_pT[t % 2][:, 8, :], ps[:, 4 + n % 2, 0:128], ACT.Copy)
                            ins = nc.scalar.activation(e_pT[t % 2][0:EP - 9 * 128, 9, :],
                                                       ps[0:EP - 9 * 128, 4 + n % 2, 128:256], ACT.Copy)
                        ins.then_inc(s("e_pT"), 1)
            split_x(1, 0)
            r_exp(1, 0)

            def f_high(n):
                g, c = divmod(n, 3)
                w = F1C[c][1]
                act.wait_ge(s("f_h"), n + 1)
                if g >= 2:
                    act.wait_ge(s("f_y"), g - 1)
                nc.scalar.activation(hp[1][0:w, g % 2, 0, c, :], hid[0:w, g % 2, c, :], ACT.Copy).then_inc(
                    s("f_high"), 1)

            for n in range(6 * NE):
                g, c = divmod(n, 3)
                w = F1C[c][1]
                if g >= 2:
                    act.wait_ge(s("f_low"), n - 5)
                act.wait_ge(s("f_gate_ps"), n + 1)
                nc.scalar.activation(hid[0:w, g % 2, c, :], ps[0:w, FB[c], :], ACT.Silu,
                                     scale=1.0 / (XS * WS)).then_inc(s("f_silu"), 1)
                if n >= 1:
                    f_high(n - 1)
                if n == 3 * 7 - 1:
                    split_x(1, 1)
                    r_exp(1, 1)
            f_high(6 * NE - 1)

        @block.vector
        def _(dve):
            done = [0]

            def link(ins):
                done[0] += 1
                ins.then_inc(s("dve_chain"), 1)
                dve.wait_ge(s("dve_chain"), done[0])

            def bc(ap, shape):
                return ap.to_broadcast(shape)

            def inv_sqrt(v, y, w, last=False):
                link(nc.vector.tensor_scalar(w.bitcast(U32), v.bitcast(U32), 1, None,
                                             ALU.logical_shift_right))
                link(nc.vector.tensor_scalar(y.bitcast(I32), w.bitcast(I32), -1.0, MAGIC, ALU.mult, ALU.add))
                for n in range(3):
                    link(nc.vector.tensor_tensor(w, y, y, ALU.mult))
                    link(nc.vector.scalar_tensor_tensor(w, w, -0.5, v, ALU.mult, ALU.mult))
                    ins = nc.vector.scalar_tensor_tensor(y, w, 1.5, y, ALU.add, ALU.mult)
                    if last and n == 2:
                        return ins
                    link(ins)

            def norm(src, dst, half):
                link(norm_sums(src, half))
                return norm_apply(src, dst, half)

            def norm_sums(src, half):
                for t in range(HT * half, HT * half + HT):
                    ins = nc.vector.bn_stats(bn6[:, t, :], src[:, t, :])
                link(ins)
                for t in range(HT * half, HT * half + HT):
                    ins = nc.vector.bn_aggr(bn2[:, t, :], bn6[:, t, :])
                link(ins)
                v, w, y = rt[:, 0, 0:HT], rt[:, 1, 0:HT], rt[:, 2, 0:HT]
                link(nc.vector.tensor_scalar(v, bn2[:, til(half), 1], 1e-5, None, ALU.add))
                return inv_sqrt(v, y, w, last=True)

            def norm_apply(src, dst, half):
                y = rt[:, 2, 0:HT]
                for t in range(HT):
                    ins = nc.vector.tensor_scalar(dst[:, HT * half + t, :], src[:, HT * half + t, :],
                                                  bn2[:, HT * half + t, 0:1], y[:, t:t + 1],
                                                  ALU.subtract, ALU.mult)
                return ins

            def rowb(n, k):
                return row(n).unsqueeze(1).to_broadcast([P, k, ROFF[n][1]])

            def shift(which, half, extra):
                L, Ex = r_l(half), r_e(half)
                dve.wait_ge(s("r_logit"), 2 * which + half + 1)
                lp = ps[:, 6 + half, 0:HT * E].rearrange("p (t e) -> p t e", e=E)
                if extra is None:
                    link(nc.vector.tensor_copy(L, lp))
                else:
                    link(nc.vector.tensor_tensor(L, lp, rowb(extra, HT), ALU.add))
                m = sm[:, 300:304]
                link(nc.vector.tensor_reduce(m, L, AX.X, ALU.max))
                nc.vector.tensor_tensor(Ex, L, m.unsqueeze(2).to_broadcast([P, HT, E]),
                                        ALU.subtract).then_inc(s("r_shift"), 1)

            def route(which, half, eps):
                L, Ex, m = r_l(half), r_e(half), sm[:, 300:304]
                dve.wait_ge(s("r_exp"), 2 * which + half + 1)
                link(nc.vector.tensor_reduce(m, Ex, AX.X, ALU.add))
                link(nc.vector.reciprocal(sm[:, 308:312], m))
                link(nc.vector.tensor_tensor(L, Ex, sm[:, 308:312].unsqueeze(2).to_broadcast([P, HT, E]),
                                             ALU.mult))
                top = sm[:, 320:352].rearrange("p (t e) -> p t e", e=E)
                for t in range(HT):
                    ins = nc.vector.max(top[:, t, :], L[:, t, :])
                link(ins)
                for t in range(HT):
                    ins = nc.vector.max_index(idx[:, t, :], top[:, t, :], L[:, t, :])
                link(ins)
                at = sm[:, 352:384].rearrange("p (t e) -> p t e", e=E)
                link(nc.vector.tensor_copy(at, idx[:, :, :]))
                link(nc.vector.tensor_tensor(sm[:, 312:316], top[:, :, 0], top[:, :, 1], ALU.add))
                link(nc.vector.tensor_scalar(sm[:, 312:316], sm[:, 312:316], eps, WS * HS, ALU.add, ALU.mult))
                link(nc.vector.reciprocal(sm[:, 316:320], sm[:, 312:316]))
                link(nc.vector.tensor_tensor(top[:, :, 0:2], top[:, :, 0:2],
                                             sm[:, 316:320].unsqueeze(2).to_broadcast([P, HT, 2]), ALU.mult))
                iota = tab("iota").unsqueeze(1).to_broadcast([P, HT, E])
                hit = [sm[:, 384:416].rearrange("p (t e) -> p t e", e=E),
                       sm[:, 416:448].rearrange("p (t e) -> p t e", e=E)]
                for k in range(2):
                    link(nc.vector.tensor_tensor(hit[k], iota,
                                                 at[:, :, k:k + 1].to_broadcast([P, HT, E]), ALU.is_equal))
                    link(nc.vector.tensor_tensor(hit[k], hit[k],
                                                 top[:, :, k:k + 1].to_broadcast([P, HT, E]), ALU.mult))
                nc.vector.tensor_tensor(comb[:, til(half), :], hit[0], hit[1], ALU.add).then_inc(
                    s("r_comb"), 1)
                dve.wait_ge(s("r_comb"), 2 * which + half + 1)

            need(dve, "x")
            for half in range(2):
                norm(res, z, half).then_inc(s("z_ready"), 1)
            need(dve, "rows")
            for half in range(2):
                nc.vector.scalar_tensor_tensor(pre[:, til(half), :], res[:, til(half), :], 2.0,
                                               rowb("a_bo", HT), ALU.mult, ALU.add)
            need(dve, "mask")
            link(nc.vector.tensor_copy(mask_f[:, :, :], mask_u8[:, :, :]))
            link(nc.vector.tensor_scalar(mask_f[:, :, :], mask_f[:, :, :], 1.0, 1e30, ALU.subtract, ALU.mult))
            dve.wait_ge(s("a_qkv"), 6)
            link(nc.vector.tensor_tensor(a_kd, a_qkv[:, 1, tok(0)], a_qkv[:, 1, tok(1)], ALU.subtract))
            for half in range(2):
                nc.vector.tensor_tensor(a_prod[:, tok(half)], a_qkv[:, 0, tok(half)], a_kd, ALU.mult).then_inc(
                    s("a_prod"), 1)
            nc.vector.tensor_tensor(a_vd, a_qkv[:, 2, tok(0)], a_qkv[:, 2, tok(1)], ALU.subtract)
            link(nc.vector.tensor_tensor(a_vs, a_qkv[:, 2, tok(0)], a_qkv[:, 2, tok(1)], ALU.add))
            for half in range(2):
                dve.wait_ge(s("a_th"), half + 1)
                link(nc.vector.scalar_tensor_tensor(a_th[:, tok(half)], a_th[:, tok(half)], 0.5, a_vd,
                                                    ALU.mult, ALU.mult))
                nc.vector.scalar_tensor_tensor(a_o[:, tok(half)], a_vs, 0.5, a_th[:, tok(half)],
                                               ALU.mult, ALU.add).then_inc(s("a_o"), 1)

            def join(half, bank, name, n):
                dve.wait_ge(s(name), n)
                link(nc.vector.tensor_tensor(pre[:, til(half), :],
                                             ps[:, bank, :].rearrange("p (t d) -> p t d", t=HT),
                                             pre[:, til(half), :], ALU.add))

            for half in range(2):
                join(half, 3 * half + 1, "a_y", half + 1)
            for half in range(2):
                link(norm(pre, res, half))
                norm(res, z, half).then_inc(s("z_ready"), 1)
                link(nc.vector.tensor_tensor(pre[:, til(half), :], res[:, til(half), :], rowb("x_bo", HT),
                                             ALU.add))

            def low_x(which, half):
                dve.wait_ge(s("x_high"), 2 * which + half + 1)
                nc.vector.scalar_tensor_tensor(xs[which][:, half, 1, :], xT[:, tok(half)], XS,
                                               xs[which][:, half, 0, :], ALU.mult, ALU.subtract).then_inc(
                    s("x_low"), 1)

            def to_experts(half):
                norm_apply(pre, res, half).then_inc(s("z_ready"), 1)
                dve.wait_ge(s("z_ready"), nth(F, half))
                link(nc.vector.tensor_tensor(pre[:, til(half), :], res[:, til(half), :],
                                             rowb("f_b2", HT), ALU.add))

            for i in range(NI):
                if i < NT:
                    dve.wait_ge(s("b_sc"), i + 1)
                    sc = b_s[:, i % 3, :].rearrange("p (h k) -> p h k", k=CTX)
                    m3 = mask_f[:, i % HT, :].unsqueeze(1)
                    nc.vector.tensor_tensor(
                        b_s[:, i % 3, 0:12 * CTX].rearrange("p (i j k) -> p i j k", i=2, k=CTX),
                        ps[:, 0:2, 0:6 * CTX].rearrange("p i (j k) -> p i j k", k=CTX),
                        m3.unsqueeze(1).to_broadcast([P, 2, 6, CTX]), ALU.add)
                    link(nc.vector.tensor_tensor(
                        sc[:, 12:16, :], ps[:, 2, 0:4 * CTX].rearrange("p (j k) -> p j k", k=CTX),
                        m3.to_broadcast([P, 4, CTX]), ALU.add))
                    nc.vector.tensor_reduce(sm[:, 16 * (i % 3):16 * (i % 3) + 16], sc, AX.X,
                                            ALU.max).then_inc(s("b_max"), 1)
                if 1 <= i <= NT:
                    t = i - 1
                    dve.wait_ge(s("b_exp"), t + 1)
                    total = sm[:, 480 + 16 * (t % 2):496 + 16 * (t % 2)]
                    link(nc.vector.tensor_reduce(total,
                                                 b_s[:, t % 3, :].rearrange("p (h k) -> p h k", k=CTX),
                                                 AX.X, ALU.add))
                    nc.vector.reciprocal(rs[t % 3], total).then_inc(s("b_rs"), 1)
                if 3 <= i:
                    t = i - 3
                    n = RAT[("y", t, 0)]
                    dve.wait_ge(s("b_ring"), n + 1)
                    nc.vector.scalar_tensor_tensor(pre[:, t, :], ps[:, ring(n), 0:128], 1.0 / (WS * HS),
                                                   pre[:, t, :], ALU.mult, ALU.add).then_inc(s("b_yadd"), 1)
                if 2 <= i < NT + 2:
                    t = i - 2
                    dve.wait_ge(s("b_high"), t + 1)
                    nc.vector.scalar_tensor_tensor(
                        b_oT[:, t % 2, 1], ps[:, 6:8, :].rearrange("p b (c n) -> p (b c) n", n=128), HS,
                        b_oT[:, t % 2, 0], ALU.mult, ALU.subtract).then_inc(s("b_low"), 1)
                if i == HT + 3:
                    dve.wait_ge(s("b_yadd"), HT)
                    link(norm_sums(pre, 0))
                if i == HT + 4:
                    to_experts(0)
            low_x(0, 0)
            need(dve, "tabs")
            shift(0, 0, "f_rb")


            def gather(which, half, e, bank):
                for t in range(HT * half, HT * half + HT):
                    y = ps[:, bank, 128 * (t % HT):128 * (t % HT) + 128]
                    if e == 0:
                        ins = nc.vector.scalar_tensor_tensor(pre[:, t, :], y, 1.0 / (WS * HS), pre[:, t, :],
                                                             ALU.mult, ALU.add)
                    else:
                        ins = nc.vector.scalar_tensor_tensor(pre[:, t, :], y, comb[:, t, e - 1:e],
                                                             pre[:, t, :], ALU.mult, ALU.add)
                return ins

            def c_low(g):
                for c in range(C0):
                    dve.wait_ge(s("c_high"), C0 * g + c + 1)
                    nc.vector.scalar_tensor_tensor(hp[0][:, g % 2, 1, c, :], hid[:, g % 2, c, :], HS,
                                                   hp[0][:, g % 2, 0, c, :], ALU.mult,
                                                   ALU.subtract).then_inc(s("c_low"), 1)

            route(0, 0, 0.0)
            def twice(half):
                nc.vector.tensor_tensor(pre[:, til(half), :], res[:, til(half), :], res[:, til(half), :],
                                        ALU.add)

            c_low(0)
            for half in range(2):
                for e in range(NE):
                    g = NE * half + e
                    if g + 1 < 2 * NE:
                        c_low(g + 1)
                    dve.wait_ge(s("c_y"), g + 1)
                    gather(0, half, e, 4 + g % 2).then_inc(s("c_acc"), 1)
                    dve.wait_ge(s("c_acc"), g + 1)
                    if e == 1:
                        join(half, 6 + half, "c_b2", half + 1)
                    if g == 0:
                        link(norm_sums(pre, 1))
                    if g == 1:
                        to_experts(1)
                    if g == 2:
                        low_x(0, 1)
                        shift(0, 1, "f_rb")
                    if g == 4:
                        route(0, 1, 0.0)
                    if g == NE:
                        link(norm_sums(pre, 0))
                    if g == NE + 1:
                        link(norm_apply(pre, res, 0))
                    if g == NE + 2:
                        link(norm_sums(res, 0))
                    if g == NE + 3:
                        norm_apply(res, z, 0).then_inc(s("z_ready"), 1)
                    if g == NE + 4:
                        twice(0)
            link(norm(pre, res, 1))
            norm(res, z, 1).then_inc(s("z_ready"), 1)
            twice(1)

            for half in range(2):
                v = hid[:, half, :, :]
                qk = v[:, :, 0:256].rearrange("p t (h k) -> p t h k", k=GK)
                beta = sm[:, 128 + 16 * half:144 + 16 * half]
                dve.wait_ge(s("d_qksq"), half + 1)
                sq = d_sq[:, half, :, :, :].rearrange("p t h w -> p (t h w)").rearrange(
                    "p (t h k) -> p t h k", t=HT, h=8)
                vv, ww, yy = rt[:, 0, 0:32], rt[:, 1, 0:32], rt[:, 2, 0:32]
                link(nc.vector.tensor_reduce(vv.rearrange("p (t h) -> p t h", t=HT), sq, AX.X, ALU.add))
                link(nc.vector.tensor_scalar(vv, vv, 1e-6, None, ALU.add))
                inv_sqrt(vv, yy, ww)
                y3 = yy.rearrange("p (t h) -> p t h", t=HT)
                link(nc.vector.tensor_scalar(y3[:, :, 0:GH], y3[:, :, 0:GH], GK ** -0.5, None, ALU.mult))
                link(nc.vector.tensor_tensor(d_qk[:, half, :, :, :], qk,
                                             y3.unsqueeze(3).to_broadcast([P, HT, 8, GK]), ALU.mult))
                dve.wait_ge(s("d_tanh"), half + 1)
                link(nc.vector.tensor_scalar(beta, beta, 0.5, 0.5, ALU.mult, ALU.add))
                b3 = beta.rearrange("p (t h) -> p t h", t=HT)
                nc.vector.tensor_tensor(d_P[:, NM * half:NM * half + NM, :].rearrange("p (t h) k -> p t h k", t=HT),
                                        d_qk[:, half, :, 4:8, :],
                                        b3.unsqueeze(3).to_broadcast([P, HT, GH, GK]), ALU.mult).then_inc(
                    s("d_norm"), 1)
            link(nc.vector.memset(e_kv[:, :, 256:272], 1.0))
            dve.wait_ge(s("e_kv"), 1)
            o = ROFF["e_bk"][0]
            link(nc.vector.tensor_tensor(e_kv[:, :, 0:256], e_kv[:, :, 0:256],
                                         rows[0:CTX, o:o + 256].unsqueeze(1).to_broadcast([CTX, B, 256]),
                                         ALU.add))
            link(nc.vector.tensor_tensor(e_sq, e_kv[:, :, 0:128], e_kv[:, :, 0:128], ALU.mult))
            vv, ww, yy = rt[0:CTX, 0, 0:B], rt[0:CTX, 1, 0:B], rt[0:CTX, 2, 0:B]
            link(nc.vector.tensor_reduce(vv, e_sq, AX.X, ALU.add))
            link(nc.vector.tensor_scalar(vv, vv, 1e-24, None, ALU.max))
            inv_sqrt(vv, yy, ww)
            nc.vector.tensor_tensor(e_kv[:, :, 0:128], e_kv[:, :, 0:128],
                                    yy.unsqueeze(2).to_broadcast([CTX, B, 128]), ALU.mult).then_inc(s("e_kn"), 1)
            dve.wait_ge(s("d_gram"), 2)
            dve.wait_ge(s("d_r"), 2)
            nc.vector.transpose(inv_a[:, :],
                                ps[:, :, 0:256].rearrange("p b (t w i) -> p i b t w", t=HT, w=2)[:, :, :, :, 0]
                                ).then_inc(s("d_ab"), 1)
            dve.wait_ge(s("d_ab"), 1)
            dve.wait_ge(s("d_zero"), 2)
            link(nc.vector.tensor_scalar(inv_x[:, CH:CH * CH:2 * CH + 2], inv_a[:, CH:CH * CH:2 * CH + 2], -1.0,
                                         None, ALU.mult))

            def at(buf, off, *dims):
                row_len = int(np.prod(buf.shape[1:]))
                return bass.AP(tensor=buf[:, :].tensor, offset=off,
                               ap=[[row_len, P]] + [list(d) for d in dims])

            for sz in (2, 4, 8, 16):
                g, step = CH // (2 * sz), 2 * sz * (CH + 1)
                parts = {16: 4, 8: 2}.get(sz, 1)
                w = sz // parts
                for second in range(2):
                    todo, off = [], 0
                    for p0 in range(0, sz, w):
                        if second:
                            ni, nk, nj = w, sz, p0 + w
                            left = inv_x, sz * (CH + 1) + CH * p0, CH, 0, 1, step
                            right = inv_t, 0, 0, 1, sz, sz * sz
                            out = at(inv_x, sz * CH + CH * p0, (step, g), (CH, ni), (1, nk))
                        else:
                            ni, nk, nj = sz, w, sz - p0
                            left = inv_a, sz * CH + p0, CH, 0, 1, step
                            right = inv_x, (CH + 1) * p0, 0, 1, CH, step
                            out = at(inv_t, p0, (sz * sz, g), (sz, ni), (1, nk))
                        prod = hid, off, nk * nj, nj, 1, ni * nk * nj

                        def piece(v, n):
                            buf, o, si, sk, sj, sg = v
                            if g > ni:
                                return at(buf, o + si * n, (sg, g), (sk, nk), (sj, nj))
                            return at(buf, o + sg * n, (si, ni), (sk, nk), (sj, nj))

                        for n in range(min(g, ni)):
                            ins = nc.vector.tensor_tensor(piece(prod, n), piece(left, n), piece(right, n),
                                                          ALU.mult)
                        todo.append((out, at(hid, off, (nj, g * ni * nk), (1, nj))))
                        off += g * ni * nk * nj
                    link(ins)
                    for out, prod in todo:
                        ins = nc.vector.tensor_reduce(out, prod, AX.X, ALU.add, negate=bool(second))
                    link(ins)
            dve.wait_ge(s("d_zero"), 3)
            for c in range(4):
                q = slice(CH * c, CH * c + CH)
                ins = nc.vector.transpose(ybd[q, :, q].rearrange("p m i -> p i m"), inv_x[q, :])
            ins.then_inc(s("d_ybd"), 1)
            for half in range(2):
                dve.wait_ge(s("d_mt"), half + 1)
                nc.vector.tensor_tensor(mbd[:, NM * half:NM * half + NM, :],
                                        ps[:, 4 * half:4 * half + 4, :].rearrange("p c (t j) -> p (c t) j", j=128),
                                        tab("blk_neg").unsqueeze(1).to_broadcast([P, NM, 128]),
                                        ALU.mult).then_inc(s("d_mbd"), 1)
            vv, ww, yy = rt[:, 0, 0:32], rt[:, 1, 0:32], rt[:, 2, 0:32]

            def d_square_sums(t):
                dve.wait_ge(s("d_sq"), t + 1)
                return nc.vector.tensor_reduce(vv.rearrange("p (b t h) -> p b t h", b=2, t=HT)[:, :, t, :],
                                               d_sq[:, :, t, :, :], AX.X, ALU.add)

            def d_less_ws(t):
                dve.wait_ge(s("d_ws"), t + 1)
                u = d_u[:, :, t, :, :].rearrange("p b h w -> p b (h w)")
                nc.vector.tensor_tensor(u, u, ps[:, 4 + t % 2, :].rearrange("p (b n) -> p b n", b=2),
                                        ALU.subtract).then_inc(s("d_u"), 1)

            for n in range(NC - 1):
                dve.wait_ge(s("d_step"), n + 1)
                nc.vector.tensor_tensor(d_S[:, n + 1, :, :], ps[:, 2 * (n % 2):2 * (n % 2) + 2, 0:GV],
                                        d_S[:, n, :, :], ALU.add).then_inc(s("d_state"), 1)
                dve.wait_ge(s("d_state"), n + 1)
                t, c = divmod(n, 4)
                if c == 0 and t >= 1:
                    d_less_ws(t - 1)
                if c == 3 and t >= 1:
                    d_square_sums(t - 1)
            d_less_ws(HT - 1)
            d_square_sums(HT - 2)
            link(d_square_sums(HT - 1))
            link(nc.vector.tensor_scalar(vv, vv, 1.0 / GV, 1e-5, ALU.mult, ALU.add))
            inv_sqrt(vv, yy, ww)
            for half in range(2):
                o = d_o[:, half, :, :, :].rearrange("p t h w -> p (t h) w")
                nc.vector.tensor_tensor(
                    o, o, yy[:, NM * half:NM * half + NM].unsqueeze(2).to_broadcast([P, NM, GV]),
                    ALU.mult).then_inc(s("d_on"), 1)
            for half in range(2):
                join(half, 4 * half + 2, "d_y", half + 1)
                norm(pre, res, half).then_inc(s("z_ready"), 1)

            for half in range(2):
                qp = z[:, til(half), :]
                dve.wait_ge(s("e_qt_ps"), half + 1)
                nc.vector.tensor_tensor(qp, ps[:, EQT[half], :].rearrange("p (t d) -> p t d", t=HT),
                                        rowb("e_bq", HT), ALU.add).then_inc(s("e_qt"), 1)
                dve.wait_ge(s("e_qt"), half + 1)
                link(nc.vector.tensor_tensor(pre[:, til(half), :], qp, qp, ALU.mult))
                vv, ww, yy = rt[:, 0, 0:HT], rt[:, 1, 0:HT], rt[:, 2, 0:HT]
                link(nc.vector.tensor_reduce(vv, pre[:, til(half), :], AX.X, ALU.add))
                link(nc.vector.tensor_scalar(vv, vv, 1e-24, None, ALU.max))
                inv_sqrt(vv, yy, ww)
                nc.vector.tensor_scalar(sm[:, 256 + HT * half:260 + HT * half], yy, 8.0 ** -0.5, None,
                                        ALU.mult).then_inc(s("e_scale"), 1)
                link(nc.vector.tensor_tensor(pre[:, til(half), :], qp, rowb("e_bo", HT), ALU.add))

            def e_tail(half, step):
                hs = til(half)
                if step == 0:
                    link(norm_sums(pre, half))
                elif step == 1:
                    link(norm_apply(pre, z, half))
                elif step == 2:
                    link(nc.vector.tensor_tensor(z[:, hs, :], z[:, hs, :], rowb("e_g", HT), ALU.mult))
                    link(nc.vector.tensor_tensor(z[:, hs, :], z[:, hs, :], rowb("e_b", HT), ALU.add))
                    link(nc.vector.tensor_tensor(pre[:, hs, :], z[:, hs, :], res[:, hs, :], ALU.add))
                elif step == 3:
                    link(norm_sums(pre, half))
                else:
                    norm_apply(pre, res, half).then_inc(s("z_ready"), 1)
                    dve.wait_ge(s("z_ready"), nth(H, half))
                    link(nc.vector.tensor_copy(pre[:, hs, :], res[:, hs, :]))

            for i in range(NT + 3):
                if 2 <= i < NT + 2:
                    t = i - 2
                    dve.wait_ge(s("e_pv"), t + 1)
                    den = rt[:, t % 2, 16:32]
                    link(nc.vector.reciprocal(den, ps[:, 6 + t % 2, 128:144]))
                    nc.vector.tensor_tensor(e_o[:, t % 2, :].rearrange("p (h d) -> p h d", h=EH),
                                            ps[:, 6 + t % 2, 0:128].rearrange("p (h d) -> p h d", h=EH),
                                            den.unsqueeze(2).to_broadcast([P, EH, 8]),
                                            ALU.mult).then_inc(s("e_o"), 1)
                if 3 <= i:
                    t = i - 3
                    dve.wait_ge(s("e_y"), t + 1)
                    nc.vector.tensor_tensor(pre[:, t, :], ps[:, 6 + t % 2, 384:512], pre[:, t, :],
                                            ALU.add).then_inc(s("e_yadd"), 1)
                    dve.wait_ge(s("e_yadd"), t + 1)
                    for step in {HT - 1: (0, 1), HT: (2,), HT + 1: (3, 4)}.get(t, ()):
                        e_tail(0, step)

            low_x(1, 0)
            shift(1, 0, None)

            def f_acc(g):
                dve.wait_ge(s("f_y"), g + 1)
                gather(1, g // NE, g % NE, 4 + g % 2).then_inc(s("f_acc"), 1)
                dve.wait_ge(s("f_acc"), g + 1)
                if g == NE or g == 2 * NE - 1:
                    link(norm_sums(pre, g // (NE + 1)))
                if g == NE + 1 or g == 2 * NE - 1:
                    norm_apply(pre, res, g // (NE + 2)).then_inc(s("out_ready"), 1)

            for g in range(2 * NE):
                for c in range(3):
                    n = 3 * g + c
                    w = F1C[c][1]
                    dve.wait_ge(s("f_silu"), n + 1)
                    dve.wait_ge(s("f_up_ps"), n + 1)
                    nc.vector.scalar_tensor_tensor(hid[0:w, g % 2, c, :], ps[0:w, FB[c] + 1, :],
                                                   HS / (XS * WS), hid[0:w, g % 2, c, :], ALU.mult,
                                                   ALU.mult).then_inc(s("f_h"), 1)
                if g == 0:
                    route(1, 0, 1e-20)
                if g >= 1:
                    f_acc(g - 1)
                if 1 <= g <= 5:
                    e_tail(1, g - 1)
                if g == 6:
                    low_x(1, 1)
                    shift(1, 1, None)
                if g == 7:
                    route(1, 1, 1e-20)
            f_acc(2 * NE - 1)

        @block.tensor
        def _(pe):
            mm = nc.tensor.matmul

            def turn(use, half, src):
                pe.wait_ge(s("z_ready"), nth(use, half))
                for t in range(HT):
                    ins = nc.tensor.transpose(ps[:, turn_bank(use, half), 128 * t:128 * t + 128],
                                              src[:, HT * half + t, :], ident)
                ins.then_inc(s("turned"), 1)

            need(pe, "tabs")
            for half in range(2):
                turn(A, half, z)
                if half == 0:
                    need(pe, "wa")
                pe.wait_ge(s("xT_ready"), nth(A, half))
                for j in range(3):
                    mm(ps[:, 3 * half + j, :], wa[:, j, :], xT[:, tok(half)], start=True, stop=True).then_inc(
                        s("a_qkv_ps"), 1)
            for half in range(2):
                pe.wait_ge(s("a_prod"), half + 1)
                mm(ps[:, 3 * half, :], tab("head8"), a_prod[:, tok(half)], start=True, stop=True).then_inc(
                    s("a_gap"), 1)
            need(pe, "ctxT", "wxkv")
            for g in range(7):
                if g >= 2:
                    pe.wait_ge(s("b_kv"), g - 1)
                if g < 3:
                    for c in range(3 * g, min(3 * g + 3, 8)):
                        ins = mm(ps[:, 6 + g % 2, B * CTX * (c - 3 * g):B * CTX * (c - 3 * g + 1)],
                                 wxkv[:, 128 * c:128 * c + 128], ctxT[:, :], start=True, stop=True)
                else:
                    b, n = divmod(g - 3, 2)
                    ins = mm(ps[0:CTX, 6 + g % 2, :], ctxT[:, CTX * b:CTX * b + CTX],
                             wxkv[:, XI + 512 * n:XI + 512 * n + 512], start=True, stop=True)
                ins.then_inc(s("b_kv_ps"), 1)
                if g == 1:
                    for half in range(2):
                        pe.wait_ge(s("a_o"), half + 1)
                        for t in range(HT):
                            ins = mm(ps[:, 3 * half + 1, 128 * t:128 * t + 128],
                                     a_o[:, S * half + 128 * t:S * half + 128 * t + 128], wa[:, 3, :],
                                     start=True, stop=True)
                        ins.then_inc(s("a_y"), 1)

            need(pe, "wxq")
            pe.wait_ge(s("b_kv"), 7)
            turn(X, 0, z)

            def b_queries(half):
                if half == 0:
                    pe.wait_ge(s("xT_ready"), nth(X, 0))
                for r in range(8):
                    n = RAT[("q", half, r)]
                    ring_free(pe, n)
                    mm(ps[:, ring(n), :], wxq[:, 128 * r:128 * r + 128], xT[:, tok(half)],
                       start=True, stop=True).then_inc(s("b_ring"), 1)

            def b_scores(t):
                if t % HT == 0:
                    pe.wait_ge(s("b_ringed"), ringed("q", t // HT, 7))
                if t >= 1:
                    pe.wait_ge(s("b_max"), t)
                for r in range(8):
                    ins = mm(ps[:, r // 3, 2 * CTX * (r % 3):2 * CTX * (r % 3 + 1)],
                             b_q[:, r, 128 * (t % HT):128 * (t % HT) + 128],
                             b_kT[:, r, t // HT, :, :].rearrange("p a k -> p (a k)"), start=True, stop=True)
                ins.then_inc(s("b_sc"), 1)

            def b_turn_p(t):
                pe.wait_ge(s("b_prob"), t + 1)
                for r in range(4):
                    n = RAT[("pT", t, r)]
                    ring_free(pe, n)
                    for j in range(4):
                        h = 4 * r + j
                        ins = nc.tensor.transpose(ps[0:CTX, ring(n), 128 * j:128 * j + 128],
                                                  b_s[:, t % 3, CTX * h:CTX * h + CTX], ident)
                    ins.then_inc(s("b_ring"), 1)

            def b_values(t):
                pe.wait_ge(s("b_ringed"), ringed("pT", t, 3))
                if t >= 1:
                    pe.wait_ge(s("b_low"), t)
                else:
                    pe.wait_ge(s("xT_ready"), nth(X, 1))
                for h in range(XH):
                    q, k = XD * (h % 2), 128 * (h // 2 % 4)
                    ins = mm(ps[q:q + XD, 6 + h // 8, k:k + 128], b_v[0:CTX, t // HT, XD * h:XD * h + XD],
                             b_pT[0:CTX, h, :], start=True, stop=True, tile_position=(0, q))
                ins.then_inc(s("b_pv"), 1)

            def b_project(t):
                n = RAT[("y", t, 0)]
                if t == 0:
                    pe.wait_ge(s("b_wo"), 1)
                ring_free(pe, n)
                pe.wait_ge(s("b_low"), t + 1)
                for k in range(8):
                    for i, (p, q) in enumerate(PASSES):
                        ins = mm(ps[:, ring(n), 0:128], b_oT[:, t % 2, p, k, :], b_wo[:, q, k, :],
                                 start=(k == 0 and i == 0), stop=(k == 7 and i == 2))
                ins.then_inc(s("b_ring"), 1)

            for i in range(NI):
                if i in (0, HT):
                    b_queries(i // HT)
                if i == 1:
                    turn(X, 1, z)
                if i < NT:
                    b_scores(i)
                if 2 <= i < NT + 2:
                    b_turn_p(i - 2)
                if i == NI - 1:
                    pe.wait_ge(s("b_low"), NT)
                    turn(F, 0, res)
                if 3 <= i:
                    b_project(i - 3)
                if 2 <= i < NT + 2:
                    b_values(i - 2)

            def logits(which, half):
                pe.wait_ge(s("xT_ready"), nth(H if which else F, half))
                for t in range(HT):
                    ins = mm(ps[:, 6 + half, E * t:E * t + E],
                             xT[:, S * half + 128 * t:S * half + 128 * t + 128], router[:, which, :],
                             start=True, stop=True)
                ins.then_inc(s("r_logit"), 1)

            need(pe, "router", "fb2")
            logits(0, 0)

            def c_hidden(g):
                half, e = divmod(g, NE)
                if e == 0:
                    pe.wait_ge(s("x_low"), half + 1)
                    pe.wait_ge(s("w_split"), 6)
                for c in range(C0):
                    if g >= 1:
                        pe.wait_ge(s("c_h"), C0 * (g - 1) + c + 1)
                    for i, (p, q) in enumerate(PASSES):
                        ins = mm(ps[:, c, :], w1[:, p, e, 128 * c:128 * c + 128], xs[0][:, half, q, :],
                                 start=(i == 0), stop=(i == 2))
                    ins.then_inc(s("c_h_ps"), 1)

            def c_out(g):
                half, e = divmod(g, NE)
                pe.wait_ge(s("c_low"), C0 * (g + 1))
                if g >= 2:
                    pe.wait_ge(s("c_acc"), g - 1)
                for t in range(HT):
                    for c in range(C0):
                        for i, (p, q) in enumerate(PASSES):
                            ins = mm(ps[:, 4 + g % 2, 128 * t:128 * t + 128],
                                     hp[0][:, g % 2, p, c, 128 * t:128 * t + 128],
                                     w2[:, q, e, D * c:D * c + D],
                                     start=(c == 0 and i == 0), stop=(c == C0 - 1 and i == 2))
                ins.then_inc(s("c_y"), 1)

            def d_project(half):
                pe.wait_ge(s("xT_ready"), nth(G, half))
                if half == 0:
                    need(pe, "wd")
                    pe.wait_ge(s("c_h"), C0 * 2 * NE)
                for t in range(HT):
                    mm(ps[:, 4 * half + t, :], xT[:, S * half + 128 * t:S * half + 128 * t + 128],
                       wd[:, 0:512], start=True, stop=True).then_inc(s("d_qkv"), 1)

            def d_betas(half):
                pe.wait_ge(s("d_silu"), HT * half + 1)
                for t in range(HT):
                    ins = mm(ps[:, 4 * half, 4 * t:4 * t + 4],
                             xT[:, S * half + 128 * t:S * half + 128 * t + 128], wd[:, 512:516],
                             start=True, stop=True)
                ins.then_inc(s("d_beta_ps"), 1)

            for g in range(2 * NE + 1):
                if g < 2 * NE:
                    c_hidden(g)
                if g == 2 * NE:
                    d_project(0)
                if g >= 1:
                    c_out(g - 1)
                if g == 3:
                    turn(F, 1, res)
                    logits(0, 1)
                if g == 2 * NE - 4:
                    turn(G, 0, z)
                if g % NE == 1:
                    half = g // NE
                    if half < 2:
                        pe.wait_ge(s("r_comb"), half + 1)
                        for t in range(HT):
                            ins = nc.tensor.transpose(ps[0:E, 6 + half, 128 * t:128 * t + 128],
                                                      comb[:, HT * half + t, :], ident)
                        ins.then_inc(s("c_combT_ps"), 1)
                        pe.wait_ge(s("c_combT"), half + 1)
                        for t in range(HT):
                            ins = mm(ps[:, 6 + half, 128 * t:128 * t + 128],
                                     combT[:, half, 128 * t:128 * t + 128], fb2[:, :], start=True, stop=True)
                        ins.then_inc(s("c_b2"), 1)

            need(pe, "wdo")
            d_betas(0)
            turn(G, 1, z)
            d_project(1)
            d_betas(1)
            need(pe, "wekv", "spread")
            for b in range(B):
                ins = mm(ps[0:CTX, 3, 256 * b:256 * b + 256], ctxT[:, CTX * b:CTX * b + CTX], wekv[:, :],
                         start=True, stop=True)
            ins.then_inc(s("e_kv_ps"), 1)
            def d_turns(half):
                pe.wait_ge(s("d_norm"), half + 1)
                for w in range(3):
                    for t in range(HT):
                        src = (d_qk[:, half, t, 4:8, :], d_P[:, NM * half + GH * t:NM * half + GH * t + GH, :], d_qk[:, half, t, 0:4, :])[w]
                        ins = nc.tensor.transpose(ps[:, 4 * half + w, 128 * t:128 * t + 128], src, ident)
                    ins.then_inc(s("d_turn_ps"), 1)
            for half in range(2):
                d_turns(half)
                pe.wait_ge(s("d_turn"), 3 * half + 3)
                if half == 0:
                    pe.wait_ge(s("e_kv"), 1)
                for h in range(GH):
                    q = slice(GK * h, GK * h + GK)
                    for t in range(HT):
                        for c in range(4):
                            n = 128 * t + CH * c
                            ins = mm(ps[CH * c:CH * c + CH, 4 * half + h, 64 * t:64 * t + 64],
                                     d_T[q, half, 0, n:n + CH], d_T[q, half, 1:3, n:n + CH],
                                     start=True, stop=True, tile_position=(GK * h, CH * c))
                ins.then_inc(s("d_gram"), 1)
            pe.wait_ge(s("d_r"), 2)
            pe.wait_ge(s("e_kn"), 1)
            pe.wait_ge(s("d_ab"), 1)
            pe.wait_ge(s("d_pt"), 1)
            for b in range(B):
                ins = nc.tensor.transpose(ps[:, 0, CTX * b:CTX * b + CTX], e_kv[:, b, 0:128], ident[0:CTX, 0:CTX])
            ins.then_inc(s("e_kT_ps"), 1)
            pe.wait_ge(s("e_k1"), 1)
            pe.wait_ge(s("d_ybd"), 1)
            for half in range(2):
                for t in range(HT):
                    for h in range(GH):
                        ins = mm(ps[:, 4 * half + t, 96 * h:96 * h + 96], ybd[:, NM * half + HT * h + t, :],
                                 d_r[:, half, t, h, :], start=True, stop=True)
                ins.then_inc(s("d_uw_ps"), 1)
            def d_turn_w(half):
                for t in range(HT):
                    ins = nc.tensor.transpose(ps[:, 4 * half, 128 * t:128 * t + 128], d_w[:, half, t, :], ident)
                ins.then_inc(s("d_wT_ps"), 1)

            for half in range(2):
                pe.wait_ge(s("d_uw"), half + 1)
                if half == 1:
                    d_turn_w(1)
                for c in (1, 2, 3, 0):
                    if half == 1 and c == 0:
                        pe.wait_ge(s("d_wT"), 1)
                    q = slice(CH * c, CH * c + CH)
                    for t in range(HT):
                        ins = mm(ps[:, 4 * half + c, 128 * t:128 * t + 128], d_w[q, half, t, :],
                                 d_qk[q, half, t, 4:8, :], start=True, stop=True, tile_position=(CH * c, 0))
                ins.then_inc(s("d_mt"), 1)
            pe.wait_ge(s("d_mbd"), 1)
            d_turn_w(0)
            pe.wait_ge(s("d_mbd"), 2)

            def d_new(n):
                t, c = divmod(n, 4)
                q = slice(CH * c, CH * c + CH)
                if n >= 2:
                    pe.wait_ge(s("d_state"), n - 1)
                for b in range(2):
                    for h in range(GH):
                        mm(ps[GK * h:GK * h + GK, 2 * (n % 2) + b, 0:GV], d_qk[q, b, t, 4 + h, :],
                           d_u[q, b, t, h, :], start=True, stop=False, tile_position=(CH * c, GK * h),
                           skip_group_check=True)

            def d_against_state(n):
                t, c = divmod(n, 4)
                if c == 0 and t >= 2:
                    pe.wait_ge(s("d_u"), t - 1)
                    pe.wait_ge(s("d_sq"), t - 1)
                pe.wait_ge(s("d_diag"), n + 1)
                for b in range(2):
                    ins = mm(ps[CH * c:CH * c + CH, 4 + t % 2, 256 * b:256 * b + 256],
                             d_wT[:, b, CH * n:CH * n + CH], sbd[:, n % 2, b, :],
                             start=(b == 0), stop=True, tile_position=(0, CH * c), skip_group_check=True)
                if c == 3:
                    ins.then_inc(s("d_ws"), 1)
                for b in range(2):
                    ins = mm(ps[CH * c:CH * c + CH, 6 + t % 2, 256 * b:256 * b + 256],
                             d_T[:, b, 2, CH * n:CH * n + CH], sbd[:, n % 2, b, :],
                             start=(b == 0), stop=False, tile_position=(0, CH * c), skip_group_check=True)
                ins.then_inc(s("d_against"), 1)

            def d_within(t):
                if t == 0:
                    pe.wait_ge(s("d_pbd"), 1)
                pe.wait_ge(s("d_u"), t + 1)
                for b in range(2):
                    for h in range(GH):
                        k = GV * (GH * b + h)
                        ins = mm(ps[:, 6 + t % 2, k:k + GV], pbd[:, NM * b + HT * h + t, :], d_u[:, b, t, h, :],
                                 start=False, stop=True, skip_group_check=True)
                ins.then_inc(s("d_o_ps"), 1)

            pe.wait_ge(s("d_wT"), 2)
            d_new(0)
            for n in range(NC - 1):
                t, c = divmod(n, 4)
                if n >= 1:
                    pe.wait_ge(s("d_state"), n)
                for b in range(2):
                    ins = mm(ps[:, 2 * (n % 2) + b, 0:GV], mbd[:, NM * b + HT * c + t, :], d_S[:, n, b, :],
                             start=False, stop=True, skip_group_check=True)
                ins.then_inc(s("d_step"), 1)
                if n + 1 < NC - 1:
                    d_new(n + 1)
                if n >= 1:
                    d_against_state(n - 1)
                if n >= 6 and c == 2:
                    d_within(t - 1)
            d_against_state(NC - 2)
            d_against_state(NC - 1)
            d_within(HT - 1)
            def e_values(b):
                for n in range(VB * b, VB * b + VB):
                    _, k0, k1 = VG[n]
                    if n >= 2:
                        pe.wait_ge(s("e_spread"), n - 1)
                    for k in range(k0, k1):
                        ins = mm(ps[:, 4 + n % 2, 144 * (k - k0):144 * (k - k0) + 144],
                                 spread[:, 128 * k:128 * k + 128], e_kv[:, b, 128:272], start=True, stop=True)
                    ins.then_inc(s("e_vb_ps"), 1)

            e_values(0)
            pe.wait_ge(s("d_wdo"), 1)
            for half in range(2):
                pe.wait_ge(s("d_on"), half + 1)
                if half == 1:
                    pe.wait_ge(s("e_spread"), VB)
                for w in range(2):
                    for t in range(HT):
                        ins = nc.tensor.transpose(
                            ps[:, 4 * half + w, 128 * t:128 * t + 128],
                            d_o[:, half, t, 2 * w:2 * w + 2, :].rearrange("p h d -> p (h d)"), ident)
                    ins.then_inc(s("d_oT_ps"), 1)
                pe.wait_ge(s("d_oT"), 2 * half + 2)
                for t in range(HT):
                    for w in range(2):
                        ins = mm(ps[:, 4 * half + 2, 128 * t:128 * t + 128],
                                 d_T[:, half, w, 128 * t:128 * t + 128], wdo[:, w, :],
                                 start=(w == 0), stop=(w == 1))
                ins.then_inc(s("d_y"), 1)

            need(pe, "we")
            for half in range(2):
                turn(EX, half, res)
                pe.wait_ge(s("xT_ready"), nth(EX, half))
                mm(ps[:, EQ[half], :], we[:, 0, :], xT[:, tok(half)], start=True, stop=True).then_inc(
                    s("e_q_ps"), 1)
                for t in range(HT):
                    ins = mm(ps[:, EQT[half], 128 * t:128 * t + 128],
                             xT[:, S * half + 128 * t:S * half + 128 * t + 128], we[:, 0, :],
                             start=True, stop=True)
                ins.then_inc(s("e_qt_ps"), 1)
            pe.wait_ge(s("e_q"), 1)
            pe.wait_ge(s("e_qt"), 1)
            pe.wait_ge(s("e_kT"), 2)
            for i in range(NT + 3):
                if i < NT:
                    if i >= 1:
                        pe.wait_ge(s("e_exp"), i)
                    half, t = divmod(i, HT)
                    if i == HT:
                        pe.wait_ge(s("e_q"), 2)
                    for k in range(4):
                        ins = mm(ps[:, k, 0:4 * CTX], e_q[:, half, 128 * t:128 * t + 128],
                                 e_kT[:, half, 4 * CTX * k:4 * CTX * (k + 1)], start=True, stop=True)
                    ins.then_inc(s("e_sc"), 1)
                if i == 0:
                    e_values(1)
                if 3 <= i:
                    t = i - 3
                    pe.wait_ge(s("e_o"), t + 1)
                    nc.tensor.transpose(ps[:, 6 + t % 2, 256:384], e_o[:, t % 2, :], ident).then_inc(
                        s("e_oT_ps"), 1)
                if 2 <= i < NT + 2:
                    t = i - 2
                    if t == 0:
                        pe.wait_ge(s("e_q"), 2)
                        pe.wait_ge(s("e_qt"), 2)
                    if t % HT == 0:
                        pe.wait_ge(s("e_vb"), VB * (t // HT + 1))
                    pe.wait_ge(s("e_pT"), 3 * t + 3)
                    if t >= 2:
                        pe.wait_ge(s("e_yadd"), t - 1)
                    for k in range(EK):
                        w = min(128, EP - 128 * k)
                        ins = mm(ps[:, 6 + t % 2, 0:144], e_pT[t % 2][0:w, k, :], e_vb[0:w, t // HT, k, :],
                                 start=(k == 0), stop=(k == EK - 1))
                    ins.then_inc(s("e_pv"), 1)
                if 3 <= i:
                    t = i - 3
                    pe.wait_ge(s("e_oT"), t + 1)
                    mm(ps[:, 6 + t % 2, 384:512], e_oT[:, t % 2, :], we[:, 1, :], start=True,
                       stop=True).then_inc(s("e_y"), 1)
                if i == NT + 2:
                    pe.wait_ge(s("e_yadd"), NT - 1)
                    turn(H, 0, res)
                if 1 <= i <= NT:
                    t = i - 1
                    pe.wait_ge(s("e_exp"), t + 1)
                    if t == 0:
                        pe.wait_ge(s("e_spread"), len(VG))
                    for r in range(3):
                        n = 3 * t + r
                        if n >= 2:
                            pe.wait_ge(s("e_pT"), n - 1)
                        for k in range(4 * r, min(4 * r + 4, EK)):
                            w = min(128, EP - 128 * k)
                            ins = nc.tensor.transpose(ps[0:w, 4 + n % 2, 128 * (k - 4 * r):128 * (k - 4 * r) + 128],
                                                      e_p[:, t % 2, 128 * k:128 * k + w], ident)
                        ins.then_inc(s("e_pT_ps"), 1)

            logits(1, 0)

            def f_hidden(g):
                half, e = divmod(g, NE)
                if e == 0:
                    pe.wait_ge(s("x_low"), 2 + half + 1)
                for c, (f, w) in enumerate(F1C):
                    n = 3 * g + c
                    if c == 2 and g in (0, 7):
                        pe.wait_ge(s("r_shift"), 3 + (g > 0))
                    for up, free, full in ((0, "f_silu", "f_gate_ps"), (1, "f_h", "f_up_ps")):
                        if g >= 1:
                            pe.wait_ge(s(free), n - 2)
                        for i, (p, q) in enumerate(PASSES):
                            ins = mm(ps[0:w, FB[c] + up, :], f_gu[:, p, e, F1 * up + f:F1 * up + f + w],
                                     xs[1][:, half, q, :], start=(i == 0), stop=(i == 2))
                        ins.then_inc(s(full), 1)

            def f_out(g):
                half, e = divmod(g, NE)
                pe.wait_ge(s("f_low"), 3 * (g + 1))
                if g >= 2:
                    pe.wait_ge(s("f_acc"), g - 1)
                for t in range(HT):
                    for c, (f, w) in enumerate(F1C):
                        for i, (p, q) in enumerate(PASSES):
                            ins = mm(ps[:, 4 + g % 2, 128 * t:128 * t + 128],
                                     hp[1][0:w, g % 2, p, c, 128 * t:128 * t + 128],
                                     f_dn[0:w, q, e, D * c:D * c + D],
                                     start=(c == 0 and i == 0), stop=(c == 2 and i == 2))
                ins.then_inc(s("f_y"), 1)

            pe.wait_ge(s("e_exp"), NT)
            for g in range(2 * NE + 1):
                if g < 2 * NE:
                    f_hidden(g)
                if g >= 1:
                    f_out(g - 1)
                if g == 6:
                    pe.wait_ge(s("f_h"), 3 * g + 3)
                    turn(H, 1, res)
                    logits(1, 1)


def tables():
    p = np.arange(P)
    k = np.arange(CH)
    j = p % CH
    t = {}
    t["ident"] = np.eye(P)
    t["head8"] = p[:, None] // 8 == p[None, :] // 8
    t["low_incl"] = j[:, None] <= k[None, :]
    t["blk_neg"] = -1.0 * (p[:, None] // CH == p[None, :] // CH)
    t["head4"] = p[:, None] // GK == np.arange(GH)[None, :]
    t["ehead"] = p[:, None] // 8 == np.arange(EH)[None, :]
    t["iota"] = np.broadcast_to(np.arange(E), (P, E))
    r = np.arange(EK * P)
    h = np.concatenate([np.arange(P) // 8, np.arange(EH)])
    vm = (r[:, None] // CTX == h[None, :]) & (r[:, None] < EP)
    t["vmask"] = vm.reshape(EK, P, 144).transpose(1, 0, 2).reshape(P, EK * 144)
    tabs = np.concatenate([np.asarray(t[n], np.float32) for n, _ in TABS], 1)
    spread = (np.arange(CTX)[:, None] == r[None, :] % CTX) & (r[None, :] < EP)
    return tabs, spread.astype(np.float32)


def kernel(**inputs):
    import concourse.bacc as bacc
    from concourse.bass_utils import run_bass_kernel_spmd as run

    i = {k: np.asarray(v) for k, v in inputs.items()}
    tabs, spread = tables()
    cat = np.concatenate
    a = {
        "x": i["x"].reshape(B * S, D),
        "tabs": tabs, "spread": spread,
        "cols": np.stack([i[n] for n in ("L0_attn_ln_g", "L0_attn_ln_b", "L0_attn_bq", "L0_attn_bk",
                                         "L0_attn_bv", "L0_xattn_ln_gamma", "L0_xattn_ln_beta",
                                         "L1_attn_ln_w", "L1_attn_ln_b", "L1_xattn_bq")]
                         + [cat([i["L1_attn_o_norm_w"]] * (P // GV))], 1),
        "rows": cat([i["L0_attn_bo"], i["L0_xattn_bo"], i["L0_ffn_shared_b2"], i["L1_xattn_bq"],
                     i["L1_xattn_bk"], i["L1_xattn_bv"], i["L1_xattn_bo"], i["L1_xattn_ln_gamma"],
                     i["L1_xattn_ln_beta"], i["L0_ffn_router_b"]]),
        "ctxT": i["ctx_768"].reshape(B * CTX, CD).T,
        "mask": i["mask_1x1xSxS2_bk0"].reshape(S, CTX),
        "wa": np.stack([i["L0_attn_W" + w] for w in "qkvo"], 1),
        "wxq": i["L0_xattn_Wq"],
        "wxkv": i["L0_xattn_Wkv"],
        "wxo": i["L0_xattn_Wo"].reshape(8, P, D).transpose(1, 0, 2),
        "router": np.stack([i["L0_ffn_router_w"].T, i["L1_ffn_gate_w"].T], 1),
        "w1": cat([i["L0_ffn_shared_w1"][None], i["L0_ffn_spec_w1"]]).transpose(2, 0, 1),
        "w2": cat([i["L0_ffn_shared_w2"][None], i["L0_ffn_spec_w2"]]).reshape(NE, D, C0, P).transpose(3, 0, 2, 1)
        .reshape(P, NE, F0),
        "fb1": cat([i["L0_ffn_shared_b1"][None], i["L0_ffn_spec_b1"]]).reshape(NE, C0, P).transpose(2, 0, 1),
        "fb2": i["L0_ffn_spec_b2"],
        "wd": cat([i["L1_attn_W" + w] for w in "qkvb"], 1),
        "wdo": i["L1_attn_Wo"].reshape(2, P, D).transpose(1, 0, 2),
        "we": np.stack([i["L1_xattn_Wq"], i["L1_xattn_Wo"]], 1),
        "wekv": cat([i["L1_xattn_Wk"], i["L1_xattn_Wv"]], 1),
        "f_gu": np.stack([cat([i["L1_ffn_shared_gate"][None], i["L1_ffn_expert_gate"]]),
                          cat([i["L1_ffn_shared_up"][None], i["L1_ffn_expert_up"]])], 1).transpose(3, 0, 1, 2).reshape(P, NE, 2 * F1),
    }
    dn = cat([i["L1_ffn_shared_down"][None], i["L1_ffn_expert_down"]]).transpose(2, 0, 1)
    pad = np.zeros((3 * P - F1, NE, D), dn.dtype)
    a["f_dn"] = cat([dn, pad]).reshape(3, P, NE, D).transpose(1, 2, 0, 3).reshape(P, NE, 3 * D)

    nc = bacc.Bacc("TRN2", target_bir_lowering=False, num_devices=1)
    arrays, args = {}, {}
    for name, v in a.items():
        v = np.ascontiguousarray(v)
        arrays["in_" + name] = v
        args[name] = nc.dram_tensor("in_" + name, v.shape, mybir.dt.from_np(v.dtype), kind="ExternalInput").ap()
    args["out"] = nc.dram_tensor("out_x", (B * S, D), FP, kind="ExternalOutput").ap()
    program(nc, args)
    r = run(nc, [arrays], core_ids=[0])
    return r.results[0]["out_x"].reshape(B, S, D)
```
